# Optimizing a Trainium2 kernel written in Bass

```python
import numpy as np
import jax
import jax.numpy as jnp

def _softmax(x, axis=-1):
    return jax.nn.softmax(x, axis=axis)

def _gelu(x):
    return jax.nn.gelu(x, approximate=True)

def _silu(x):
    return jax.nn.silu(x)

def _sigmoid(x):
    return jax.nn.sigmoid(x)

def _layernorm(x, axis=-1, eps=1e-05):
    m = jnp.mean(x, axis=axis, keepdims=True)
    v = jnp.var(x, axis=axis, keepdims=True)
    return (x - m) / jnp.sqrt(v + eps)

def _scatter_add(tgt, idx, src, axis=0):
    return tgt.at[idx].add(src)

def _segment_sum(src, seg, n):
    return jax.ops.segment_sum(src, seg, n)
kernel_name = 'mk_sandwich_d1_jaxref_r4_2397e0'

def setup_inputs(seed: int=0):
    np.random.seed(seed)
    _w = jnp.asarray

    def _L0_attn_setup():
        import jax, jax.numpy as jnp
        import numpy as np
        B, S, D = (2, 1024, 512)
        H = 16
        DC = 128
        DKQV = 512
        DR = 256
        DCKV = 128
        DOUT = 512
        DH = DKQV // H
        DRH = DR // H
        SCALER = 1.0 / float(np.sqrt(DH + DRH))

        def _rope(x):
            dr = x.shape[-1]
            inv_freq = 1.0 / 10000.0 ** (jnp.arange(0, dr, 2, dtype=jnp.float32) / dr)
            t = jnp.arange(x.shape[1], dtype=jnp.float32)
            freqs = t[:, None] * inv_freq[None, :]
            emb = jnp.concatenate([freqs, freqs], axis=-1)[None, :, None, :]
            x1, x2 = jnp.split(x, 2, axis=-1)
            rot = jnp.concatenate([-x2, x1], axis=-1)
            return x * jnp.cos(emb) + rot * jnp.sin(emb)
        key = jax.random.key(seed)
        ks = jax.random.split(key, 20)

        def lin(k, din, dout):
            s = 1.0 / np.sqrt(din)
            kw, kb = jax.random.split(k)
            W = jax.random.uniform(kw, (din, dout), jnp.float32, -s, s)
            b = jax.random.uniform(kb, (dout,), jnp.float32, -s, s)
            return (W, b)
        h_t = jax.random.normal(ks[0], (B, S, D), jnp.float32)
        Wc, bc = lin(ks[1], D, DC)
        Wcq, bcq = lin(ks[2], DC, DKQV)
        Wqr, bqr = lin(ks[3], DC, DR)
        Wckv, bckv = lin(ks[4], D, DCKV)
        Wck, bck = lin(ks[5], DCKV, DKQV)
        Wkr, bkr = lin(ks[6], D, DR)
        Wv, bv = lin(ks[7], DCKV, DKQV)
        Wo, bo = lin(ks[8], DKQV, DOUT)
        return dict(h_t=h_t, Wc=Wc, bc=bc, Wcq=Wcq, bcq=bcq, Wqr=Wqr, bqr=bqr, Wckv=Wckv, bckv=bckv, Wck=Wck, bck=bck, Wkr=Wkr, bkr=bkr, Wv=Wv, bv=bv, Wo=Wo, bo=bo)
    _L0_attn_in = _L0_attn_setup()

    def _L0_ffn_setup():
        import jax, jax.numpy as jnp
        import numpy as np
        E = 64
        K = 6
        CAP = 128
        SCALE = 1.0
        H = 512
        I = 192
        SI = I * 2
        B, S = (2, 256)

        def _moe(x, gate_w, gate_up_proj, down_proj, shared_gate_w, shared_up_w, shared_down_w):
            b, s, h = x.shape
            T = b * s
            xf = x.reshape(T, h)
            scores = jax.nn.softmax(xf @ gate_w.T, axis=-1)
            topk_w, topk_idx = jax.lax.top_k(scores, K)
            topk_w = topk_w * SCALE
            flat_e = topk_idx.reshape(-1)
            order = jnp.argsort(flat_e)
            sorted_e = flat_e[order]
            sorted_tok = (order // K).astype(jnp.int32)
            sorted_w = topk_w.reshape(-1)[order]
            counts = jnp.zeros((E,), jnp.int32).at[flat_e].add(1)
            offsets = jnp.cumsum(counts) - counts
            pos = jnp.arange(T * K, dtype=jnp.int32) - offsets[sorted_e]
            buf_tok = jnp.full((E, CAP), T, jnp.int32).at[sorted_e, pos].set(sorted_tok, mode='drop')
            buf_w = jnp.zeros((E, CAP), x.dtype).at[sorted_e, pos].set(sorted_w, mode='drop')
            xp = jnp.concatenate([xf, jnp.zeros((1, h), x.dtype)], axis=0)
            gx = xp[buf_tok]
            gu = jnp.einsum('ech,ehi->eci', gx, gate_up_proj)
            g, u = jnp.split(gu, 2, axis=-1)
            hid = jax.nn.silu(g) * u
            eo = jnp.einsum('eci,eih->ech', hid, down_proj) * buf_w[..., None]
            routed = jnp.zeros((T + 1, h), x.dtype).at[buf_tok.reshape(-1)].add(eo.reshape(-1, h))[:T]
            shared = jax.nn.silu(xf @ shared_gate_w.T) * (xf @ shared_up_w.T) @ shared_down_w.T
            return (routed + shared).reshape(b, s, h)
        key = jax.random.key(seed)
        ks = jax.random.split(key, 7)
        x = jax.random.normal(ks[0], (B, S, H), jnp.float32)
        gate_w = jax.random.normal(ks[1], (E, H), jnp.float32) * 0.02
        gate_up_proj = jax.random.normal(ks[2], (E, H, 2 * I), jnp.float32) * 0.02
        down_proj = jax.random.normal(ks[3], (E, I, H), jnp.float32) * 0.02
        shared_gate_w = jax.random.normal(ks[4], (SI, H), jnp.float32) * 0.02
        shared_up_w = jax.random.normal(ks[5], (SI, H), jnp.float32) * 0.02
        shared_down_w = jax.random.normal(ks[6], (H, SI), jnp.float32) * 0.02
        return dict(x=x, gate_w=gate_w, gate_up_proj=gate_up_proj, down_proj=down_proj, shared_gate_w=shared_gate_w, shared_up_w=shared_up_w, shared_down_w=shared_down_w)
    _L0_ffn_in = _L0_ffn_setup()
    _d = {'L0_attn_h_t': _L0_attn_in['h_t'], 'L0_attn_Wc': _L0_attn_in['Wc'], 'L0_attn_bc': _L0_attn_in['bc'], 'L0_attn_Wcq': _L0_attn_in['Wcq'], 'L0_attn_bcq': _L0_attn_in['bcq'], 'L0_attn_Wqr': _L0_attn_in['Wqr'], 'L0_attn_bqr': _L0_attn_in['bqr'], 'L0_attn_Wckv': _L0_attn_in['Wckv'], 'L0_attn_bckv': _L0_attn_in['bckv'], 'L0_attn_Wck': _L0_attn_in['Wck'], 'L0_attn_bck': _L0_attn_in['bck'], 'L0_attn_Wkr': _L0_attn_in['Wkr'], 'L0_attn_bkr': _L0_attn_in['bkr'], 'L0_attn_Wv': _L0_attn_in['Wv'], 'L0_attn_bv': _L0_attn_in['bv'], 'L0_attn_Wo': _L0_attn_in['Wo'], 'L0_attn_bo': _L0_attn_in['bo'], 'L0_ffn_gate_w': _L0_ffn_in['gate_w'], 'L0_ffn_gate_up_proj': _L0_ffn_in['gate_up_proj'], 'L0_ffn_down_proj': _L0_ffn_in['down_proj'], 'L0_ffn_shared_gate_w': _L0_ffn_in['shared_gate_w'], 'L0_ffn_shared_up_w': _L0_ffn_in['shared_up_w'], 'L0_ffn_shared_down_w': _L0_ffn_in['shared_down_w']}
    _x0 = _d['L0_attn_h_t']
    _d['L0_attn_h_t'] = jax.random.normal(jax.random.fold_in(jax.random.key(seed), 1), (4, 2048, 512), dtype=_x0.dtype)
    del _x0
    return _d

def reference(L0_attn_h_t, L0_attn_Wc, L0_attn_bc, L0_attn_Wcq, L0_attn_bcq, L0_attn_Wqr, L0_attn_bqr, L0_attn_Wckv, L0_attn_bckv, L0_attn_Wck, L0_attn_bck, L0_attn_Wkr, L0_attn_bkr, L0_attn_Wv, L0_attn_bv, L0_attn_Wo, L0_attn_bo, L0_ffn_gate_w, L0_ffn_gate_up_proj, L0_ffn_down_proj, L0_ffn_shared_gate_w, L0_ffn_shared_up_w, L0_ffn_shared_down_w):

    def _L0_attn_ref(h_t, Wc, bc, Wcq, bcq, Wqr, bqr, Wckv, bckv, Wck, bck, Wkr, bkr, Wv, bv, Wo, bo):
        import jax, jax.numpy as jnp
        import numpy as np
        B, S, D = (2, 1024, 512)
        H = 16
        DC = 128
        DKQV = 512
        DR = 256
        DCKV = 128
        DOUT = 512
        DH = DKQV // H
        DRH = DR // H
        SCALER = 1.0 / float(np.sqrt(DH + DRH))

        def _rope(x):
            dr = x.shape[-1]
            inv_freq = 1.0 / 10000.0 ** (jnp.arange(0, dr, 2, dtype=jnp.float32) / dr)
            t = jnp.arange(x.shape[1], dtype=jnp.float32)
            freqs = t[:, None] * inv_freq[None, :]
            emb = jnp.concatenate([freqs, freqs], axis=-1)[None, :, None, :]
            x1, x2 = jnp.split(x, 2, axis=-1)
            rot = jnp.concatenate([-x2, x1], axis=-1)
            return x * jnp.cos(emb) + rot * jnp.sin(emb)
        b, s = (h_t.shape[0], h_t.shape[1])
        cq = h_t @ Wc + bc
        q = (cq @ Wcq + bcq).reshape(b, s, H, DH)
        qr = _rope((cq @ Wqr + bqr).reshape(b, s, H, DRH))
        q = jnp.concatenate([q, qr], axis=-1)
        ckv = h_t @ Wckv + bckv
        k = (ckv @ Wck + bck).reshape(b, s, H, DH)
        kr = _rope((h_t @ Wkr + bkr).reshape(b, s, H, DRH))
        k = jnp.concatenate([k, kr], axis=-1)
        v = (ckv @ Wv + bv).reshape(b, s, H, DH)
        scores = jnp.einsum('bsid,bsjd->bsij', q, k) * SCALER
        attn = jax.nn.softmax(scores, axis=-1)
        out = jnp.einsum('bsij,bsjd->bsid', attn, v).reshape(b, s, DKQV)
        return out @ Wo + bo

    def _L0_ffn_ref(x, gate_w, gate_up_proj, down_proj, shared_gate_w, shared_up_w, shared_down_w):
        import jax, jax.numpy as jnp
        import numpy as np
        E = 64
        K = 6
        CAP = 128
        SCALE = 1.0
        H = 512
        I = 192
        SI = I * 2
        B, S = (2, 256)

        def _moe(x, gate_w, gate_up_proj, down_proj, shared_gate_w, shared_up_w, shared_down_w):
            b, s, h = x.shape
            T = b * s
            xf = x.reshape(T, h)
            scores = jax.nn.softmax(xf @ gate_w.T, axis=-1)
            topk_w, topk_idx = jax.lax.top_k(scores, K)
            topk_w = topk_w * SCALE
            flat_e = topk_idx.reshape(-1)
            order = jnp.argsort(flat_e)
            sorted_e = flat_e[order]
            sorted_tok = (order // K).astype(jnp.int32)
            sorted_w = topk_w.reshape(-1)[order]
            counts = jnp.zeros((E,), jnp.int32).at[flat_e].add(1)
            offsets = jnp.cumsum(counts) - counts
            pos = jnp.arange(T * K, dtype=jnp.int32) - offsets[sorted_e]
            buf_tok = jnp.full((E, CAP), T, jnp.int32).at[sorted_e, pos].set(sorted_tok, mode='drop')
            buf_w = jnp.zeros((E, CAP), x.dtype).at[sorted_e, pos].set(sorted_w, mode='drop')
            xp = jnp.concatenate([xf, jnp.zeros((1, h), x.dtype)], axis=0)
            gx = xp[buf_tok]
            gu = jnp.einsum('ech,ehi->eci', gx, gate_up_proj)
            g, u = jnp.split(gu, 2, axis=-1)
            hid = jax.nn.silu(g) * u
            eo = jnp.einsum('eci,eih->ech', hid, down_proj) * buf_w[..., None]
            routed = jnp.zeros((T + 1, h), x.dtype).at[buf_tok.reshape(-1)].add(eo.reshape(-1, h))[:T]
            shared = jax.nn.silu(xf @ shared_gate_w.T) * (xf @ shared_up_w.T) @ shared_down_w.T
            return (routed + shared).reshape(b, s, h)
        return _moe(x, gate_w, gate_up_proj, down_proj, shared_gate_w, shared_up_w, shared_down_w)
    x = L0_attn_h_t
    x = x + _layernorm(_L0_attn_ref(_layernorm(x, axis=-1), L0_attn_Wc, L0_attn_bc, L0_attn_Wcq, L0_attn_bcq, L0_attn_Wqr, L0_attn_bqr, L0_attn_Wckv, L0_attn_bckv, L0_attn_Wck, L0_attn_bck, L0_attn_Wkr, L0_attn_bkr, L0_attn_Wv, L0_attn_bv, L0_attn_Wo, L0_attn_bo), axis=-1)
    x = x + _layernorm(_L0_ffn_ref(_layernorm(x, axis=-1), L0_ffn_gate_w, L0_ffn_gate_up_proj, L0_ffn_down_proj, L0_ffn_shared_gate_w, L0_ffn_shared_up_w, L0_ffn_shared_down_w), axis=-1)
    return x

_drawn_inputs = setup_inputs


def setup_inputs(seed=0):
    import zlib

    import numpy as np

    out = dict(_drawn_inputs(seed))
    spreads = {}
    factors = {'L0_attn_bc': 8.0,
     'L0_attn_bcq': 5.344,
     'L0_attn_bqr': 4.533,
     'L0_attn_bck': 5.747,
     'L0_attn_bkr': 8.0}
    for name, (base, spread) in spreads.items():
        noise = np.random.default_rng([zlib.crc32(name.encode()), seed]).standard_normal(out[name].shape)
        drawn = base * np.exp(spread * noise) if base else spread * noise
        out[name] = jnp.asarray(drawn.astype(out[name].dtype))
    for name, factor in factors.items():
        out[name] = (out[name] * factor).astype(out[name].dtype)
    return out
```

```python
from contextlib import ExitStack

import numpy as np

import concourse.bass as bass
from concourse import mybir

F32 = mybir.dt.float32
F32R = mybir.dt.float32r
BF16 = mybir.dt.bfloat16
I32 = mybir.dt.int32
U32 = mybir.dt.uint32
ALU = mybir.AluOpType
ACT = mybir.ActivationFunctionType
AX = mybir.AxisListType

P = 128
T = 4 * 2048
NT = T // P
D = 512
KD = D // P
H = 16
DH = 32
DR = 16
DQ = DH + DR
HS = 64
DC = 128
SCALE = 1.0 / float(np.sqrt(DQ))
E = 64
TOPK = 6
CAP = 128
I = 192
SI = 384
EPS = 1e-5
B4 = 4
NBLK = P // (2 * B4)
BIG = 1.0e30
KEY0 = 16384.0
GU = SI + E // 2

C_ID, C_TRI, C_EB, C_NEG, C_TRASH, C_TOK, C_END = np.cumsum([0, P, P, E, B4, 8, 1]).tolist()


def constants():
    c = np.zeros((P, C_END), np.float32)
    p = np.arange(P)
    c[:, C_ID:C_ID + P] = np.eye(P)
    c[:, C_TRI:C_TRI + P] = p[:, None] < p[None, :]
    c[:, C_EB:C_EB + E] = KEY0 - CAP * np.arange(E)
    c[:, C_NEG:C_NEG + B4] = np.where((p[:, None] // H) % B4 == np.arange(B4), 0.0, -BIG)
    c[:, C_TRASH:C_TRASH + 8] = p[:, None] + P * np.arange(8) + E * CAP - KEY0
    c[:, C_TOK] = p
    slots = np.tile(T + np.arange(CAP, dtype=np.int32), E + TOPK).reshape((E + TOPK) * CAP, 1)
    return c, slots


class Count:

    def __init__(self, sem, per, total, n=1, place=0):
        self.sem, self.per, self.total, self.n, self.place = sem, per, total, n, place

    def at(self, t, k=None):
        k = self.per if k is None else k
        if not isinstance(t, int):
            return t * (self.per // self.n) + (k - self.place * self.per // self.n)
        m = (t - self.place) // self.n
        return min(max(m * self.per + k, 0) if m >= 0 else 0, self.total // self.n * self.per)


def layer_kernel(nc, x, cst, slot_init, w_lat, b_lat, w_q, b_q, w_ck, b_ck, w_v, b_v, w_o, b_o,
                 w_gu, w_sd, w_eg, w_ed, out):
    x1_d = nc.dram_tensor("x1_scratch", (T, D), F32).ap()
    xf_d = nc.dram_tensor("xf_scratch", (T + CAP, D + E), F32).ap()
    acc_d = nc.dram_tensor("acc_scratch", (T + CAP, D), F32).ap()
    v_d = nc.dram_tensor("v_scratch", (2, P, D), F32).ap()
    o_d = nc.dram_tensor("o_scratch", (2, P, D), F32).ap()
    slot_d = nc.dram_tensor("slot_scratch", ((E + TOPK) * CAP, 1), I32).ap()

    token_pipeline(nc, x, cst, slot_init, w_lat, b_lat, w_q, b_q, w_ck, b_ck, w_v, b_v, w_o, b_o, w_gu, w_sd,
                   x1_d, xf_d, acc_d, v_d, o_d, slot_d)
    experts(nc, cst, w_eg, w_ed, xf_d, acc_d, slot_d)
    last_norm(nc, x1_d, acc_d, out)


def token_pipeline(nc, x, cst, slot_init, w_lat, b_lat, w_q, b_q, w_ck, b_ck, w_v, b_v, w_o, b_o, w_gu, w_sd,
                   x1_d, xf_d, acc_d, v_d, o_d, slot_d):
    ctx = ExitStack()
    with ctx:
        def sb(name, shape, dt=F32):
            return ctx.enter_context(nc.sbuf_tensor(name, shape, dt))

        def sem(name):
            return ctx.enter_context(nc.semaphore(name))

        def count(name, per=1, n=1, place=0):
            return Count(sem(name), per, NT, n, place)

        bank = [ctx.enter_context(nc.psum_tensor(f"bank{n}", [P, 512], F32)) for n in range(2, 8)]
        score_ps = ctx.enter_context(nc.psum_tensor("score_ps", [P, 1024], F32))
        b2, b3, b4, b5, b6, b7 = (b[:] for b in bank)

        c = sb("c", [P, C_END])
        ident = c[:, C_ID:C_ID + P]
        tri = sb("tri", [P, P], BF16)
        ones = sb("ones", [P, P], BF16)
        mhalf = sb("mhalf", [P, 1])
        wlat = sb("wlat", [P, 2, KD, 512], F32R)
        wq = sb("wq", [P, 2, 1, H * DQ], F32R)
        wck = sb("wck", [P, 2, 1, D], F32R)
        wv = sb("wv", [P, 2, 1, D], F32R)
        wo = sb("wo", [P, 2, KD, D], F32R)
        wgu = sb("wgu", [P, 2, KD, 2 * GU], F32R)
        wsd = sb("wsd", [P, 2, SI // P, D], F32R)
        blat = sb("blat", [P, 512])
        bq = sb("bq", [P, H * DQ])
        bck = sb("bck", [P, D])
        bv = sb("bv", [P, D])
        bo = sb("bo", [P, D])
        xin = sb("xin", [P, 2, D])
        xn = sb("xn", [P, D])
        xT = sb("xT", [P, 2, KD, P], F32R)
        lat = sb("lat", [P, 2 * DC])
        latT = sb("latT", [P, 2, 2, P], F32R)
        q = sb("q", [P, H, HS])
        k = sb("k", [P, 2, H, HS])
        v = sb("v", [P, D])
        vbd = sb("vbd", [P, 2, NBLK, 2, DH])
        qT_all = sb("qT", [P, P, H])
        kT_all = sb("kT", [P, P, H])
        qT, kT = qT_all[0:DQ], kT_all[0:DQ]
        prob = sb("prob", [P, NBLK, B4, H])
        probT = sb("probT", [P, 8, P])
        o = sb("o", [P, D])
        oin = sb("oin", [P, D])
        oT = sb("oT", [P, 2, KD, P], F32R)
        y = sb("y", [P, D])
        yn = sb("yn", [P, D])
        xres = sb("xres", [P, D])
        x1 = sb("x1", [P, D])
        xf = sb("xf", [P, 2, D + E])
        xfT = sb("xfT", [P, 2, KD, P], F32R)
        th = sb("th", [P, 2, I])
        h = sb("h", [P, SI])
        hT = sb("hT", [P, 2, SI // P, P], F32R)
        sh = sb("sh", [P, D])
        zero = sb("zero", [P, D + E])
        st = [sb(f"st{n}", [P, 6]) for n in range(3)]
        mv = [sb(f"mv{n}", [P, 2]) for n in range(3)]
        ve = [sb(f"ve{n}", [P, 1]) for n in range(3)]
        rstd = [sb(f"rstd{n}", [P, 1]) for n in range(3)]
        smax4 = sb("smax4", [P, NBLK, B4])
        smask4 = sb("smask4", [P, NBLK, B4])
        smax = sb("smax", [P, NBLK])
        sref = sb("sref", [P, NBLK, B4])
        ssum = sb("ssum", [P, NBLK])
        srec = sb("srec", [P, NBLK])
        lg = sb("lg", [P, E + 2])
        top = sb("top", [P, 8])
        rep = sb("rep", [P, 8])
        lgr = sb("lgr", [P, E + 2])
        ntop = sb("ntop", [P, 1])
        ex = sb("ex", [P, E])
        esum = sb("esum", [P, 1])
        erec = sb("erec", [P, 1])
        chosen = sb("chosen", [P, E], BF16)
        before = sb("before", [P, E], BF16)
        fits = sb("fits", [P, E])
        key = sb("key", [P, E])
        key2 = sb("key2", [P, E])
        key8 = sb("key8", [P, 8])
        none8 = sb("none8", [P, 8])
        slot = sb("slot", [P, 8], I32)
        tok = sb("tok", [P, 1])
        toki = sb("toki", [P, 1], I32)

        flat = lambda ap: ap.rearrange("p a b -> p (a b)")
        qs, ks, vs = flat(qT_all[:]), flat(kT_all[:]), vbd[:].rearrange("p a n b d -> p (a n b d)")
        ps, pts = prob[:].rearrange("p n t h -> p (n t h)"), flat(probT[:])
        parts = [(qs[:, 512 * n:512 * n + 512], wlat, n, w_lat[n * P:(n + 1) * P, :]) for n in range(KD)]
        parts += [(ks[:, 0:H * DQ], wq, 0, w_q), (ks[:, 768:1280], wck, 0, w_ck), (ks[:, 1280:1792], wv, 0, w_v)]
        parts += [(vs[:, D * n:D * n + D], wo, n, w_o[n * P:(n + 1) * P, :]) for n in range(KD)]
        parts += [(st_, wgu, n, w_gu[n * P:(n + 1) * P, :])
                  for n, st_ in enumerate((ps[:, 0:2 * GU], pts[:, 0:2 * GU], qs[:, 0:2 * GU], qs[:, 1024:1024 + 2 * GU]))]
        parts += [(ks[:, D * n:D * n + D], wsd, n, w_sd[n * P:(n + 1) * P, :]) for n in range(SI // P)]
        WAIT_FOR = {13: 4, 14: 4, 15: 7, 16: 7, 17: 7}

        consts_in = sem("consts_in")
        part_in = [sem(f"part_in{n}") for n in range(len(parts))]
        biases_in = sem("biases_in")
        part_hi = sem("part_hi")
        part_lo = sem("part_lo")
        scratch_init = sem("scratch_init")
        zeroed = sem("zeroed")
        cast_done = sem("cast_done")
        x_in = [count(f"x_in{n}", 16, 2, n) for n in range(2)]
        xres_in = count("xres_in", 16)
        v_out = count("v_out", 16)
        v_in = [count(f"v_in{n}", 32, 2, n) for n in range(2)]
        o_out = count("o_out", 64)
        o_in = count("o_in", 16)
        x1_out = count("x1_out", 16)
        acc_out = count("acc_out", 16)
        xf_out = [count(f"xf_out{n}", 16, 2, n) for n in range(2)]
        slots_out = count("slots_out", 16 * TOPK)
        pe_xT = count("pe_xT")
        pe_lat = count("pe_lat")
        pe_latT = count("pe_latT")
        pe_q = count("pe_q", 2)
        pe_k = count("pe_k")
        pe_v = count("pe_v")
        pe_qT = count("pe_qT", 2)
        pe_kT = count("pe_kT", 2)
        pe_s = count("pe_s")
        pe_pT = count("pe_pT", 2)
        pe_pv = count("pe_pv")
        pe_oT = count("pe_oT")
        pe_wo = count("pe_wo")
        pe_xfT = count("pe_xfT")
        pe_gu = count("pe_gu", 2)
        pe_hT = count("pe_hT")
        pe_sh = count("pe_sh")
        pe_pos = count("pe_pos")
        a_xT = count("a_xT")
        a_latT = count("a_latT")
        a_qT = count("a_qT", 4)
        a_kT = count("a_kT", 4)
        a_exp = count("a_exp")
        a_pT = count("a_pT", 2)
        a_oT = count("a_oT")
        a_xfT = count("a_xfT")
        a_th = count("a_th", 2)
        a_hT = count("a_hT")
        a_sh = count("a_sh")
        a_gate = count("a_gate")
        d_ln = [count(f"d_ln{n}", 3) for n in range(3)]
        d_xT = count("d_xT")
        d_latT = count("d_latT")
        d_oT = count("d_oT")
        d_xfT = count("d_xfT")
        d_hT = count("d_hT")
        d_y = count("d_y")
        d_lat = count("d_lat", 2)
        d_q = count("d_q", 2)
        d_k = count("d_k")
        d_v = count("d_v")
        d_s = count("d_s", 7)
        d_pv = count("d_pv")
        d_h = count("d_h", 4)
        d_r = count("d_r", 9)
        d_pos = count("d_pos", 9)
        g_rstd = [count(f"g_rstd{n}", 2) for n in range(3)]
        g_x1 = count("g_x1")

        block = ctx.enter_context(nc.Block())

        FIRST, LOOP, LAST = -2, 6, NT + 4
        REST = NT - 2
        PAIRS = (REST - LOOP) // 2
        assert LOOP + 2 * PAIRS == REST

        def active(t):
            return not isinstance(t, int) or 0 <= t < NT

        def pipeline(eng, iteration):
            for i in range(FIRST, LOOP):
                iteration(i, i % 2, True)
            with eng.Fori(0, PAIRS) as r:
                for u in range(2):
                    iteration(r * 2 + (LOOP + u), (LOOP + u) % 2, False)
            for i in range(REST, LAST):
                iteration(i, i % 2, True)

        def settle(eng):
            eng.nop(nofuse=True)

        def rows(ap, t):
            return ap[t * P:(t + 1) * P, :] if isinstance(t, int) else ap[bass.ts(t, P), :]

        @block.sync
        def _(sp):
            sp.dma_start(c[:], cst).then_inc(consts_in, 16)
            for n, (stage, _, _, src) in enumerate(parts):
                if n in WAIT_FOR:
                    sp.wait_ge(part_lo, WAIT_FOR[n])
                sp.dma_start(stage, src).then_inc(part_in[n], 16)
            for dst, src in ((blat, b_lat), (bq, b_q), (bck, b_ck), (bv, b_v), (bo, b_o)):
                sp.dma_start(dst[:], src.partition_broadcast(P)).then_inc(biases_in, 16)

            def iteration(i, par, peeled):
                if active(i + 2):
                    sp.wait_ge(d_ln[0].sem, d_ln[0].at(i))
                    settle(sp)
                    sp.dma_start(xin[:, par, :], rows(x, i + 2)).then_inc(x_in[par].sem, 16)
                if peeled and i == FIRST:
                    sp.dma_start(slot_d, slot_init).then_inc(scratch_init, 16)
                    sp.wait_ge(zeroed, 3)
                    sp.dma_start(xf_d[T:T + CAP, :], zero[:]).then_inc(scratch_init, 16)
                    sp.dma_start(acc_d[T:T + CAP, :], zero[:, 0:D]).then_inc(scratch_init, 16)
                if active(i - 3):
                    sp.wait_ge(g_x1.sem, g_x1.at(i - 4))
                    settle(sp)
                    sp.dma_start(xres[:], rows(x, i - 3)).then_inc(xres_in.sem, 16)
                if active(i - 1):
                    sp.wait_ge(d_v.sem, d_v.at(i - 1))
                    sp.wait_ge(v_in[1 - par].sem, v_in[1 - par].at(i - 3))
                    sp.dma_start(v_d[1 - par], v[:]).then_inc(v_out.sem, 16)
                    sp.wait_ge(v_out.sem, v_out.at(i - 1))
                    settle(sp)
                    sp.wait_ge(pe_pv.sem, pe_pv.at(i - 3))
                    settle(sp)
                    src = v_d[1 - par].rearrange("(cg b t) (j d) -> b (t j) cg d", cg=NBLK, b=2, j=H)
                    for b in range(2):
                        sp.dma_start(vbd[64 * b:64 * b + 64, 1 - par, :, b, :], src[b]).then_inc(v_in[1 - par].sem, 16)
                if active(i - 3):
                    sp.wait_ge(g_x1.sem, g_x1.at(i - 3))
                    settle(sp)
                    sp.dma_start(rows(x1_d, i - 3), x1[:]).then_inc(x1_out.sem, 16)
                if active(i - 4):
                    sp.wait_ge(a_sh.sem, a_sh.at(i - 4))
                    settle(sp)
                    sp.dma_start(rows(acc_d, i - 4), sh[:]).then_inc(acc_out.sem, 16)
                    sp.wait_ge(d_r.sem, d_r.at(i - 4))
                    settle(sp)
                    sp.dma_start(rows(xf_d, i - 4), xf[:, par, :]).then_inc(xf_out[par].sem, 16)
                if active(i - 2):
                    sp.wait_ge(d_pv.sem, d_pv.at(i - 2))
                    sp.wait_ge(o_in.sem, o_in.at(i - 4))
                    dst = o_d[par].rearrange("(c g b t) (h d) -> g b (t h) c d", c=8, g=2, b=2, h=H)
                    src = o[:].rearrange("p (c b d) -> p b c d", c=8, b=2)
                    for g in range(2):
                        for b in range(2):
                            sp.dma_start(dst[g, b], src[64 * g:64 * g + 64, b]).then_inc(o_out.sem, 16)
                    sp.wait_ge(o_out.sem, o_out.at(i - 2))
                    sp.wait_ge(pe_oT.sem, pe_oT.at(i - 3))
                    sp.dma_start(oin[:], o_d[par]).then_inc(o_in.sem, 16)

            pipeline(sp, iteration)
            sp.wait_ge(acc_out.sem, acc_out.at(NT - 1))
            sp.wait_ge(x1_out.sem, x1_out.at(NT - 1))
            for n in range(2):
                sp.wait_ge(xf_out[n].sem, xf_out[n].at(NT - 2 + n))

        @block.tensor
        def _(pe):
            pe.wait_ge(consts_in, 16)
            pe.wait_ge(part_lo, len(parts))
            pe.wait_ge(cast_done, 1)

            def transposes(dst, srcs, done):
                for n, s in enumerate(srcs):
                    last = nc.tensor.transpose(dst[0:s.shape[1], n * P:(n + 1) * P], s, ident)
                last.then_inc(done.sem, 1)

            def product(dst, lhs, rhs, done):
                for n, (a, b) in enumerate(zip(lhs, rhs)):
                    nc.tensor.matmul(dst, a[:, 0], b[:, 0], start=(n == 0), stop=False)
                    nc.tensor.matmul(dst, a[:, 0], b[:, 1], start=False, stop=False)
                    last = nc.tensor.matmul(dst, a[:, 1], b[:, 0], start=False, stop=(n == len(lhs) - 1))
                last.then_inc(done.sem, 1)

            def iteration(i, par, peeled):
                if peeled:
                    for cnt, s in ((d_xT, 1), (d_lat, 1), (d_latT, 1), (d_q, 2), (d_k, 2), (d_v, 2), (a_qT, 3),
                                   (a_kT, 3), (a_pT, 3), (d_pv, 3), (d_oT, 4), (d_y, 4), (d_xfT, 4), (d_h, 5),
                                   (d_hT, 5), (a_sh, 5), (d_pos, 5)):
                        pe.wait_ge(cnt.sem, cnt.at(i - s))
                if active(i):
                    pe.wait_ge(d_ln[0].sem, d_ln[0].at(i))
                    pe.wait_ge(d_xfT.sem, d_xfT.at(i - 4))
                    transposes(b2, [xn[:, n * P:(n + 1) * P] for n in range(KD)], pe_xT)

                def turn(src, done, n, dst):
                    transposes(dst, [src[:, 2 * m:2 * m + 2, :].rearrange("p h d -> p (h d)")
                                     for m in range(4 * n, 4 * n + 4)], done)

                if active(i - 2):
                    pe.wait_ge(d_q.sem, d_q.at(i - 2))
                    pe.wait_ge(a_pT.sem, a_pT.at(i - 3))
                    turn(q, pe_qT, 0, b3)
                if active(i - 2):
                    pe.wait_ge(d_xT.sem, d_xT.at(i))
                    turn(q, pe_qT, 1, b2)
                if active(i - 4):
                    pe.wait_ge(d_xfT.sem, d_xfT.at(i - 4))
                    pe.wait_ge(d_y.sem, d_y.at(i - 4))
                    product(b7[:, 0:GU], [xfT[:, :, n, :] for n in range(KD)], [wgu[:, :, n, 0:GU] for n in range(KD)], pe_gu)
                if active(i - 4):
                    pe.wait_ge(a_sh.sem, a_sh.at(i - 5))
                    product(b4[:, 0:GU], [xfT[:, :, n, :] for n in range(KD)], [wgu[:, :, n, GU:] for n in range(KD)], pe_gu)
                if active(i - 2):
                    pe.wait_ge(d_k.sem, d_k.at(i - 2))
                    pe.wait_ge(d_lat.sem, d_lat.at(i - 2))
                    pe.wait_ge(a_qT.sem, a_qT.at(i - 2, 2))
                    turn(k[:, par], pe_kT, 0, b3)
                    pe.wait_ge(a_qT.sem, a_qT.at(i - 2, 4))
                    turn(k[:, par], pe_kT, 1, b2)
                if active(i):
                    pe.wait_ge(d_xT.sem, d_xT.at(i))
                    pe.wait_ge(d_pv.sem, d_pv.at(i - 3))
                    product(b5, [xT[:, :, n, :] for n in range(KD)], [wlat[:, :, n, :] for n in range(KD)], pe_lat)
                if active(i - 3):
                    pe.wait_ge(o_in.sem, o_in.at(i - 3))
                    pe.wait_ge(a_kT.sem, a_kT.at(i - 2, 2))
                    transposes(b3, [oin[:, n * P:(n + 1) * P] for n in range(KD)], pe_oT)
                if active(i - 1):
                    pe.wait_ge(d_latT.sem, d_latT.at(i - 1))
                    pe.wait_ge(d_pos.sem, d_pos.at(i - 5))
                    product(b6, [latT[:, :, 1, :]], [wv[:, :, 0, :]], pe_v)
                if active(i - 2):
                    pe.wait_ge(a_kT.sem, a_kT.at(i - 2))
                    pe.wait_ge(d_s.sem, d_s.at(i - 3, 5))
                    settle(pe)
                    for blk in range(NBLK):
                        for g in range(2):
                            t0 = (blk // 2) * 16 + g * 8 + (blk % 2) * B4
                            last = nc.tensor.matmul(score_ps[64 * g:64 * g + 64, blk * 64:blk * 64 + 64],
                                                    qT[:, t0:t0 + B4, :].rearrange("p t h -> p (t h)"),
                                                    kT[:, t0:t0 + B4, :].rearrange("p t h -> p (t h)"),
                                                    start=True, stop=True)
                    last.then_inc(pe_s.sem, 1)
                if active(i - 3):
                    pe.wait_ge(d_oT.sem, d_oT.at(i - 3))
                    pe.wait_ge(d_h.sem, d_h.at(i - 4, 2))
                    pe.wait_ge(d_r.sem, d_r.at(i - 4, 2))
                    product(b7, [oT[:, :, n, :] for n in range(KD)], [wo[:, :, n, :] for n in range(KD)], pe_wo)
                if active(i - 4):
                    pe.wait_ge(d_h.sem, d_h.at(i - 4))
                    pe.wait_ge(a_kT.sem, a_kT.at(i - 2, 4))
                    transposes(b2, [h[:, n * P:(n + 1) * P] for n in range(SI // P)], pe_hT)
                if active(i - 1):
                    pe.wait_ge(d_h.sem, d_h.at(i - 4))
                    pe.wait_ge(d_r.sem, d_r.at(i - 4, 2))
                    for n, b in enumerate((b4, b5)):
                        if n == 1:
                            pe.wait_ge(d_lat.sem, d_lat.at(i))
                        product(b[:, 0:8 * DQ], [latT[:, :, 0, :]], [wq[:, :, 0, n * 8 * DQ:(n + 1) * 8 * DQ]], pe_q)
                    pe.wait_ge(d_v.sem, d_v.at(i - 1))
                    product(b6, [latT[:, :, 1, :]], [wck[:, :, 0, :]], pe_k)
                if active(i):
                    pe.wait_ge(d_lat.sem, d_lat.at(i))
                    pe.wait_ge(d_oT.sem, d_oT.at(i - 3))
                    transposes(b3, [lat[:, n * P:(n + 1) * P] for n in range(2)], pe_latT)
                if active(i - 4):
                    pe.wait_ge(d_hT.sem, d_hT.at(i - 4))
                    pe.wait_ge(d_q.sem, d_q.at(i - 1, 1))
                    product(b4, [hT[:, :, n, :] for n in range(SI // P)], [wsd[:, :, n, :] for n in range(SI // P)], pe_sh)
                if active(i - 2):
                    pe.wait_ge(a_exp.sem, a_exp.at(i - 2))
                    pe.wait_ge(d_hT.sem, d_hT.at(i - 4))
                    pr = prob[:].rearrange("p n t h -> p (n t h)")
                    transposes(b2, [pr[:, n * P:(n + 1) * P] for n in range(4)], pe_pT)
                    pe.wait_ge(d_latT.sem, d_latT.at(i))
                    transposes(b3, [pr[:, n * P:(n + 1) * P] for n in range(4, 8)], pe_pT)
                if active(i - 4):
                    pe.wait_ge(d_k.sem, d_k.at(i - 1))
                    pe.wait_ge(d_r.sem, d_r.at(i - 4))
                    pe.wait_ge(d_pos.sem, d_pos.at(i - 5))
                    nc.tensor.matmul(b6[:, 0:E], tri[:], chosen[:], start=True, stop=False)
                    nc.tensor.matmul(b6[:, 0:E], ones[:], before[:], start=False, stop=True).then_inc(pe_pos.sem, 1)
                if active(i - 2):
                    pe.wait_ge(a_pT.sem, a_pT.at(i - 2))
                    pe.wait_ge(d_q.sem, d_q.at(i - 1))
                    pe.wait_ge(v_in[par].sem, v_in[par].at(i - 2))
                    settle(pe)
                    for n in range(8):
                        for g in range(2):
                            last = nc.tensor.matmul(b5[64 * g:64 * g + 64, n * 64:n * 64 + 64],
                                                    probT[:, n, 64 * g:64 * g + 64],
                                                    vbd[:, par, 2 * n + g].rearrange("p b d -> p (b d)"),
                                                    start=True, stop=True)
                    last.then_inc(pe_pv.sem, 1)
                if active(i - 3):
                    pe.wait_ge(d_ln[2].sem, d_ln[2].at(i - 3))
                    pe.wait_ge(a_pT.sem, a_pT.at(i - 2, 1))
                    transposes(b2, [xf[:, 1 - par, n * P:(n + 1) * P] for n in range(KD)], pe_xfT)

            pipeline(pe, iteration)

        @block.scalar
        def _(act):
            for n, (stage, w, m, _) in enumerate(parts):
                act.wait_ge(part_in[n], 16)
                nc.scalar.copy(w[:, 0, m, :], stage).then_inc(part_hi, 1)
            act.wait_ge(part_lo, len(parts))

            def copy(dst, src, done):
                nc.scalar.copy(dst, src).then_inc(done.sem, 1)

            def iteration(i, par, peeled):
                def spread(dst, src, done, n):
                    dv = dst.rearrange("p t (m a) -> p a m t", a=2)
                    for a in range(2):
                        copy(dv[:, a, 4 * n:4 * n + 4, :],
                             src[64 * a:64 * a + DQ, :].rearrange("p (m t) -> p m t", t=P), done)

                if active(i):
                    act.wait_ge(pe_xT.sem, pe_xT.at(i))
                    act.wait_ge(pe_lat.sem, pe_lat.at(i - 1))
                    copy(xT[:, 0].rearrange("p k t -> p (k t)"), b2[:], a_xT)
                if active(i - 2):
                    act.wait_ge(pe_s.sem, pe_s.at(i - 3))
                    act.wait_ge(pe_qT.sem, pe_qT.at(i - 2, 1))
                    spread(qT, b3, a_qT, 0)
                if active(i - 4):
                    act.wait_ge(pe_gu.sem, pe_gu.at(i - 4, 1))
                    act.wait_ge(d_h.sem, d_h.at(i - 5))
                    nc.scalar.activation(th[:, 0, :], b7[:, 0:I], ACT.Tanh, scale=0.5).then_inc(a_th.sem, 1)
                if active(i - 2):
                    act.wait_ge(pe_qT.sem, pe_qT.at(i - 2, 2))
                    spread(qT, b2, a_qT, 1)
                if active(i - 4):
                    act.wait_ge(pe_gu.sem, pe_gu.at(i - 4, 2))
                    nc.scalar.activation(th[:, 1, :], b4[:, 0:I], ACT.Tanh, scale=0.5).then_inc(a_th.sem, 1)
                if active(i - 2):
                    act.wait_ge(pe_kT.sem, pe_kT.at(i - 2, 1))
                    spread(kT, b3, a_kT, 0)
                    act.wait_ge(pe_kT.sem, pe_kT.at(i - 2, 2))
                    spread(kT, b2, a_kT, 1)
                if active(i - 4):
                    act.wait_ge(d_r.sem, d_r.at(i - 4, 4))
                    nc.scalar.activation(ex[:], lg[:, 0:E], ACT.Exp, bias=ntop[:, 0:1],
                                         accum_out=esum[:, 0:1]).then_inc(a_gate.sem, 1)
                if active(i - 3):
                    act.wait_ge(pe_oT.sem, pe_oT.at(i - 3))
                    act.wait_ge(pe_wo.sem, pe_wo.at(i - 4))
                    copy(oT[:, 0].rearrange("p k t -> p (k t)"), b3[:], a_oT)
                if active(i - 4):
                    act.wait_ge(pe_hT.sem, pe_hT.at(i - 4))
                    act.wait_ge(pe_sh.sem, pe_sh.at(i - 5))
                    copy(hT[:, 0].rearrange("p k t -> p (k t)"), b2[:, 0:SI], a_hT)
                if active(i - 2):
                    act.wait_ge(d_s.sem, d_s.at(i - 2, 5))
                    pf = prob[:].rearrange("p n t h -> p (n t h)")
                    nc.scalar.activation(pf, pf, ACT.Exp, scale=SCALE).then_inc(a_exp.sem, 1)
                if active(i):
                    act.wait_ge(pe_latT.sem, pe_latT.at(i))
                    act.wait_ge(pe_k.sem, pe_k.at(i - 1))
                    copy(latT[:, 0].rearrange("p k t -> p (k t)"), b3[:, 0:2 * P], a_latT)
                if active(i - 4):
                    act.wait_ge(pe_sh.sem, pe_sh.at(i - 4))
                    act.wait_ge(acc_out.sem, acc_out.at(i - 5))
                    copy(sh[:], b4[:], a_sh)
                if active(i - 2):
                    act.wait_ge(pe_pv.sem, pe_pv.at(i - 3))
                    for n, b in enumerate((b2, b3)):
                        act.wait_ge(pe_pT.sem, pe_pT.at(i - 2, n + 1))
                        copy(probT[:, 4 * n:4 * n + 4, :].rearrange("p k t -> p (k t)"), b[:], a_pT)
                if active(i - 3):
                    act.wait_ge(pe_xfT.sem, pe_xfT.at(i - 3))
                    act.wait_ge(pe_gu.sem, pe_gu.at(i - 4))
                    copy(xfT[:, 0].rearrange("p k t -> p (k t)"), b2[:], a_xfT)

            pipeline(act, iteration)

        @block.vector
        def _(dve):
            nc.vector.memset(zero[:], 0.0).then_inc(zeroed, 1)
            nc.vector.memset(q[:], 0.0)
            nc.vector.memset(k[:], 0.0)
            nc.vector.memset(before[:], 0.0)
            nc.vector.memset(ones[:], 1.0)
            nc.vector.memset(mhalf[:], -0.5)
            nc.vector.memset(lg[:, E:E + 1], -1.0e38)
            nc.vector.memset(lg[:, E + 1:E + 2], -2.0e38)
            nc.vector.memset(rep[:, 6:7], -1.0e38)
            nc.vector.memset(rep[:, 7:8], -2.0e38).then_inc(zeroed, 1)
            dve.wait_ge(consts_in, 16)
            nc.vector.tensor_copy(tok[:], c[:, C_TOK:C_TOK + 1])
            nc.vector.tensor_copy(tri[:], c[:, C_TRI:C_TRI + P]).then_inc(cast_done, 1)
            for n, (stage, w, m, _) in enumerate(parts):
                dve.wait_ge(part_hi, n + 1)
                nc.vector.tensor_tensor(w[:, 1, m, :], stage, w[:, 0, m, :].bitcast(F32), ALU.subtract).then_inc(part_lo, 1)
            dve.wait_ge(part_lo, len(parts))
            nc.vector.memset(vbd[:], 0.0).then_inc(zeroed, 1)
            dve.wait_ge(biases_in, 16 * 5)
            dve.wait_ge(zeroed, 3)
            dve.wait_ge(cast_done, 1)

            def stats(n, src, t):
                nc.vector.bn_stats(st[n][:], src).then_inc(d_ln[n].sem, 1)
                dve.wait_ge(d_ln[n].sem, d_ln[n].at(t, 1))
                dve.wait_ge(g_rstd[n].sem, g_rstd[n].at(t - 1))
                settle(dve)
                nc.vector.bn_aggr(mv[n][:], st[n][:]).then_inc(d_ln[n].sem, 1)

            def normalise(n, dst, src, t):
                dve.wait_ge(g_rstd[n].sem, g_rstd[n].at(t))
                nc.vector.tensor_scalar(dst, src, mv[n][:, 0:1], rstd[n][:, 0:1], ALU.subtract,
                                        ALU.mult).then_inc(d_ln[n].sem, 1)

            def low_part(dst, src, done):
                nc.vector.tensor_tensor(dst[:, 1].rearrange("p k t -> p (k t)"), src,
                                        dst[:, 0].bitcast(F32).rearrange("p k t -> p (k t)"),
                                        ALU.subtract).then_inc(done.sem, 1)

            def iteration(i, par, peeled):
                if active(i):
                    dve.wait_ge(a_xT.sem, a_xT.at(i))
                    low_part(xT, b2[:], d_xT)
                if active(i - 4):
                    for n, b in enumerate((b7, b4)):
                        dve.wait_ge(a_th.sem, a_th.at(i - 4, n + 1))
                        dve.wait_ge(pe_hT.sem, pe_hT.at(i - 5))
                        g = b[:, 0:I]
                        hh = h[:, n * I:(n + 1) * I]
                        nc.vector.scalar_tensor_tensor(th[:, n, :], th[:, n, :], 1.0, g, ALU.add,
                                                       ALU.mult).then_inc(d_h.sem, 1)
                        if n == 0:
                            dve.wait_ge(a_gate.sem, a_gate.at(i - 5))
                            dve.wait_ge(d_r.sem, d_r.at(i - 5))
                        nc.vector.tensor_copy(lg[:, n * 32:n * 32 + 32], b[:, 2 * I:GU]).then_inc(d_r.sem, 1)
                        dve.wait_ge(d_h.sem, d_h.at(i - 4, 2 * n + 1))
                        nc.vector.scalar_tensor_tensor(hh, th[:, n, :], 0.5, b[:, I:2 * I], ALU.mult,
                                                       ALU.mult).then_inc(d_h.sem, 1)
                    dve.wait_ge(d_r.sem, d_r.at(i - 4, 2))
                    settle(dve)
                    nc.vector.max(top[:], lg[:, 0:E]).then_inc(d_r.sem, 1)
                    dve.wait_ge(d_r.sem, d_r.at(i - 4, 3))
                    nc.vector.tensor_scalar(ntop[:], top[:, 0:1], -1.0, None, ALU.mult).then_inc(d_r.sem, 1)
                    nc.vector.tensor_copy(rep[:, 0:TOPK], top[:, 0:TOPK]).then_inc(d_r.sem, 1)
                    dve.wait_ge(d_r.sem, d_r.at(i - 4, 5))
                    settle(dve)
                    nc.vector.match_replace(lgr[:], rep[:], lg[:], -3.0e38).then_inc(d_r.sem, 1)
                if active(i):
                    dve.wait_ge(pe_lat.sem, pe_lat.at(i))
                    dve.wait_ge(pe_latT.sem, pe_latT.at(i - 1))
                    nc.vector.tensor_tensor(lat[:], b5[:, 0:2 * DC], blat[:, 0:2 * DC], ALU.add).then_inc(d_lat.sem, 1)
                    dve.wait_ge(pe_kT.sem, pe_kT.at(i - 2))
                    nc.vector.tensor_tensor(k[:, par, :, DH:DQ], b5[:, 2 * DC:].rearrange("p (h d) -> p h d", h=H),
                                            blat[:, 2 * DC:].rearrange("p (h d) -> p h d", h=H),
                                            ALU.add).then_inc(d_lat.sem, 1)
                if active(i + 1):
                    dve.wait_ge(x_in[1 - par].sem, x_in[1 - par].at(i + 1))
                    stats(0, xin[:, 1 - par, :], i + 1)
                    dve.wait_ge(pe_xT.sem, pe_xT.at(i))
                    normalise(0, xn[:], xin[:, 1 - par, :], i + 1)

                if active(i - 3):
                    dve.wait_ge(a_oT.sem, a_oT.at(i - 3))
                    low_part(oT, b3[:], d_oT)
                if active(i - 1):
                    dve.wait_ge(pe_v.sem, pe_v.at(i - 1))
                    dve.wait_ge(v_out.sem, v_out.at(i - 2))
                    nc.vector.tensor_tensor(v[:], b6[:], bv[:], ALU.add).then_inc(d_v.sem, 1)
                if active(i - 4):
                    dve.wait_ge(d_r.sem, d_r.at(i - 4, 6))
                    dve.wait_ge(pe_pos.sem, pe_pos.at(i - 5))
                    dve.wait_ge(d_pos.sem, d_pos.at(i - 5))
                    nc.vector.tensor_tensor(chosen[:], lgr[:, 0:E], lg[:, 0:E], ALU.not_equal).then_inc(d_r.sem, 1)
                    dve.wait_ge(a_gate.sem, a_gate.at(i - 4))
                    nc.vector.reciprocal(erec[:], esum[:]).then_inc(d_r.sem, 1)
                    dve.wait_ge(d_r.sem, d_r.at(i - 4, 8))
                    nc.vector.tensor_scalar(xf[:, par, D:D + E], ex[:], erec[:, 0:1], None, ALU.mult).then_inc(d_r.sem, 1)
                if active(i - 2):
                    dve.wait_ge(pe_s.sem, pe_s.at(i - 2))
                    sp4 = score_ps[:].rearrange("p (n t h) -> p n t h", n=NBLK, t=B4)
                    nc.vector.tensor_reduce(smax4[:], sp4, AX.X, ALU.max).then_inc(d_s.sem, 1)
                    dve.wait_ge(d_s.sem, d_s.at(i - 2, 1))
                    neg = c[:, C_NEG:C_NEG + B4].unsqueeze(1).broadcast_to([P, NBLK, B4])
                    nc.vector.tensor_tensor(smask4[:], smax4[:], neg, ALU.add).then_inc(d_s.sem, 1)
                    dve.wait_ge(d_s.sem, d_s.at(i - 2, 2))
                    nc.vector.tensor_reduce(smax[:], smask4[:], AX.X, ALU.max).then_inc(d_s.sem, 1)
                    dve.wait_ge(d_s.sem, d_s.at(i - 2, 3))
                    nc.vector.tensor_tensor(sref[:], smax[:].unsqueeze(2).broadcast_to([P, NBLK, B4]), neg,
                                            ALU.subtract).then_inc(d_s.sem, 1)
                    dve.wait_ge(d_s.sem, d_s.at(i - 2, 4))
                    dve.wait_ge(pe_pT.sem, pe_pT.at(i - 3))
                    nc.vector.tensor_tensor(prob[:], sp4, sref[:].unsqueeze(3).broadcast_to([P, NBLK, B4, H]),
                                            ALU.subtract).then_inc(d_s.sem, 1)
                if active(i - 4):
                    dve.wait_ge(a_hT.sem, a_hT.at(i - 4))
                    low_part(hT, b2[:, 0:SI], d_hT)
                if active(i - 3):
                    dve.wait_ge(pe_wo.sem, pe_wo.at(i - 3))
                    dve.wait_ge(d_ln[1].sem, d_ln[1].at(i - 4))
                    nc.vector.tensor_tensor(y[:], b7[:], bo[:], ALU.add).then_inc(d_y.sem, 1)
                    dve.wait_ge(d_y.sem, d_y.at(i - 3))
                    stats(1, y[:], i - 3)
                if active(i - 1):
                    dve.wait_ge(pe_qT.sem, pe_qT.at(i - 2))
                    for n, b in enumerate((b4, b5)):
                        dve.wait_ge(pe_q.sem, pe_q.at(i - 1, n + 1))
                        nc.vector.tensor_tensor(q[:, 8 * n:8 * n + 8, 0:DQ],
                                                b[:, 0:8 * DQ].rearrange("p (h d) -> p h d", d=DQ),
                                                bq[:, n * 8 * DQ:(n + 1) * 8 * DQ].rearrange("p (h d) -> p h d", d=DQ),
                                                ALU.add).then_inc(d_q.sem, 1)
                    dve.wait_ge(pe_k.sem, pe_k.at(i - 1))
                    nc.vector.tensor_tensor(k[:, 1 - par, :, 0:DH], b6[:].rearrange("p (h d) -> p h d", d=DH),
                                            bck[:].rearrange("p (h d) -> p h d", d=DH), ALU.add).then_inc(d_k.sem, 1)
                if active(i - 3):
                    dve.wait_ge(g_x1.sem, g_x1.at(i - 4))
                    normalise(1, yn[:], y[:], i - 3)
                if active(i - 2):
                    dve.wait_ge(a_exp.sem, a_exp.at(i - 2))
                    nc.vector.tensor_reduce(ssum[:], prob[:].rearrange("p n t h -> p n (t h)"), AX.X,
                                            ALU.add).then_inc(d_s.sem, 1)
                    dve.wait_ge(d_s.sem, d_s.at(i - 2, 6))
                    dve.wait_ge(d_pv.sem, d_pv.at(i - 3))
                    nc.vector.reciprocal(srec[:], ssum[:]).then_inc(d_s.sem, 1)
                if active(i):
                    dve.wait_ge(a_latT.sem, a_latT.at(i))
                    low_part(latT, b3[:, 0:2 * P], d_latT)
                if active(i - 3):
                    dve.wait_ge(g_x1.sem, g_x1.at(i - 3))
                    stats(2, x1[:], i - 3)
                if active(i - 4):
                    dve.wait_ge(pe_pos.sem, pe_pos.at(i - 4))
                    nc.vector.scalar_tensor_tensor(fits[:], b6[:, 0:E], float(CAP), chosen[:], ALU.is_lt,
                                                   ALU.mult).then_inc(d_pos.sem, 1)
                    nc.vector.tensor_tensor(key[:], c[:, C_EB:C_EB + E], b6[:, 0:E], ALU.subtract).then_inc(d_pos.sem, 1)
                    dve.wait_ge(d_pos.sem, d_pos.at(i - 4, 2))
                    nc.vector.tensor_tensor(key2[:], key[:], fits[:], ALU.mult).then_inc(d_pos.sem, 1)
                    nc.vector.tensor_tensor(before[:], before[:], chosen[:], ALU.add).then_inc(d_pos.sem, 1)
                    dve.wait_ge(d_pos.sem, d_pos.at(i - 4, 3))
                    settle(dve)
                    nc.vector.max(key8[:], key2[:]).then_inc(d_pos.sem, 1)
                    dve.wait_ge(d_pos.sem, d_pos.at(i - 4, 5))
                    nc.vector.scalar_tensor_tensor(none8[:], key8[:], 0.0, c[:, C_TRASH:C_TRASH + 8], ALU.is_equal,
                                                   ALU.mult).then_inc(d_pos.sem, 1)
                    dve.wait_ge(slots_out.sem, slots_out.at(i - 5))
                    nc.vector.tensor_copy(toki[:], tok[:]).then_inc(d_pos.sem, 1)
                    dve.wait_ge(d_pos.sem, d_pos.at(i - 4, 7))
                    nc.vector.tensor_scalar(tok[:], tok[:], float(P), None, ALU.add).then_inc(d_pos.sem, 1)
                    nc.vector.scalar_tensor_tensor(slot[:], none8[:], KEY0, key8[:], ALU.add,
                                                   ALU.subtract).then_inc(d_pos.sem, 1)
                if active(i - 3):
                    dve.wait_ge(xf_out[1 - par].sem, xf_out[1 - par].at(i - 5))
                    normalise(2, xf[:, 1 - par, 0:D], x1[:], i - 3)
                if active(i - 2):
                    dve.wait_ge(pe_pv.sem, pe_pv.at(i - 2))
                    dve.wait_ge(o_out.sem, o_out.at(i - 3))
                    dve.wait_ge(d_s.sem, d_s.at(i - 2))
                    nc.vector.tensor_tensor(o[:].rearrange("p (n d) -> p n d", d=DH),
                                            b5[:].rearrange("p (n d) -> p n d", d=DH),
                                            srec[:].unsqueeze(2).broadcast_to([P, NBLK, DH]), ALU.mult).then_inc(d_pv.sem, 1)
                if active(i - 3):
                    dve.wait_ge(a_xfT.sem, a_xfT.at(i - 3))
                    low_part(xfT, b2[:], d_xfT)

            pipeline(dve, iteration)

        @block.gpsimd
        def _(pool):
            pool.wait_ge(zeroed, 3)
            pool.wait_ge(scratch_init, 48)

            def root(n, t):
                pool.wait_ge(d_ln[n].sem, d_ln[n].at(t, 2))
                settle(pool)
                nc.gpsimd.tensor_scalar(ve[n][:], mv[n][:, 1:2], EPS, None, ALU.add).then_inc(g_rstd[n].sem, 1)
                pool.wait_ge(g_rstd[n].sem, g_rstd[n].at(t, 1))
                nc.gpsimd.tensor_tensor(rstd[n][:], ve[n][:], mhalf[:], ALU.pow).then_inc(g_rstd[n].sem, 1)

            def iteration(i, par, peeled):
                if active(i + 1):
                    root(0, i + 1)
                if active(i - 3):
                    root(1, i - 3)
                    pool.wait_ge(d_ln[1].sem, d_ln[1].at(i - 3))
                    pool.wait_ge(xres_in.sem, xres_in.at(i - 3))
                    pool.wait_ge(x1_out.sem, x1_out.at(i - 4))
                    pool.wait_ge(d_ln[2].sem, d_ln[2].at(i - 4))
                    nc.gpsimd.tensor_tensor(x1[:], yn[:], xres[:], ALU.add).then_inc(g_x1.sem, 1)
                    root(2, i - 3)
                if active(i - 4):
                    pool.wait_ge(d_pos.sem, d_pos.at(i - 4))
                    settle(pool)
                    for n in range(TOPK):
                        nc.gpsimd.indirect_dma_start(slot_d, bass.IndirectOffsetOnAxis(slot[:, n:n + 1].bitcast(U32), 0),
                                                     toki[:], None).then_inc(slots_out.sem, 16)

            pipeline(pool, iteration)

            pool.wait_ge(slots_out.sem, slots_out.at(NT - 1))


def experts(nc, cst, w_eg, w_ed, xf_d, acc_d, slot_d):
    w1_d = w_eg.rearrange("e (p c) n -> (e p) (c n)", c=KD)
    w2_d = w_ed.rearrange("e (p c) n -> (e p) (c n)", c=2)
    PI = I // 2
    with ExitStack() as ctx:
        def sb(name, shape, dt=F32):
            return ctx.enter_context(nc.sbuf_tensor(name, shape, dt))

        def count(name, per=1, n=1, place=0):
            return Count(ctx.enter_context(nc.semaphore(name)), per, E, n, place)

        rowsT_ps, hidT_ps, out_ps, idx_ps = (ctx.enter_context(nc.psum_tensor(f"e_ps{n}", [P, 512], F32))[:]
                                             for n in range(4))
        gu_ps = [ctx.enter_context(nc.psum_tensor(f"e_gu{n}", [P, 2 * I], F32))[:] for n in range(2)]
        NW = 4
        w1 = sb("w1", [P, NW, KD, 2 * I])
        w2 = sb("w2", [PI, NW, 2, D])
        ident = sb("e_ident", [P, P])
        table = sb("table", [E, CAP], I32)
        tablef = sb("tablef", [E, CAP])
        idx = sb("idx", [CAP, E], I32)
        gidx = sb("gidx", [CAP, 2, 1], I32)
        sidx = sb("sidx", [CAP, 2, 1], I32)
        xg = sb("xg", [P, 2, D + E])
        xgT = sb("xgT", [P, 2, KD, P])
        gate = sb("gate", [P, 2])
        tanh = sb("tanh", [P, 2, I])
        hid = sb("hid", [P, 2, I])
        hidT = sb("hidT", [PI, 2, P])
        eo = sb("eo", [P, 2, D])

        start = ctx.enter_context(nc.semaphore("start"))
        setup = ctx.enter_context(nc.semaphore("setup"))
        w1_in = [count(f"w1_in{n}", 32, NW, n) for n in range(NW)]
        x_got = [count(f"x_got{n}", 16, 2, n) for n in range(2)]
        added = count("added", 16)
        e_xT = count("e_xT")
        e_gu = count("e_gu")
        e_hT = count("e_hT")
        e_out = count("e_out")
        ea_xT = count("ea_xT")
        ea_tanh = count("ea_tanh")
        ea_hT = count("ea_hT")
        ea_out = count("ea_out")
        ed_gidx = count("ed_gidx")
        ed_sidx = count("ed_sidx")
        ed_gate = count("ed_gate")
        ed_h = count("ed_h", 2)

        block = ctx.enter_context(nc.Block())
        FIRST, LOOP, LAST = -3, 2, E + 1
        ROUNDS = (E - 2 - LOOP) // NW
        REST = LOOP + ROUNDS * NW
        assert REST + 2 <= E

        def active(e):
            return not isinstance(e, int) or 0 <= e < E

        def pipeline(eng, iteration):
            for j in range(FIRST, LOOP):
                iteration(j, j % NW)
            with eng.Fori(0, ROUNDS) as r:
                for u in range(NW):
                    iteration(r * NW + (LOOP + u), (LOOP + u) % NW)
            for j in range(REST, LAST):
                iteration(j, j % NW)

        @block.sync
        def _(sp):
            sp.dma_start(table[:], slot_d[0:E * CAP, :].rearrange("(e s) o -> e (s o)", s=CAP)).then_inc(start, 16)
            sp.dma_start(ident[:], cst[:, C_ID:C_ID + P]).then_inc(start, 16)

            def load(e, place):
                sp.wait_ge(e_out.sem, e_out.at(e - NW))
                sp.nop(nofuse=True)
                a, b = ((w1_d[e * P:(e + 1) * P, :], w2_d[e * PI:(e + 1) * PI, :]) if isinstance(e, int) else
                        (w1_d[bass.ts(e, P), :], w2_d[bass.ts(e, PI), :]))
                sp.dma_start(w1[:, place].rearrange("p c n -> p (c n)"), a).then_inc(w1_in[place].sem, 16)
                sp.dma_start(w2[:, place].rearrange("p c n -> p (c n)"), b).then_inc(w1_in[place].sem, 16)

            for e in range(NW):
                load(e, e)
            with sp.Fori(1, E // NW) as r:
                for u in range(NW):
                    load(r * NW + u, u)

        @block.tensor
        def _(pe):
            pe.wait_ge(start, 32)
            pe.wait_ge(setup, 1)
            nc.tensor.transpose(idx_ps[:, 0:E], tablef[:], ident[0:E, 0:E]).then_inc(setup, 1)

            def iteration(j, place):
                par = place % 2
                if active(j):
                    pe.wait_ge(ea_xT.sem, ea_xT.at(j))
                    pe.wait_ge(w1_in[place].sem, w1_in[place].at(j))
                    pe.wait_ge(ed_h.sem, ed_h.at(j - 2))
                    for n in range(KD):
                        last = nc.tensor.matmul(gu_ps[par], xgT[:, par, n, :], w1[:, place, n, :],
                                                start=(n == 0), stop=(n == KD - 1))
                    last.then_inc(e_gu.sem, 1)
                if active(j - 1):
                    pe.wait_ge(ed_h.sem, ed_h.at(j - 1))
                    pe.wait_ge(ea_hT.sem, ea_hT.at(j - 2))
                    for n in range(2):
                        last = nc.tensor.transpose(hidT_ps[0:PI, n * P:(n + 1) * P],
                                                   hid[:, 1 - par, :].rearrange("p (i c) -> p c i", c=2)[:, n, :],
                                                   ident[:])
                    last.then_inc(e_hT.sem, 1)
                if active(j + 1):
                    pe.wait_ge(x_got[1 - par].sem, x_got[1 - par].at(j + 1))
                    pe.wait_ge(ea_xT.sem, ea_xT.at(j))
                    for n in range(KD):
                        last = nc.tensor.transpose(rowsT_ps[:, n * P:(n + 1) * P],
                                                   xg[:, 1 - par, 0:D].rearrange("p (i c) -> p c i", c=KD)[:, n, :],
                                                   ident[:])
                    last.then_inc(e_xT.sem, 1)
                if active(j - 1):
                    pe.wait_ge(ea_hT.sem, ea_hT.at(j - 1))
                    pe.wait_ge(ea_out.sem, ea_out.at(j - 2))
                    for n in range(2):
                        last = nc.tensor.matmul(out_ps, hidT[:, n, :], w2[:, (place - 1) % NW, n, :],
                                                start=(n == 0), stop=(n == 1))
                    last.then_inc(e_out.sem, 1)

            pipeline(pe, iteration)

        @block.scalar
        def _(act):
            def iteration(j, place):
                par = place % 2
                if active(j - 1):
                    act.wait_ge(e_hT.sem, e_hT.at(j - 1))
                    act.wait_ge(e_out.sem, e_out.at(j - 2))
                    nc.scalar.copy(hidT[:].rearrange("p c s -> p (c s)"), hidT_ps[0:PI, 0:2 * P]).then_inc(ea_hT.sem, 1)
                if active(j + 1):
                    act.wait_ge(e_xT.sem, e_xT.at(j + 1))
                    act.wait_ge(e_gu.sem, e_gu.at(j - 1))
                    nc.scalar.copy(xgT[:, 1 - par].rearrange("p k s -> p (k s)"), rowsT_ps).then_inc(ea_xT.sem, 1)
                if active(j - 1):
                    act.wait_ge(e_out.sem, e_out.at(j - 1))
                    act.wait_ge(added.sem, added.at(j - 3))
                    nc.scalar.copy(eo[:, 1 - par, :], out_ps).then_inc(ea_out.sem, 1)
                if active(j):
                    act.wait_ge(e_gu.sem, e_gu.at(j))
                    act.wait_ge(ed_h.sem, ed_h.at(j - 2))
                    nc.scalar.activation(tanh[:, par, :], gu_ps[par][:, 0:I], ACT.Tanh, scale=0.5).then_inc(ea_tanh.sem, 1)

            pipeline(act, iteration)

        @block.vector
        def _(dve):
            dve.wait_ge(start, 32)
            nc.vector.tensor_copy(tablef[:], table[:]).then_inc(setup, 1)
            dve.wait_ge(setup, 2)
            nc.vector.tensor_copy(idx[:], idx_ps[:, 0:E]).then_inc(setup, 1)
            dve.wait_ge(setup, 3)

            def column(ap, e):
                return ap[:, e:e + 1] if isinstance(e, int) else ap[:, bass.ds(e, 1)]

            def iteration(j, place):
                par = place % 2
                if active(j + 2):
                    dve.wait_ge(x_got[par].sem, x_got[par].at(j))
                    dve.nop(nofuse=True)
                    nc.vector.tensor_copy(gidx[:, par, :], column(idx[:], j + 2)).then_inc(ed_gidx.sem, 1)
                if active(j - 1):
                    dve.wait_ge(added.sem, added.at(j - 3))
                    dve.nop(nofuse=True)
                    nc.vector.tensor_copy(sidx[:, 1 - par, :], column(idx[:], j - 1)).then_inc(ed_sidx.sem, 1)
                if active(j):
                    dve.wait_ge(x_got[par].sem, x_got[par].at(j))
                    dve.wait_ge(ed_h.sem, ed_h.at(j - 1))
                    nc.vector.tensor_scalar(gate[:, par:par + 1], column(xg[:, par, D:D + E], j), 0.5, None,
                                            ALU.mult).then_inc(ed_gate.sem, 1)
                    dve.wait_ge(ea_tanh.sem, ea_tanh.at(j))
                    nc.vector.scalar_tensor_tensor(tanh[:, par, :], tanh[:, par, :], 1.0, gu_ps[par][:, 0:I],
                                                   ALU.add, ALU.mult).then_inc(ed_h.sem, 1)
                    dve.wait_ge(ed_h.sem, ed_h.at(j, 1))
                    dve.wait_ge(ed_gate.sem, ed_gate.at(j))
                    dve.wait_ge(e_hT.sem, e_hT.at(j - 2))
                    nc.vector.scalar_tensor_tensor(hid[:, par, :], tanh[:, par, :], gate[:, par:par + 1],
                                                   gu_ps[par][:, I:], ALU.mult, ALU.mult).then_inc(ed_h.sem, 1)

            pipeline(dve, iteration)

        @block.gpsimd
        def _(pool):
            def iteration(j, place):
                par = place % 2
                if active(j + 2):
                    pool.wait_ge(ed_gidx.sem, ed_gidx.at(j + 2))
                    pool.wait_ge(e_xT.sem, e_xT.at(j))
                    pool.wait_ge(ed_gate.sem, ed_gate.at(j))
                    pool.nop(nofuse=True)
                    nc.gpsimd.indirect_dma_start(xg[:, par, :], None, xf_d, bass.IndirectOffsetOnAxis(
                        gidx[:, par, :].bitcast(U32), 0)).then_inc(x_got[par].sem, 16)
                if active(j - 1):
                    pool.wait_ge(ea_out.sem, ea_out.at(j - 1))
                    pool.wait_ge(ed_sidx.sem, ed_sidx.at(j - 1))
                    pool.wait_ge(added.sem, added.at(j - 2))
                    pool.nop(nofuse=True)
                    nc.gpsimd.indirect_dma_start(acc_d, bass.IndirectOffsetOnAxis(
                        sidx[:, 1 - par, :].bitcast(U32), 0), eo[:, 1 - par, :], None,
                        compute_op=ALU.add).then_inc(added.sem, 16)

            pipeline(pool, iteration)
            pool.wait_ge(added.sem, added.at(E - 1))


def last_norm(nc, x1_d, acc_d, out):
    G, NB = 2, 4
    NG = NT // G
    with ExitStack() as ctx:
        def sb(name, shape, dt=F32):
            return ctx.enter_context(nc.sbuf_tensor(name, shape, dt))

        def count(name, per=1, n=1, place=0):
            return Count(ctx.enter_context(nc.semaphore(name)), per, NG, n, place)

        acc = sb("f_acc", [P, NB, G, D])
        res = sb("f_res", [P, NB, G, D])
        st = sb("f_st", [P, NB, G, 6])
        mv = sb("f_mv", [P, NB, G, 2])
        ve = sb("f_ve", [P, NB, G])
        rstd = sb("f_rstd", [P, NB, G])
        mhalf = sb("f_mhalf", [P, G])
        ready = ctx.enter_context(nc.semaphore("f_ready"))
        acc_in = [count(f"f_acc_in{n}", 16, NB, n) for n in range(NB)]
        res_in = [count(f"f_res_in{n}", 16, NB, n) for n in range(NB)]
        f_out = [count(f"f_out{n}", 16, NB, n) for n in range(NB)]
        stats = count("f_stats", 2 * G)
        roots = count("f_roots", 2)
        normed = count("f_normed", G)
        summed = count("f_summed", 1)

        def group(ap):
            return ap.rearrange("(g p r) d -> (g p) (r d)", p=P, r=G)

        def rows(ap, t):
            return ap[t * P:(t + 1) * P, :] if isinstance(t, int) else ap[bass.ts(t, P), :]

        def ring(eng, body, first=0):
            for u in range(NB):
                body(u, u)
            with eng.Fori(1, NG // NB) as r:
                for u in range(NB):
                    body(r * NB + u, u)

        block = ctx.enter_context(nc.Block())

        @block.sync
        def _(sp):
            def load(t, u):
                sp.wait_ge(f_out[u].sem, f_out[u].at(t - NB))
                sp.nop(nofuse=True)
                sp.dma_start(acc[:, u].rearrange("p r d -> p (r d)"), rows(group(acc_d[0:T, :]), t)).then_inc(acc_in[u].sem, 16)
                sp.dma_start(res[:, u].rearrange("p r d -> p (r d)"), rows(group(x1_d), t)).then_inc(res_in[u].sem, 16)

            ring(sp, load)

        @block.scalar
        def _(act):
            def store(t, u):
                act.wait_ge(summed.sem, summed.at(t))
                act.nop(nofuse=True)
                act.dma_start(rows(group(out), t), res[:, u].rearrange("p r d -> p (r d)")).then_inc(f_out[u].sem, 16)

            ring(act, store)
            for u in range(NB):
                act.wait_ge(f_out[u].sem, 16 * (NG // NB))

        @block.vector
        def _(dve):
            nc.vector.memset(mhalf[:], -0.5).then_inc(ready, 1)

            def statistics(t, u):
                dve.wait_ge(acc_in[u].sem, acc_in[u].at(t))
                dve.wait_ge(roots.sem, roots.at(t - NB))
                for g in range(G):
                    nc.vector.bn_stats(st[:, u, g, :], acc[:, u, g, :]).then_inc(stats.sem, 1)
                dve.wait_ge(stats.sem, stats.at(t, G))
                dve.nop(nofuse=True)
                for g in range(G):
                    nc.vector.bn_aggr(mv[:, u, g, :], st[:, u, g, :]).then_inc(stats.sem, 1)

            def normalise(t, u):
                dve.wait_ge(roots.sem, roots.at(t))
                for g in range(G):
                    nc.vector.tensor_scalar(acc[:, u, g, :], acc[:, u, g, :], mv[:, u, g, 0:1], rstd[:, u, g:g + 1],
                                            ALU.subtract, ALU.mult).then_inc(normed.sem, 1)

            def body(t, u):
                statistics(t, u)
                if not isinstance(t, int) or t > 0:
                    normalise(t - 1, (u - 1) % NB)

            ring(dve, body)
            normalise(NG - 1, NB - 1)

        @block.gpsimd
        def _(pool):
            pool.wait_ge(ready, 1)

            def add(t, u):
                pool.wait_ge(normed.sem, normed.at(t))
                pool.wait_ge(res_in[u].sem, res_in[u].at(t))
                nc.gpsimd.tensor_tensor(res[:, u], acc[:, u], res[:, u], ALU.add).then_inc(summed.sem, 1)

            def body(t, u):
                pool.wait_ge(stats.sem, stats.at(t))
                pool.wait_ge(normed.sem, normed.at(t - NB))
                pool.nop(nofuse=True)
                nc.gpsimd.tensor_scalar(ve[:, u], mv[:, u, :, 1], EPS, None, ALU.add).then_inc(roots.sem, 1)
                pool.wait_ge(roots.sem, roots.at(t, 1))
                nc.gpsimd.tensor_tensor(rstd[:, u], ve[:, u], mhalf[:], ALU.pow).then_inc(roots.sem, 1)
                if not isinstance(t, int) or t > 0:
                    add(t - 1, (u - 1) % NB)

            ring(pool, body)
            add(NG - 1, NB - 1)


def kernel(**inputs):
    from concourse import bacc
    from concourse.bass_utils import run_bass_kernel_spmd

    a = {n: np.asarray(v) for n, v in inputs.items()}
    at, ff = (lambda n: a["L0_attn_" + n]), (lambda n: a["L0_ffn_" + n])
    cst, slot_init = constants()
    w_q = np.concatenate([at("Wcq").reshape(DC, H, DH), at("Wqr").reshape(DC, H, DR)], 2).reshape(DC, H * DQ)
    b_q = np.concatenate([at("bcq").reshape(H, DH), at("bqr").reshape(H, DR)], 1).reshape(H * DQ)
    g, u, r = ff("shared_gate_w").T, ff("shared_up_w").T, ff("gate_w").T
    w_gu = np.concatenate([g[:, 0:I], u[:, 0:I], r[:, 0:E // 2], g[:, I:], u[:, I:], r[:, E // 2:]], 1)
    arrays = {
        "x": at("h_t").reshape(T, D), "cst": cst, "slot_init": slot_init,
        "w_lat": np.concatenate([at("Wc"), at("Wckv"), at("Wkr")], 1),
        "b_lat": np.concatenate([at("bc"), at("bckv"), at("bkr")]),
        "w_q": w_q, "b_q": b_q, "w_ck": at("Wck"), "b_ck": at("bck"), "w_v": at("Wv"), "b_v": at("bv"),
        "w_o": at("Wo"), "b_o": at("bo"), "w_gu": w_gu, "w_sd": ff("shared_down_w").T,
        "w_eg": ff("gate_up_proj"), "w_ed": ff("down_proj"),
    }
    arrays = {n: np.ascontiguousarray(v) for n, v in arrays.items()}
    nc = bacc.Bacc("TRN2", target_bir_lowering=False, num_devices=1)
    args = [nc.dram_tensor(n, v.shape, mybir.dt.from_np(v.dtype), kind="ExternalInput").ap() for n, v in arrays.items()]
    out = nc.dram_tensor("out", (T, D), F32, kind="ExternalOutput").ap()
    layer_kernel(nc, *args, out)
    r = run_bass_kernel_spmd(nc, [arrays], core_ids=[0])
    return r.results[0]["out"].reshape(4, 2048, D)
```

```python
from contextlib import ExitStack

import numpy as np

import concourse.bass as bass
from concourse import mybir

F32 = mybir.dt.float32
F32R = mybir.dt.float32r
BF16 = mybir.dt.bfloat16
I32 = mybir.dt.int32
U32 = mybir.dt.uint32
ALU = mybir.AluOpType
ACT = mybir.ActivationFunctionType
AX = mybir.AxisListType

P = 128
T = 4 * 2048
NT = T // P
D = 512
KD = D // P
H = 16
DH = 32
DR = 16
DQ = DH + DR
HS = 64
DC = 128
SCALE = 1.0 / float(np.sqrt(DQ))
E = 64
TOPK = 6
CAP = 128
I = 192
SI = 384
EPS = 1e-5
B4 = 4
NBLK = P // (2 * B4)
BIG = 1.0e30
KEY0 = 16384.0
GU = SI + E // 2

C_ID, C_TRI, C_EB, C_NEG, C_TRASH, C_TOK, C_END = np.cumsum([0, P, P, E, B4, 8, 1]).tolist()


def constants():
    c = np.zeros((P, C_END), np.float32)
    p = np.arange(P)
    c[:, C_ID:C_ID + P] = np.eye(P)
    c[:, C_TRI:C_TRI + P] = p[:, None] < p[None, :]
    c[:, C_EB:C_EB + E] = KEY0 - CAP * np.arange(E)
    c[:, C_NEG:C_NEG + B4] = np.where((p[:, None] // H) % B4 == np.arange(B4), 0.0, -BIG)
    c[:, C_TRASH:C_TRASH + 8] = p[:, None] + P * np.arange(8) + E * CAP - KEY0
    c[:, C_TOK] = p
    slots = np.tile(T + np.arange(CAP, dtype=np.int32), E + TOPK).reshape((E + TOPK) * CAP, 1)
    return c, slots


class Count:

    def __init__(self, sem, per, total, n=1, place=0):
        self.sem, self.per, self.total, self.n, self.place = sem, per, total, n, place

    def at(self, t, k=None):
        k = self.per if k is None else k
        if not isinstance(t, int):
            return t * (self.per // self.n) + (k - self.place * self.per // self.n)
        m = (t - self.place) // self.n
        return min(max(m * self.per + k, 0) if m >= 0 else 0, self.total // self.n * self.per)


def layer_kernel(nc, x, cst, slot_init, w_lat, b_lat, w_q, b_q, w_ck, b_ck, w_v, b_v, w_o, b_o,
                 w_gu, w_sd, w_eg, w_ed, out):
    x1_d = nc.dram_tensor("x1_scratch", (T, D), F32).ap()
    xf_d = nc.dram_tensor("xf_scratch", (T + CAP, D + E), F32).ap()
    acc_d = nc.dram_tensor("acc_scratch", (T + CAP, D), F32).ap()
    v_d = nc.dram_tensor("v_scratch", (2, P, D), F32).ap()
    o_d = nc.dram_tensor("o_scratch", (2, P, D), F32).ap()
    slot_d = nc.dram_tensor("slot_scratch", ((E + TOPK) * CAP, 1), I32).ap()

    token_pipeline(nc, x, cst, slot_init, w_lat, b_lat, w_q, b_q, w_ck, b_ck, w_v, b_v, w_o, b_o, w_gu, w_sd,
                   x1_d, xf_d, acc_d, v_d, o_d, slot_d)
    experts(nc, cst, w_eg, w_ed, xf_d, acc_d, slot_d)
    last_norm(nc, x1_d, acc_d, out)


def token_pipeline(nc, x, cst, slot_init, w_lat, b_lat, w_q, b_q, w_ck, b_ck, w_v, b_v, w_o, b_o, w_gu, w_sd,
                   x1_d, xf_d, acc_d, v_d, o_d, slot_d):
    ctx = ExitStack()
    with ctx:
        def sb(name, shape, dt=F32):
            return ctx.enter_context(nc.sbuf_tensor(name, shape, dt))

        def sem(name):
            return ctx.enter_context(nc.semaphore(name))

        def count(name, per=1, n=1, place=0):
            return Count(sem(name), per, NT, n, place)

        bank = [ctx.enter_context(nc.psum_tensor(f"bank{n}", [P, 512], F32)) for n in range(2, 8)]
        score_ps = ctx.enter_context(nc.psum_tensor("score_ps", [P, 1024], F32))
        b2, b3, b4, b5, b6, b7 = (b[:] for b in bank)
        s0, s1 = score_ps[:, 0:512], score_ps[:, 512:1024]
        pos_ps = s1[:, 0:E]

        c = sb("c", [P, C_END])
        ident = c[:, C_ID:C_ID + P]
        tri = sb("tri", [P, P], BF16)
        ones = sb("ones", [P, P], BF16)
        mhalf = sb("mhalf", [P, 1])
        wlat = sb("wlat", [P, 2, KD, 512], F32R)
        wq = sb("wq", [P, 2, 1, H * DQ], F32R)
        wck = sb("wck", [P, 2, 1, D], F32R)
        wv = sb("wv", [P, 2, 1, D], F32R)
        wo = sb("wo", [P, 2, KD, D], F32R)
        wgu = sb("wgu", [P, 2, KD, 2 * GU], F32R)
        wsd = sb("wsd", [P, 2, SI // P, D], F32R)
        blat = sb("blat", [P, 512])
        bq = sb("bq", [P, H * DQ])
        bck = sb("bck", [P, D])
        bv = sb("bv", [P, D])
        bo = sb("bo", [P, D])
        xin = sb("xin", [P, 2, D])
        xn = sb("xn", [P, D])
        xT = sb("xT", [P, 2, KD, P], F32R)
        lat = sb("lat", [P, 2 * DC])
        latT = sb("latT", [P, 2, 2, 2, P], F32R)
        q = sb("q", [P, H, HS])
        k = sb("k", [P, 2, H, HS])
        v = sb("v", [P, D])
        vbd = sb("vbd", [P, 2, NBLK, 2, DH])
        qT_all = sb("qT", [P, P, H])
        kT_all = sb("kT", [P, P, H])
        qT, kT = qT_all[0:DQ], kT_all[0:DQ]
        prob = sb("prob", [P, NBLK, B4, H])
        probT = sb("probT", [P, 8, P])
        o = sb("o", [P, D])
        oin = sb("oin", [P, D])
        oT = sb("oT", [P, 2, KD, P], F32R)
        y = sb("y", [P, D])
        yn = sb("yn", [P, D])
        xres = sb("xres", [P, D])
        x1 = sb("x1", [P, D])
        xf = sb("xf", [P, 2, D + E])
        xfT = sb("xfT", [P, 2, KD, P], F32R)
        th = sb("th", [P, 2, I])
        h = sb("h", [P, SI])
        hT = sb("hT", [P, 2, SI // P, P], F32R)
        sh = sb("sh", [P, D])
        zero = sb("zero", [P, D + E])
        st = [sb(f"st{n}", [P, 6]) for n in range(3)]
        mv = [sb(f"mv{n}", [P, 2]) for n in range(3)]
        ve = [sb(f"ve{n}", [P, 1]) for n in range(3)]
        rstd = [sb(f"rstd{n}", [P, 1]) for n in range(3)]
        smax4 = sb("smax4", [P, NBLK, B4])
        smask4 = sb("smask4", [P, NBLK, B4])
        smax = sb("smax", [P, NBLK])
        sref = sb("sref", [P, NBLK, B4])
        ssum = sb("ssum", [P, NBLK])
        srec = sb("srec", [P, NBLK])
        lg = sb("lg", [P, E + 2])
        top = sb("top", [P, 8])
        rep = sb("rep", [P, 8])
        lgr = sb("lgr", [P, E + 2])
        ntop = sb("ntop", [P, 1])
        ex = sb("ex", [P, E])
        esum = sb("esum", [P, 1])
        erec = sb("erec", [P, 1])
        chosen = sb("chosen", [P, E], BF16)
        before = sb("before", [P, E], BF16)
        fits = sb("fits", [P, E])
        key = sb("key", [P, E])
        key2 = sb("key2", [P, E])
        key8 = sb("key8", [P, 8])
        none8 = sb("none8", [P, 8])
        slot = sb("slot", [P, 8], I32)
        tok = sb("tok", [P, 1])
        toki = sb("toki", [P, 1], I32)

        flat = lambda ap: ap.rearrange("p a b -> p (a b)")
        qs, ks, vs = flat(qT_all[:]), flat(kT_all[:]), vbd[:].rearrange("p a n b d -> p (a n b d)")
        ps, pts = prob[:].rearrange("p n t h -> p (n t h)"), flat(probT[:])
        parts = [(qs[:, 512 * n:512 * n + 512], wlat, n, w_lat[n * P:(n + 1) * P, :]) for n in range(KD)]
        parts += [(ks[:, 0:H * DQ], wq, 0, w_q), (ks[:, 768:1280], wck, 0, w_ck), (ks[:, 1280:1792], wv, 0, w_v)]
        parts += [(vs[:, D * n:D * n + D], wo, n, w_o[n * P:(n + 1) * P, :]) for n in range(KD)]
        parts += [(st_, wgu, n, w_gu[n * P:(n + 1) * P, :])
                  for n, st_ in enumerate((ps[:, 0:2 * GU], pts[:, 0:2 * GU], qs[:, 0:2 * GU], qs[:, 1024:1024 + 2 * GU]))]
        parts += [(ks[:, D * n:D * n + D], wsd, n, w_sd[n * P:(n + 1) * P, :]) for n in range(SI // P)]
        WAIT_FOR = {13: 4, 14: 4, 15: 7, 16: 7, 17: 7}

        consts_in = sem("consts_in")
        part_in = [sem(f"part_in{n}") for n in range(len(parts))]
        biases_in = sem("biases_in")
        part_hi = sem("part_hi")
        part_lo = sem("part_lo")
        scratch_init = sem("scratch_init")
        zeroed = sem("zeroed")
        cast_done = sem("cast_done")
        x_in = [count(f"x_in{n}", 16, 2, n) for n in range(2)]
        xres_in = count("xres_in", 16)
        v_out = count("v_out", 16)
        v_in = [count(f"v_in{n}", 32, 2, n) for n in range(2)]
        o_out = count("o_out", 64)
        o_in = count("o_in", 16)
        x1_out = count("x1_out", 16)
        acc_out = count("acc_out", 16)
        xf_out = [count(f"xf_out{n}", 16, 2, n) for n in range(2)]
        slots_out = count("slots_out", 16 * TOPK)
        pe_xT = count("pe_xT")
        pe_lat = count("pe_lat")
        pe_latT = count("pe_latT")
        pe_q = count("pe_q", 2)
        pe_k = count("pe_k")
        pe_v = count("pe_v")
        pe_qT = count("pe_qT", 2)
        pe_kT = count("pe_kT", 2)
        pe_s = count("pe_s")
        pe_pT = count("pe_pT", 2)
        pe_pv = count("pe_pv")
        pe_oT = count("pe_oT")
        pe_wo = count("pe_wo")
        pe_xfT = count("pe_xfT")
        pe_gu = count("pe_gu", 2)
        pe_hT = count("pe_hT")
        pe_sh = count("pe_sh")
        pe_pos = count("pe_pos")
        a_xT = count("a_xT")
        a_latT = count("a_latT")
        a_qT = count("a_qT", 4)
        a_kT = count("a_kT", 4)
        a_exp = count("a_exp")
        a_pT = count("a_pT", 2)
        a_oT = count("a_oT")
        a_xfT = count("a_xfT")
        a_th = count("a_th", 2)
        a_hT = count("a_hT")
        a_sh = count("a_sh")
        a_gate = count("a_gate")
        d_ln = [count(f"d_ln{n}", 3) for n in range(3)]
        d_xT = count("d_xT")
        d_latT = count("d_latT")
        d_oT = count("d_oT")
        d_xfT = count("d_xfT")
        d_hT = count("d_hT")
        d_y = count("d_y")
        d_lat = count("d_lat", 2)
        d_q = count("d_q", 2)
        d_k = count("d_k")
        d_v = count("d_v")
        d_s = count("d_s", 7)
        d_pv = count("d_pv")
        d_h = count("d_h", 4)
        d_r = count("d_r", 9)
        d_pos = count("d_pos", 9)
        g_rstd = [count(f"g_rstd{n}", 2) for n in range(3)]
        g_x1 = count("g_x1")

        block = ctx.enter_context(nc.Block())

        FIRST, LOOP, LAST = -2, 6, NT + 5
        REST = NT - 2
        PAIRS = (REST - LOOP) // 2
        assert LOOP + 2 * PAIRS == REST

        def active(t):
            return not isinstance(t, int) or 0 <= t < NT

        def pipeline(eng, iteration):
            for i in range(FIRST, LOOP):
                iteration(i, i % 2)
            with eng.Fori(0, PAIRS) as r:
                for u in range(2):
                    iteration(r * 2 + (LOOP + u), (LOOP + u) % 2)
            for i in range(REST, LAST):
                iteration(i, i % 2)

        def settle(eng):
            eng.nop(nofuse=True)

        def rows(ap, t):
            return ap[t * P:(t + 1) * P, :] if isinstance(t, int) else ap[bass.ts(t, P), :]

        @block.sync
        def _(sp):
            sp.dma_start(c[:], cst).then_inc(consts_in, 16)
            for n, (stage, _, _, src) in enumerate(parts):
                if n in WAIT_FOR:
                    sp.wait_ge(part_lo, WAIT_FOR[n])
                sp.dma_start(stage, src).then_inc(part_in[n], 16)
            for dst, src in ((blat, b_lat), (bq, b_q), (bck, b_ck), (bv, b_v), (bo, b_o)):
                sp.dma_start(dst[:], src.partition_broadcast(P)).then_inc(biases_in, 16)

            def iteration(i, par):
                if active(i - 3):
                    sp.wait_ge(d_pv.sem, d_pv.at(i - 3))
                    sp.wait_ge(o_in.sem, o_in.at(i - 5))
                    dst = o_d[1 - par].rearrange("(c g b t) (h d) -> g b (t h) c d", c=8, g=2, b=2, h=H)
                    src = o[:].rearrange("p (c b d) -> p b c d", c=8, b=2)
                    for g in range(2):
                        for b in range(2):
                            sp.dma_start(dst[g, b], src[64 * g:64 * g + 64, b]).then_inc(o_out.sem, 16)
                    sp.wait_ge(o_out.sem, o_out.at(i - 3))
                    sp.wait_ge(pe_oT.sem, pe_oT.at(i - 4))
                    sp.dma_start(oin[:], o_d[1 - par]).then_inc(o_in.sem, 16)
                if active(i + 2):
                    sp.wait_ge(d_ln[0].sem, d_ln[0].at(i))
                    settle(sp)
                    sp.dma_start(xin[:, par, :], rows(x, i + 2)).then_inc(x_in[par].sem, 16)
                if isinstance(i, int) and i == FIRST:
                    sp.dma_start(slot_d, slot_init).then_inc(scratch_init, 16)
                    sp.wait_ge(zeroed, 3)
                    sp.dma_start(xf_d[T:T + CAP, :], zero[:]).then_inc(scratch_init, 16)
                    sp.dma_start(acc_d[T:T + CAP, :], zero[:, 0:D]).then_inc(scratch_init, 16)
                if active(i - 4):
                    sp.wait_ge(g_x1.sem, g_x1.at(i - 4))
                    settle(sp)
                    sp.dma_start(rows(x1_d, i - 4), x1[:]).then_inc(x1_out.sem, 16)
                if active(i - 3):
                    sp.wait_ge(g_x1.sem, g_x1.at(i - 4))
                    settle(sp)
                    sp.dma_start(xres[:], rows(x, i - 3)).then_inc(xres_in.sem, 16)
                if active(i - 5):
                    sp.wait_ge(a_sh.sem, a_sh.at(i - 5))
                    settle(sp)
                    sp.dma_start(rows(acc_d, i - 5), sh[:]).then_inc(acc_out.sem, 16)
                if active(i - 1):
                    sp.wait_ge(d_v.sem, d_v.at(i - 1))
                    sp.wait_ge(v_in[1 - par].sem, v_in[1 - par].at(i - 3))
                    sp.dma_start(v_d[1 - par], v[:]).then_inc(v_out.sem, 16)
                    sp.wait_ge(v_out.sem, v_out.at(i - 1))
                    settle(sp)
                    sp.wait_ge(pe_pv.sem, pe_pv.at(i - 3))
                    settle(sp)
                    src = v_d[1 - par].rearrange("(cg b t) (j d) -> b (t j) cg d", cg=NBLK, b=2, j=H)
                    for b in range(2):
                        sp.dma_start(vbd[64 * b:64 * b + 64, 1 - par, :, b, :], src[b]).then_inc(v_in[1 - par].sem, 16)
                if active(i - 4):
                    sp.wait_ge(d_r.sem, d_r.at(i - 4))
                    settle(sp)
                    sp.dma_start(rows(xf_d, i - 4), xf[:, par, :]).then_inc(xf_out[par].sem, 16)

            pipeline(sp, iteration)
            sp.wait_ge(acc_out.sem, acc_out.at(NT - 1))
            sp.wait_ge(x1_out.sem, x1_out.at(NT - 1))
            for n in range(2):
                sp.wait_ge(xf_out[n].sem, xf_out[n].at(NT - 2 + n))

        @block.tensor
        def _(pe):
            pe.wait_ge(consts_in, 16)
            pe.wait_ge(part_lo, len(parts))
            pe.wait_ge(cast_done, 1)

            def transposes(dst, srcs, done):
                for n, s in enumerate(srcs):
                    last = nc.tensor.transpose(dst[0:s.shape[1], n * P:(n + 1) * P], s, ident)
                last.then_inc(done.sem, 1)

            def product(dst, lhs, rhs, low, t, done):
                for n, (a, b) in enumerate(zip(lhs, rhs)):
                    nc.tensor.matmul(dst, a[:, 0], b[:, 0], start=(n == 0), stop=False)
                    nc.tensor.matmul(dst, a[:, 0], b[:, 1], start=False, stop=False)
                pe.wait_ge(low.sem, low.at(t))
                for n, (a, b) in enumerate(zip(lhs, rhs)):
                    last = nc.tensor.matmul(dst, a[:, 1], b[:, 0], start=False, stop=(n == len(lhs) - 1))
                last.then_inc(done.sem, 1)

            def turn(src, done, n, dst):
                transposes(dst, [src[:, 2 * m:2 * m + 2, :].rearrange("p h d -> p (h d)")
                                 for m in range(4 * n, 4 * n + 4)], done)

            def iteration(i, par):
                if isinstance(i, int):
                    for cnt, s in ((d_xT, 0), (d_lat, 1), (d_latT, 1), (d_q, 2), (d_k, 2), (d_v, 2), (a_qT, 3),
                                   (a_kT, 3), (a_pT, 3), (d_pv, 3), (d_oT, 4), (d_y, 4), (d_xfT, 5), (d_h, 5),
                                   (d_hT, 5), (a_sh, 5)):
                        pe.wait_ge(cnt.sem, cnt.at(i - s))
                if active(i - 2):
                    pe.wait_ge(d_q.sem, d_q.at(i - 2))
                    pe.wait_ge(d_latT.sem, d_latT.at(i - 1))
                    turn(q, pe_qT, 0, b3)
                if active(i - 2):
                    pe.wait_ge(d_xT.sem, d_xT.at(i))
                    turn(q, pe_qT, 1, b2)
                if active(i):
                    pe.wait_ge(a_xT.sem, a_xT.at(i))
                    pe.wait_ge(d_pv.sem, d_pv.at(i - 3))
                    product(b5, [xT[:, :, n, :] for n in range(KD)], [wlat[:, :, n, :] for n in range(KD)], d_xT, i, pe_lat)
                if active(i - 2):
                    pe.wait_ge(d_k.sem, d_k.at(i - 2))
                    pe.wait_ge(d_lat.sem, d_lat.at(i - 2))
                    pe.wait_ge(a_qT.sem, a_qT.at(i - 2, 2))
                    turn(k[:, par], pe_kT, 0, b3)
                    pe.wait_ge(a_qT.sem, a_qT.at(i - 2, 4))
                    turn(k[:, par], pe_kT, 1, b2)
                if active(i - 4):
                    pe.wait_ge(d_ln[2].sem, d_ln[2].at(i - 4))
                    pe.wait_ge(a_pT.sem, a_pT.at(i - 3, 1))
                    transposes(s0, [xf[:, par, n * P:(n + 1) * P] for n in range(KD)], pe_xfT)
                if active(i - 1):
                    pe.wait_ge(a_latT.sem, a_latT.at(i - 1))
                    pe.wait_ge(d_k.sem, d_k.at(i - 2))
                    product(b6, [latT[:, 1 - par, :, 1, :]], [wv[:, :, 0, :]], d_latT, i - 1, pe_v)
                if active(i - 4):
                    pe.wait_ge(a_xfT.sem, a_xfT.at(i - 4))
                    pe.wait_ge(a_sh.sem, a_sh.at(i - 5))
                    product(b7[:, 0:GU], [xfT[:, :, n, :] for n in range(KD)], [wgu[:, :, n, 0:GU] for n in range(KD)],
                            d_xfT, i - 4, pe_gu)
                if active(i - 4):
                    pe.wait_ge(d_q.sem, d_q.at(i - 2, 1))
                    product(b4[:, 0:GU], [xfT[:, :, n, :] for n in range(KD)], [wgu[:, :, n, GU:] for n in range(KD)],
                            d_xfT, i - 4, pe_gu)
                if active(i - 3):
                    pe.wait_ge(o_in.sem, o_in.at(i - 3))
                    pe.wait_ge(a_kT.sem, a_kT.at(i - 2, 2))
                    transposes(b3, [oin[:, n * P:(n + 1) * P] for n in range(KD)], pe_oT)
                if active(i - 2):
                    pe.wait_ge(a_kT.sem, a_kT.at(i - 2))
                    pe.wait_ge(d_xfT.sem, d_xfT.at(i - 4))
                    pe.wait_ge(a_pT.sem, a_pT.at(i - 3))
                    pe.wait_ge(d_pos.sem, d_pos.at(i - 5, 2))
                    settle(pe)
                    for blk in range(NBLK):
                        for g in range(2):
                            t0 = (blk // 2) * 16 + g * 8 + (blk % 2) * B4
                            last = nc.tensor.matmul(score_ps[64 * g:64 * g + 64, blk * 64:blk * 64 + 64],
                                                    qT[:, t0:t0 + B4, :].rearrange("p t h -> p (t h)"),
                                                    kT[:, t0:t0 + B4, :].rearrange("p t h -> p (t h)"),
                                                    start=True, stop=True)
                    last.then_inc(pe_s.sem, 1)
                if active(i - 4):
                    pe.wait_ge(d_h.sem, d_h.at(i - 4))
                    pe.wait_ge(a_kT.sem, a_kT.at(i - 2, 4))
                    transposes(b2, [h[:, n * P:(n + 1) * P] for n in range(SI // P)], pe_hT)
                if active(i):
                    pe.wait_ge(d_lat.sem, d_lat.at(i))
                    pe.wait_ge(d_oT.sem, d_oT.at(i - 3))
                    transposes(b3, [lat[:, n * P:(n + 1) * P] for n in range(2)], pe_latT)
                if active(i - 3):
                    pe.wait_ge(a_oT.sem, a_oT.at(i - 3))
                    pe.wait_ge(d_h.sem, d_h.at(i - 4, 2))
                    pe.wait_ge(d_r.sem, d_r.at(i - 4, 2))
                    product(b7, [oT[:, :, n, :] for n in range(KD)], [wo[:, :, n, :] for n in range(KD)], d_oT, i - 3, pe_wo)
                if active(i - 1):
                    pe.wait_ge(d_h.sem, d_h.at(i - 4))
                    pe.wait_ge(d_r.sem, d_r.at(i - 4, 2))
                    for n, b in enumerate((b4, b5)):
                        if n == 1:
                            pe.wait_ge(d_lat.sem, d_lat.at(i))
                        product(b[:, 0:8 * DQ], [latT[:, 1 - par, :, 0, :]], [wq[:, :, 0, n * 8 * DQ:(n + 1) * 8 * DQ]],
                                d_latT, i - 1, pe_q)
                    pe.wait_ge(d_v.sem, d_v.at(i - 1))
                    product(b6, [latT[:, 1 - par, :, 1, :]], [wck[:, :, 0, :]], d_latT, i - 1, pe_k)
                if active(i - 2):
                    pe.wait_ge(a_exp.sem, a_exp.at(i - 2))
                    pr = prob[:].rearrange("p n t h -> p (n t h)")
                    transposes(s0, [pr[:, n * P:(n + 1) * P] for n in range(4)], pe_pT)
                    transposes(s1, [pr[:, n * P:(n + 1) * P] for n in range(4, 8)], pe_pT)
                if active(i - 4):
                    pe.wait_ge(a_hT.sem, a_hT.at(i - 4))
                    pe.wait_ge(d_y.sem, d_y.at(i - 3))
                    product(b7, [hT[:, :, n, :] for n in range(SI // P)], [wsd[:, :, n, :] for n in range(SI // P)],
                            d_hT, i - 4, pe_sh)
                if active(i - 4):
                    pe.wait_ge(d_r.sem, d_r.at(i - 4, 7))
                    pe.wait_ge(d_pos.sem, d_pos.at(i - 5))
                    pe.wait_ge(a_pT.sem, a_pT.at(i - 2))
                    nc.tensor.matmul(pos_ps, tri[:], chosen[:], start=True, stop=False)
                    nc.tensor.matmul(pos_ps, ones[:], before[:], start=False, stop=True).then_inc(pe_pos.sem, 1)
                if active(i + 1):
                    pe.wait_ge(d_ln[0].sem, d_ln[0].at(i + 1))
                    pe.wait_ge(d_hT.sem, d_hT.at(i - 4))
                    transposes(b2, [xn[:, n * P:(n + 1) * P] for n in range(KD)], pe_xT)
                if active(i - 2):
                    pe.wait_ge(a_pT.sem, a_pT.at(i - 2))
                    pe.wait_ge(d_q.sem, d_q.at(i - 1))
                    pe.wait_ge(v_in[par].sem, v_in[par].at(i - 2))
                    settle(pe)
                    for n in range(8):
                        for g in range(2):
                            last = nc.tensor.matmul(b5[64 * g:64 * g + 64, n * 64:n * 64 + 64],
                                                    probT[:, n, 64 * g:64 * g + 64],
                                                    vbd[:, par, 2 * n + g].rearrange("p b d -> p (b d)"),
                                                    start=True, stop=True)
                    last.then_inc(pe_pv.sem, 1)

            pipeline(pe, iteration)

        @block.scalar
        def _(act):
            for n, (stage, w, m, _) in enumerate(parts):
                act.wait_ge(part_in[n], 16)
                nc.scalar.copy(w[:, 0, m, :], stage).then_inc(part_hi, 1)
            act.wait_ge(part_lo, len(parts))

            def copy(dst, src, done):
                nc.scalar.copy(dst, src).then_inc(done.sem, 1)

            def iteration(i, par):
                def spread(dst, src, done, n):
                    dv = dst.rearrange("p t (m a) -> p a m t", a=2)
                    for a in range(2):
                        copy(dv[:, a, 4 * n:4 * n + 4, :],
                             src[64 * a:64 * a + DQ, :].rearrange("p (m t) -> p m t", t=P), done)

                if active(i - 2):
                    act.wait_ge(pe_s.sem, pe_s.at(i - 3))
                    act.wait_ge(pe_qT.sem, pe_qT.at(i - 2, 1))
                    spread(qT, b3, a_qT, 0)
                    act.wait_ge(pe_qT.sem, pe_qT.at(i - 2, 2))
                    spread(qT, b2, a_qT, 1)
                    act.wait_ge(pe_kT.sem, pe_kT.at(i - 2, 1))
                    spread(kT, b3, a_kT, 0)
                if active(i - 4):
                    act.wait_ge(pe_xfT.sem, pe_xfT.at(i - 4))
                    act.wait_ge(pe_gu.sem, pe_gu.at(i - 5))
                    copy(xfT[:, 0].rearrange("p k t -> p (k t)"), s0, a_xfT)
                if active(i - 2):
                    act.wait_ge(pe_kT.sem, pe_kT.at(i - 2, 2))
                    spread(kT, b2, a_kT, 1)
                if active(i - 4):
                    for n, b in enumerate((b7, b4)):
                        act.wait_ge(pe_gu.sem, pe_gu.at(i - 4, n + 1))
                        act.wait_ge(d_h.sem, d_h.at(i - 5))
                        nc.scalar.activation(th[:, n, :], b[:, 0:I], ACT.Tanh, scale=0.5).then_inc(a_th.sem, 1)
                if active(i - 3):
                    act.wait_ge(pe_oT.sem, pe_oT.at(i - 3))
                    act.wait_ge(pe_wo.sem, pe_wo.at(i - 4))
                    copy(oT[:, 0].rearrange("p k t -> p (k t)"), b3, a_oT)
                if active(i - 4):
                    act.wait_ge(d_r.sem, d_r.at(i - 4, 4))
                    nc.scalar.activation(ex[:], lg[:, 0:E], ACT.Exp, bias=ntop[:, 0:1],
                                         accum_out=esum[:, 0:1]).then_inc(a_gate.sem, 1)
                    act.wait_ge(pe_hT.sem, pe_hT.at(i - 4))
                    act.wait_ge(pe_sh.sem, pe_sh.at(i - 5))
                    copy(hT[:, 0].rearrange("p k t -> p (k t)"), b2[:, 0:SI], a_hT)
                if active(i):
                    act.wait_ge(pe_latT.sem, pe_latT.at(i))
                    act.wait_ge(pe_k.sem, pe_k.at(i - 2))
                    copy(latT[:, par, 0].rearrange("p k t -> p (k t)"), b3[:, 0:2 * P], a_latT)
                if active(i - 2):
                    act.wait_ge(d_s.sem, d_s.at(i - 2, 5))
                    pf = prob[:].rearrange("p n t h -> p (n t h)")
                    nc.scalar.activation(pf, pf, ACT.Exp, scale=SCALE).then_inc(a_exp.sem, 1)
                    act.wait_ge(pe_pv.sem, pe_pv.at(i - 3))
                    for n, b in enumerate((s0, s1)):
                        act.wait_ge(pe_pT.sem, pe_pT.at(i - 2, n + 1))
                        copy(probT[:, 4 * n:4 * n + 4, :].rearrange("p k t -> p (k t)"), b, a_pT)
                if active(i - 4):
                    act.wait_ge(pe_sh.sem, pe_sh.at(i - 4))
                    act.wait_ge(acc_out.sem, acc_out.at(i - 5))
                    copy(sh[:], b7, a_sh)
                if active(i + 1):
                    act.wait_ge(pe_xT.sem, pe_xT.at(i + 1))
                    act.wait_ge(pe_lat.sem, pe_lat.at(i))
                    copy(xT[:, 0].rearrange("p k t -> p (k t)"), b2, a_xT)

            pipeline(act, iteration)

        @block.vector
        def _(dve):
            nc.vector.memset(zero[:], 0.0).then_inc(zeroed, 1)
            nc.vector.memset(q[:], 0.0)
            nc.vector.memset(k[:], 0.0)
            nc.vector.memset(before[:], 0.0)
            nc.vector.memset(ones[:], 1.0)
            nc.vector.memset(mhalf[:], -0.5)
            nc.vector.memset(lg[:, E:E + 1], -1.0e38)
            nc.vector.memset(lg[:, E + 1:E + 2], -2.0e38)
            nc.vector.memset(rep[:, 6:7], -1.0e38)
            nc.vector.memset(rep[:, 7:8], -2.0e38).then_inc(zeroed, 1)
            dve.wait_ge(consts_in, 16)
            nc.vector.tensor_copy(tok[:], c[:, C_TOK:C_TOK + 1])
            nc.vector.tensor_copy(tri[:], c[:, C_TRI:C_TRI + P]).then_inc(cast_done, 1)
            for n, (stage, w, m, _) in enumerate(parts):
                dve.wait_ge(part_hi, n + 1)
                nc.vector.tensor_tensor(w[:, 1, m, :], stage, w[:, 0, m, :].bitcast(F32), ALU.subtract).then_inc(part_lo, 1)
            dve.wait_ge(part_lo, len(parts))
            nc.vector.memset(vbd[:], 0.0).then_inc(zeroed, 1)
            dve.wait_ge(biases_in, 16 * 5)
            dve.wait_ge(zeroed, 3)
            dve.wait_ge(cast_done, 1)

            def stats(n, src, t):
                nc.vector.bn_stats(st[n][:], src).then_inc(d_ln[n].sem, 1)
                dve.wait_ge(d_ln[n].sem, d_ln[n].at(t, 1))
                dve.wait_ge(g_rstd[n].sem, g_rstd[n].at(t - 1))
                settle(dve)
                nc.vector.bn_aggr(mv[n][:], st[n][:]).then_inc(d_ln[n].sem, 1)

            def normalise(n, dst, src, t):
                dve.wait_ge(g_rstd[n].sem, g_rstd[n].at(t))
                nc.vector.tensor_scalar(dst, src, mv[n][:, 0:1], rstd[n][:, 0:1], ALU.subtract,
                                        ALU.mult).then_inc(d_ln[n].sem, 1)

            def low_part(dst, src, done):
                nc.vector.tensor_tensor(dst[:, 1].rearrange("p k t -> p (k t)"), src,
                                        dst[:, 0].bitcast(F32).rearrange("p k t -> p (k t)"),
                                        ALU.subtract).then_inc(done.sem, 1)

            def gated(i, n, b):
                dve.wait_ge(a_th.sem, a_th.at(i - 4, n + 1))
                dve.wait_ge(pe_hT.sem, pe_hT.at(i - 5))
                nc.vector.scalar_tensor_tensor(th[:, n, :], th[:, n, :], 1.0, b[:, 0:I], ALU.add,
                                               ALU.mult).then_inc(d_h.sem, 1)
                if n == 0:
                    dve.wait_ge(a_gate.sem, a_gate.at(i - 5))
                    dve.wait_ge(d_r.sem, d_r.at(i - 5))
                nc.vector.tensor_copy(lg[:, n * 32:n * 32 + 32], b[:, 2 * I:GU]).then_inc(d_r.sem, 1)
                dve.wait_ge(d_h.sem, d_h.at(i - 4, 2 * n + 1))
                nc.vector.scalar_tensor_tensor(h[:, n * I:(n + 1) * I], th[:, n, :], 0.5, b[:, I:2 * I], ALU.mult,
                                               ALU.mult).then_inc(d_h.sem, 1)

            def iteration(i, par):
                if active(i - 4):
                    dve.wait_ge(g_x1.sem, g_x1.at(i - 4))
                    stats(2, x1[:], i - 4)
                if active(i + 1):
                    dve.wait_ge(x_in[1 - par].sem, x_in[1 - par].at(i + 1))
                    stats(0, xin[:, 1 - par, :], i + 1)
                if active(i - 4):
                    dve.wait_ge(xf_out[par].sem, xf_out[par].at(i - 6))
                    normalise(2, xf[:, par, 0:D], x1[:], i - 4)
                if active(i):
                    dve.wait_ge(pe_lat.sem, pe_lat.at(i))
                    dve.wait_ge(pe_latT.sem, pe_latT.at(i - 1))
                    nc.vector.tensor_tensor(lat[:], b5[:, 0:2 * DC], blat[:, 0:2 * DC], ALU.add).then_inc(d_lat.sem, 1)
                if active(i + 1):
                    dve.wait_ge(pe_xT.sem, pe_xT.at(i))
                    normalise(0, xn[:], xin[:, 1 - par, :], i + 1)
                if active(i - 4):
                    dve.wait_ge(a_xfT.sem, a_xfT.at(i - 4))
                    low_part(xfT, s0, d_xfT)
                if active(i):
                    dve.wait_ge(pe_kT.sem, pe_kT.at(i - 2))
                    nc.vector.tensor_tensor(k[:, par, :, DH:DQ], b5[:, 2 * DC:].rearrange("p (h d) -> p h d", h=H),
                                            blat[:, 2 * DC:].rearrange("p (h d) -> p h d", h=H),
                                            ALU.add).then_inc(d_lat.sem, 1)
                if active(i - 1):
                    dve.wait_ge(pe_v.sem, pe_v.at(i - 1))
                    dve.wait_ge(v_out.sem, v_out.at(i - 2))
                    nc.vector.tensor_tensor(v[:], b6[:], bv[:], ALU.add).then_inc(d_v.sem, 1)
                if active(i - 5):
                    dve.wait_ge(pe_pos.sem, pe_pos.at(i - 5))
                    nc.vector.scalar_tensor_tensor(fits[:], pos_ps, float(CAP), chosen[:], ALU.is_lt,
                                                   ALU.mult).then_inc(d_pos.sem, 1)
                    nc.vector.tensor_tensor(key[:], c[:, C_EB:C_EB + E], pos_ps, ALU.subtract).then_inc(d_pos.sem, 1)
                    dve.wait_ge(d_pos.sem, d_pos.at(i - 5, 2))
                    nc.vector.tensor_tensor(key2[:], key[:], fits[:], ALU.mult).then_inc(d_pos.sem, 1)
                    nc.vector.tensor_tensor(before[:], before[:], chosen[:], ALU.add).then_inc(d_pos.sem, 1)
                    dve.wait_ge(d_pos.sem, d_pos.at(i - 5, 3))
                    settle(dve)
                    nc.vector.max(key8[:], key2[:]).then_inc(d_pos.sem, 1)
                    dve.wait_ge(d_pos.sem, d_pos.at(i - 5, 5))
                    nc.vector.scalar_tensor_tensor(none8[:], key8[:], 0.0, c[:, C_TRASH:C_TRASH + 8], ALU.is_equal,
                                                   ALU.mult).then_inc(d_pos.sem, 1)
                    dve.wait_ge(slots_out.sem, slots_out.at(i - 6))
                    nc.vector.tensor_copy(toki[:], tok[:]).then_inc(d_pos.sem, 1)
                    dve.wait_ge(d_pos.sem, d_pos.at(i - 5, 7))
                    nc.vector.tensor_scalar(tok[:], tok[:], float(P), None, ALU.add).then_inc(d_pos.sem, 1)
                    nc.vector.scalar_tensor_tensor(slot[:], none8[:], KEY0, key8[:], ALU.add,
                                                   ALU.subtract).then_inc(d_pos.sem, 1)
                if active(i - 4):
                    gated(i, 0, b7)
                    gated(i, 1, b4)
                if active(i - 3):
                    dve.wait_ge(a_oT.sem, a_oT.at(i - 3))
                    low_part(oT, b3, d_oT)
                if active(i - 4):
                    dve.wait_ge(d_r.sem, d_r.at(i - 4, 2))
                    settle(dve)
                    nc.vector.max(top[:], lg[:, 0:E]).then_inc(d_r.sem, 1)
                    dve.wait_ge(d_r.sem, d_r.at(i - 4, 3))
                    nc.vector.tensor_scalar(ntop[:], top[:, 0:1], -1.0, None, ALU.mult).then_inc(d_r.sem, 1)
                    nc.vector.tensor_copy(rep[:, 0:TOPK], top[:, 0:TOPK]).then_inc(d_r.sem, 1)
                    dve.wait_ge(d_r.sem, d_r.at(i - 4, 5))
                    settle(dve)
                    nc.vector.match_replace(lgr[:], rep[:], lg[:], -3.0e38).then_inc(d_r.sem, 1)
                if active(i - 2):
                    dve.wait_ge(pe_s.sem, pe_s.at(i - 2))
                    sp4 = score_ps[:].rearrange("p (n t h) -> p n t h", n=NBLK, t=B4)
                    nc.vector.tensor_reduce(smax4[:], sp4, AX.X, ALU.max).then_inc(d_s.sem, 1)
                    dve.wait_ge(d_s.sem, d_s.at(i - 2, 1))
                    neg = c[:, C_NEG:C_NEG + B4].unsqueeze(1).broadcast_to([P, NBLK, B4])
                    nc.vector.tensor_tensor(smask4[:], smax4[:], neg, ALU.add).then_inc(d_s.sem, 1)
                    dve.wait_ge(d_s.sem, d_s.at(i - 2, 2))
                    nc.vector.tensor_reduce(smax[:], smask4[:], AX.X, ALU.max).then_inc(d_s.sem, 1)
                    dve.wait_ge(d_s.sem, d_s.at(i - 2, 3))
                    nc.vector.tensor_tensor(sref[:], smax[:].unsqueeze(2).broadcast_to([P, NBLK, B4]), neg,
                                            ALU.subtract).then_inc(d_s.sem, 1)
                    dve.wait_ge(d_s.sem, d_s.at(i - 2, 4))
                    dve.wait_ge(pe_pT.sem, pe_pT.at(i - 3))
                    nc.vector.tensor_tensor(prob[:], sp4, sref[:].unsqueeze(3).broadcast_to([P, NBLK, B4, H]),
                                            ALU.subtract).then_inc(d_s.sem, 1)
                if active(i - 4):
                    dve.wait_ge(a_hT.sem, a_hT.at(i - 4))
                    low_part(hT, b2[:, 0:SI], d_hT)
                if active(i):
                    dve.wait_ge(a_latT.sem, a_latT.at(i))
                    low_part(latT[:, par], b3[:, 0:2 * P], d_latT)
                if active(i - 3):
                    dve.wait_ge(pe_wo.sem, pe_wo.at(i - 3))
                    dve.wait_ge(d_ln[1].sem, d_ln[1].at(i - 4))
                    nc.vector.tensor_tensor(y[:], b7, bo[:], ALU.add).then_inc(d_y.sem, 1)
                if active(i - 4):
                    dve.wait_ge(d_r.sem, d_r.at(i - 4, 6))
                    dve.wait_ge(pe_pos.sem, pe_pos.at(i - 5))
                    dve.wait_ge(d_pos.sem, d_pos.at(i - 5))
                    nc.vector.tensor_tensor(chosen[:], lgr[:, 0:E], lg[:, 0:E], ALU.not_equal).then_inc(d_r.sem, 1)
                if active(i - 3):
                    dve.wait_ge(d_y.sem, d_y.at(i - 3))
                    stats(1, y[:], i - 3)
                if active(i - 1):
                    dve.wait_ge(pe_qT.sem, pe_qT.at(i - 2))
                    for n, b in enumerate((b4, b5)):
                        dve.wait_ge(pe_q.sem, pe_q.at(i - 1, n + 1))
                        nc.vector.tensor_tensor(q[:, 8 * n:8 * n + 8, 0:DQ],
                                                b[:, 0:8 * DQ].rearrange("p (h d) -> p h d", d=DQ),
                                                bq[:, n * 8 * DQ:(n + 1) * 8 * DQ].rearrange("p (h d) -> p h d", d=DQ),
                                                ALU.add).then_inc(d_q.sem, 1)
                    dve.wait_ge(pe_k.sem, pe_k.at(i - 1))
                    nc.vector.tensor_tensor(k[:, 1 - par, :, 0:DH], b6[:].rearrange("p (h d) -> p h d", d=DH),
                                            bck[:].rearrange("p (h d) -> p h d", d=DH), ALU.add).then_inc(d_k.sem, 1)
                if active(i - 3):
                    dve.wait_ge(g_x1.sem, g_x1.at(i - 4))
                    normalise(1, yn[:], y[:], i - 3)
                if active(i - 4):
                    dve.wait_ge(a_gate.sem, a_gate.at(i - 4))
                    nc.vector.reciprocal(erec[:], esum[:]).then_inc(d_r.sem, 1)
                    dve.wait_ge(d_r.sem, d_r.at(i - 4, 8))
                    nc.vector.tensor_scalar(xf[:, par, D:D + E], ex[:], erec[:, 0:1], None, ALU.mult).then_inc(d_r.sem, 1)
                if active(i - 2):
                    dve.wait_ge(a_exp.sem, a_exp.at(i - 2))
                    nc.vector.tensor_reduce(ssum[:], prob[:].rearrange("p n t h -> p n (t h)"), AX.X,
                                            ALU.add).then_inc(d_s.sem, 1)
                    dve.wait_ge(d_s.sem, d_s.at(i - 2, 6))
                    dve.wait_ge(d_pv.sem, d_pv.at(i - 3))
                    nc.vector.reciprocal(srec[:], ssum[:]).then_inc(d_s.sem, 1)
                if active(i + 1):
                    dve.wait_ge(a_xT.sem, a_xT.at(i + 1))
                    low_part(xT, b2, d_xT)
                if active(i - 2):
                    dve.wait_ge(pe_pv.sem, pe_pv.at(i - 2))
                    dve.wait_ge(o_out.sem, o_out.at(i - 3))
                    dve.wait_ge(d_s.sem, d_s.at(i - 2))
                    nc.vector.tensor_tensor(o[:].rearrange("p (n d) -> p n d", d=DH),
                                            b5[:].rearrange("p (n d) -> p n d", d=DH),
                                            srec[:].unsqueeze(2).broadcast_to([P, NBLK, DH]), ALU.mult).then_inc(d_pv.sem, 1)

            pipeline(dve, iteration)

        @block.gpsimd
        def _(pool):
            pool.wait_ge(zeroed, 3)
            pool.wait_ge(scratch_init, 48)

            def root(n, t):
                pool.wait_ge(d_ln[n].sem, d_ln[n].at(t, 2))
                settle(pool)
                nc.gpsimd.tensor_scalar(ve[n][:], mv[n][:, 1:2], EPS, None, ALU.add).then_inc(g_rstd[n].sem, 1)
                pool.wait_ge(g_rstd[n].sem, g_rstd[n].at(t, 1))
                nc.gpsimd.tensor_tensor(rstd[n][:], ve[n][:], mhalf[:], ALU.pow).then_inc(g_rstd[n].sem, 1)

            def iteration(i, par):
                if active(i - 4):
                    root(2, i - 4)
                if active(i + 1):
                    root(0, i + 1)
                if active(i - 5):
                    pool.wait_ge(d_pos.sem, d_pos.at(i - 5))
                    settle(pool)
                    for n in range(TOPK):
                        nc.gpsimd.indirect_dma_start(slot_d, bass.IndirectOffsetOnAxis(slot[:, n:n + 1].bitcast(U32), 0),
                                                     toki[:], None).then_inc(slots_out.sem, 16)
                if active(i - 3):
                    root(1, i - 3)
                    pool.wait_ge(d_ln[1].sem, d_ln[1].at(i - 3))
                    pool.wait_ge(xres_in.sem, xres_in.at(i - 3))
                    pool.wait_ge(x1_out.sem, x1_out.at(i - 4))
                    pool.wait_ge(d_ln[2].sem, d_ln[2].at(i - 4))
                    nc.gpsimd.tensor_tensor(x1[:], yn[:], xres[:], ALU.add).then_inc(g_x1.sem, 1)

            pipeline(pool, iteration)

            pool.wait_ge(slots_out.sem, slots_out.at(NT - 1))


def experts(nc, cst, w_eg, w_ed, xf_d, acc_d, slot_d):
    w1_d = w_eg.rearrange("e (p c) n -> (e p) (c n)", c=KD)
    w2_d = w_ed.rearrange("e (p c) n -> (e p) (c n)", c=2)
    PI = I // 2
    with ExitStack() as ctx:
        def sb(name, shape, dt=F32):
            return ctx.enter_context(nc.sbuf_tensor(name, shape, dt))

        def count(name, per=1, n=1, place=0):
            return Count(ctx.enter_context(nc.semaphore(name)), per, E, n, place)

        rowsT_ps, hidT_ps, out_ps, idx_ps = (ctx.enter_context(nc.psum_tensor(f"e_ps{n}", [P, 512], F32))[:]
                                             for n in range(4))
        gu_ps = [ctx.enter_context(nc.psum_tensor(f"e_gu{n}", [P, 2 * I], F32))[:] for n in range(2)]
        NW = 4
        w1 = sb("w1", [P, NW, KD, 2 * I])
        w2 = sb("w2", [PI, NW, 2, D])
        ident = sb("e_ident", [P, P])
        table = sb("table", [E, CAP], I32)
        tablef = sb("tablef", [E, CAP])
        idx = sb("idx", [CAP, E], I32)
        gidx = sb("gidx", [CAP, 2, 1], I32)
        sidx = sb("sidx", [CAP, 2, 1], I32)
        xg = sb("xg", [P, 2, D + E])
        xgT = sb("xgT", [P, 2, KD, P])
        gate = sb("gate", [P, 2])
        tanh = sb("tanh", [P, 2, I])
        hid = sb("hid", [P, 2, I])
        hidT = sb("hidT", [PI, 2, P])
        eo = sb("eo", [P, 2, D])

        start = ctx.enter_context(nc.semaphore("start"))
        setup = ctx.enter_context(nc.semaphore("setup"))
        w1_in = [count(f"w1_in{n}", 32, NW, n) for n in range(NW)]
        x_got = [count(f"x_got{n}", 16, 2, n) for n in range(2)]
        added = count("added", 16)
        e_xT = count("e_xT")
        e_gu = count("e_gu")
        e_hT = count("e_hT")
        e_out = count("e_out")
        ea_xT = count("ea_xT")
        ea_tanh = count("ea_tanh")
        ea_hT = count("ea_hT")
        ea_out = count("ea_out")
        ed_gidx = count("ed_gidx")
        ed_sidx = count("ed_sidx")
        ed_gate = count("ed_gate")
        ed_h = count("ed_h", 2)

        block = ctx.enter_context(nc.Block())
        FIRST, LOOP, LAST = -3, 2, E + 1
        ROUNDS = (E - 2 - LOOP) // NW
        REST = LOOP + ROUNDS * NW
        assert REST + 2 <= E

        def active(e):
            return not isinstance(e, int) or 0 <= e < E

        def pipeline(eng, iteration):
            for j in range(FIRST, LOOP):
                iteration(j, j % NW)
            with eng.Fori(0, ROUNDS) as r:
                for u in range(NW):
                    iteration(r * NW + (LOOP + u), (LOOP + u) % NW)
            for j in range(REST, LAST):
                iteration(j, j % NW)

        @block.sync
        def _(sp):
            sp.dma_start(table[:], slot_d[0:E * CAP, :].rearrange("(e s) o -> e (s o)", s=CAP)).then_inc(start, 16)
            sp.dma_start(ident[:], cst[:, C_ID:C_ID + P]).then_inc(start, 16)

            def load(e, place):
                sp.wait_ge(e_out.sem, e_out.at(e - NW))
                sp.nop(nofuse=True)
                a, b = ((w1_d[e * P:(e + 1) * P, :], w2_d[e * PI:(e + 1) * PI, :]) if isinstance(e, int) else
                        (w1_d[bass.ts(e, P), :], w2_d[bass.ts(e, PI), :]))
                sp.dma_start(w1[:, place].rearrange("p c n -> p (c n)"), a).then_inc(w1_in[place].sem, 16)
                sp.dma_start(w2[:, place].rearrange("p c n -> p (c n)"), b).then_inc(w1_in[place].sem, 16)

            for e in range(NW):
                load(e, e)
            with sp.Fori(1, E // NW) as r:
                for u in range(NW):
                    load(r * NW + u, u)

        @block.tensor
        def _(pe):
            pe.wait_ge(start, 32)
            pe.wait_ge(setup, 1)
            nc.tensor.transpose(idx_ps[:, 0:E], tablef[:], ident[0:E, 0:E]).then_inc(setup, 1)

            def iteration(j, place):
                par = place % 2
                if active(j):
                    pe.wait_ge(ea_xT.sem, ea_xT.at(j))
                    pe.wait_ge(w1_in[place].sem, w1_in[place].at(j))
                    pe.wait_ge(ed_h.sem, ed_h.at(j - 2))
                    for n in range(KD):
                        last = nc.tensor.matmul(gu_ps[par], xgT[:, par, n, :], w1[:, place, n, :],
                                                start=(n == 0), stop=(n == KD - 1))
                    last.then_inc(e_gu.sem, 1)
                if active(j - 1):
                    pe.wait_ge(ed_h.sem, ed_h.at(j - 1))
                    pe.wait_ge(ea_hT.sem, ea_hT.at(j - 2))
                    for n in range(2):
                        last = nc.tensor.transpose(hidT_ps[0:PI, n * P:(n + 1) * P],
                                                   hid[:, 1 - par, :].rearrange("p (i c) -> p c i", c=2)[:, n, :],
                                                   ident[:])
                    last.then_inc(e_hT.sem, 1)
                if active(j + 1):
                    pe.wait_ge(x_got[1 - par].sem, x_got[1 - par].at(j + 1))
                    pe.wait_ge(ea_xT.sem, ea_xT.at(j))
                    for n in range(KD):
                        last = nc.tensor.transpose(rowsT_ps[:, n * P:(n + 1) * P],
                                                   xg[:, 1 - par, 0:D].rearrange("p (i c) -> p c i", c=KD)[:, n, :],
                                                   ident[:])
                    last.then_inc(e_xT.sem, 1)
                if active(j - 1):
                    pe.wait_ge(ea_hT.sem, ea_hT.at(j - 1))
                    pe.wait_ge(ea_out.sem, ea_out.at(j - 2))
                    for n in range(2):
                        last = nc.tensor.matmul(out_ps, hidT[:, n, :], w2[:, (place - 1) % NW, n, :],
                                                start=(n == 0), stop=(n == 1))
                    last.then_inc(e_out.sem, 1)

            pipeline(pe, iteration)

        @block.scalar
        def _(act):
            def iteration(j, place):
                par = place % 2
                if active(j - 1):
                    act.wait_ge(e_hT.sem, e_hT.at(j - 1))
                    act.wait_ge(e_out.sem, e_out.at(j - 2))
                    nc.scalar.copy(hidT[:].rearrange("p c s -> p (c s)"), hidT_ps[0:PI, 0:2 * P]).then_inc(ea_hT.sem, 1)
                if active(j + 1):
                    act.wait_ge(e_xT.sem, e_xT.at(j + 1))
                    act.wait_ge(e_gu.sem, e_gu.at(j - 1))
                    nc.scalar.copy(xgT[:, 1 - par].rearrange("p k s -> p (k s)"), rowsT_ps).then_inc(ea_xT.sem, 1)
                if active(j - 1):
                    act.wait_ge(e_out.sem, e_out.at(j - 1))
                    act.wait_ge(added.sem, added.at(j - 3))
                    nc.scalar.copy(eo[:, 1 - par, :], out_ps).then_inc(ea_out.sem, 1)
                if active(j):
                    act.wait_ge(e_gu.sem, e_gu.at(j))
                    act.wait_ge(ed_h.sem, ed_h.at(j - 2))
                    nc.scalar.activation(tanh[:, par, :], gu_ps[par][:, 0:I], ACT.Tanh, scale=0.5).then_inc(ea_tanh.sem, 1)

            pipeline(act, iteration)

        @block.vector
        def _(dve):
            dve.wait_ge(start, 32)
            nc.vector.tensor_copy(tablef[:], table[:]).then_inc(setup, 1)
            dve.wait_ge(setup, 2)
            nc.vector.tensor_copy(idx[:], idx_ps[:, 0:E]).then_inc(setup, 1)
            dve.wait_ge(setup, 3)

            def column(ap, e):
                return ap[:, e:e + 1] if isinstance(e, int) else ap[:, bass.ds(e, 1)]

            def iteration(j, place):
                par = place % 2
                if active(j + 2):
                    dve.wait_ge(x_got[par].sem, x_got[par].at(j))
                    dve.nop(nofuse=True)
                    nc.vector.tensor_copy(gidx[:, par, :], column(idx[:], j + 2)).then_inc(ed_gidx.sem, 1)
                if active(j - 1):
                    dve.wait_ge(added.sem, added.at(j - 3))
                    dve.nop(nofuse=True)
                    nc.vector.tensor_copy(sidx[:, 1 - par, :], column(idx[:], j - 1)).then_inc(ed_sidx.sem, 1)
                if active(j):
                    dve.wait_ge(x_got[par].sem, x_got[par].at(j))
                    dve.wait_ge(ed_h.sem, ed_h.at(j - 1))
                    nc.vector.tensor_scalar(gate[:, par:par + 1], column(xg[:, par, D:D + E], j), 0.5, None,
                                            ALU.mult).then_inc(ed_gate.sem, 1)
                    dve.wait_ge(ea_tanh.sem, ea_tanh.at(j))
                    nc.vector.scalar_tensor_tensor(tanh[:, par, :], tanh[:, par, :], 1.0, gu_ps[par][:, 0:I],
                                                   ALU.add, ALU.mult).then_inc(ed_h.sem, 1)
                    dve.wait_ge(ed_h.sem, ed_h.at(j, 1))
                    dve.wait_ge(ed_gate.sem, ed_gate.at(j))
                    dve.wait_ge(e_hT.sem, e_hT.at(j - 2))
                    nc.vector.scalar_tensor_tensor(hid[:, par, :], tanh[:, par, :], gate[:, par:par + 1],
                                                   gu_ps[par][:, I:], ALU.mult, ALU.mult).then_inc(ed_h.sem, 1)

            pipeline(dve, iteration)

        @block.gpsimd
        def _(pool):
            def iteration(j, place):
                par = place % 2
                if active(j + 2):
                    pool.wait_ge(ed_gidx.sem, ed_gidx.at(j + 2))
                    pool.wait_ge(e_xT.sem, e_xT.at(j))
                    pool.wait_ge(ed_gate.sem, ed_gate.at(j))
                    pool.nop(nofuse=True)
                    nc.gpsimd.indirect_dma_start(xg[:, par, :], None, xf_d, bass.IndirectOffsetOnAxis(
                        gidx[:, par, :].bitcast(U32), 0)).then_inc(x_got[par].sem, 16)
                if active(j - 1):
                    pool.wait_ge(ea_out.sem, ea_out.at(j - 1))
                    pool.wait_ge(ed_sidx.sem, ed_sidx.at(j - 1))
                    pool.wait_ge(added.sem, added.at(j - 2))
                    pool.nop(nofuse=True)
                    nc.gpsimd.indirect_dma_start(acc_d, bass.IndirectOffsetOnAxis(
                        sidx[:, 1 - par, :].bitcast(U32), 0), eo[:, 1 - par, :], None,
                        compute_op=ALU.add).then_inc(added.sem, 16)

            pipeline(pool, iteration)
            pool.wait_ge(added.sem, added.at(E - 1))


def last_norm(nc, x1_d, acc_d, out):
    G, NB = 2, 4
    NG = NT // G
    with ExitStack() as ctx:
        def sb(name, shape, dt=F32):
            return ctx.enter_context(nc.sbuf_tensor(name, shape, dt))

        def count(name, per=1, n=1, place=0):
            return Count(ctx.enter_context(nc.semaphore(name)), per, NG, n, place)

        acc = sb("f_acc", [P, NB, G, D])
        res = sb("f_res", [P, NB, G, D])
        st = sb("f_st", [P, NB, G, 6])
        mv = sb("f_mv", [P, NB, G, 2])
        ve = sb("f_ve", [P, NB, G])
        rstd = sb("f_rstd", [P, NB, G])
        mhalf = sb("f_mhalf", [P, G])
        ready = ctx.enter_context(nc.semaphore("f_ready"))
        acc_in = [count(f"f_acc_in{n}", 16, NB, n) for n in range(NB)]
        res_in = [count(f"f_res_in{n}", 16, NB, n) for n in range(NB)]
        f_out = [count(f"f_out{n}", 16, NB, n) for n in range(NB)]
        stats = count("f_stats", 2 * G)
        roots = count("f_roots", 2)
        normed = count("f_normed", G)
        summed = count("f_summed", 1)

        def group(ap):
            return ap.rearrange("(g p r) d -> (g p) (r d)", p=P, r=G)

        def rows(ap, t):
            return ap[t * P:(t + 1) * P, :] if isinstance(t, int) else ap[bass.ts(t, P), :]

        def ring(eng, body, first=0):
            for u in range(NB):
                body(u, u)
            with eng.Fori(1, NG // NB) as r:
                for u in range(NB):
                    body(r * NB + u, u)

        block = ctx.enter_context(nc.Block())

        @block.sync
        def _(sp):
            def load(t, u):
                sp.wait_ge(f_out[u].sem, f_out[u].at(t - NB))
                sp.nop(nofuse=True)
                sp.dma_start(acc[:, u].rearrange("p r d -> p (r d)"), rows(group(acc_d[0:T, :]), t)).then_inc(acc_in[u].sem, 16)
                sp.dma_start(res[:, u].rearrange("p r d -> p (r d)"), rows(group(x1_d), t)).then_inc(res_in[u].sem, 16)

            ring(sp, load)

        @block.scalar
        def _(act):
            def store(t, u):
                act.wait_ge(summed.sem, summed.at(t))
                act.nop(nofuse=True)
                act.dma_start(rows(group(out), t), res[:, u].rearrange("p r d -> p (r d)")).then_inc(f_out[u].sem, 16)

            ring(act, store)
            for u in range(NB):
                act.wait_ge(f_out[u].sem, 16 * (NG // NB))

        @block.vector
        def _(dve):
            nc.vector.memset(mhalf[:], -0.5).then_inc(ready, 1)

            def statistics(t, u):
                dve.wait_ge(acc_in[u].sem, acc_in[u].at(t))
                dve.wait_ge(roots.sem, roots.at(t - NB))
                for g in range(G):
                    nc.vector.bn_stats(st[:, u, g, :], acc[:, u, g, :]).then_inc(stats.sem, 1)
                dve.wait_ge(stats.sem, stats.at(t, G))
                dve.nop(nofuse=True)
                for g in range(G):
                    nc.vector.bn_aggr(mv[:, u, g, :], st[:, u, g, :]).then_inc(stats.sem, 1)

            def normalise(t, u):
                dve.wait_ge(roots.sem, roots.at(t))
                for g in range(G):
                    nc.vector.tensor_scalar(acc[:, u, g, :], acc[:, u, g, :], mv[:, u, g, 0:1], rstd[:, u, g:g + 1],
                                            ALU.subtract, ALU.mult).then_inc(normed.sem, 1)

            def body(t, u):
                statistics(t, u)
                if not isinstance(t, int) or t > 0:
                    normalise(t - 1, (u - 1) % NB)

            ring(dve, body)
            normalise(NG - 1, NB - 1)

        @block.gpsimd
        def _(pool):
            pool.wait_ge(ready, 1)

            def add(t, u):
                pool.wait_ge(normed.sem, normed.at(t))
                pool.wait_ge(res_in[u].sem, res_in[u].at(t))
                nc.gpsimd.tensor_tensor(res[:, u], acc[:, u], res[:, u], ALU.add).then_inc(summed.sem, 1)

            def body(t, u):
                pool.wait_ge(stats.sem, stats.at(t))
                pool.wait_ge(normed.sem, normed.at(t - NB))
                pool.nop(nofuse=True)
                nc.gpsimd.tensor_scalar(ve[:, u], mv[:, u, :, 1], EPS, None, ALU.add).then_inc(roots.sem, 1)
                pool.wait_ge(roots.sem, roots.at(t, 1))
                nc.gpsimd.tensor_tensor(rstd[:, u], ve[:, u], mhalf[:], ALU.pow).then_inc(roots.sem, 1)
                if not isinstance(t, int) or t > 0:
                    add(t - 1, (u - 1) % NB)

            ring(pool, body)
            add(NG - 1, NB - 1)


def kernel(**inputs):
    from concourse import bacc
    from concourse.bass_utils import run_bass_kernel_spmd

    a = {n: np.asarray(v) for n, v in inputs.items()}
    at, ff = (lambda n: a["L0_attn_" + n]), (lambda n: a["L0_ffn_" + n])
    cst, slot_init = constants()
    w_q = np.concatenate([at("Wcq").reshape(DC, H, DH), at("Wqr").reshape(DC, H, DR)], 2).reshape(DC, H * DQ)
    b_q = np.concatenate([at("bcq").reshape(H, DH), at("bqr").reshape(H, DR)], 1).reshape(H * DQ)
    g, u, r = ff("shared_gate_w").T, ff("shared_up_w").T, ff("gate_w").T
    w_gu = np.concatenate([g[:, 0:I], u[:, 0:I], r[:, 0:E // 2], g[:, I:], u[:, I:], r[:, E // 2:]], 1)
    arrays = {
        "x": at("h_t").reshape(T, D), "cst": cst, "slot_init": slot_init,
        "w_lat": np.concatenate([at("Wc"), at("Wckv"), at("Wkr")], 1),
        "b_lat": np.concatenate([at("bc"), at("bckv"), at("bkr")]),
        "w_q": w_q, "b_q": b_q, "w_ck": at("Wck"), "b_ck": at("bck"), "w_v": at("Wv"), "b_v": at("bv"),
        "w_o": at("Wo"), "b_o": at("bo"), "w_gu": w_gu, "w_sd": ff("shared_down_w").T,
        "w_eg": ff("gate_up_proj"), "w_ed": ff("down_proj"),
    }
    arrays = {n: np.ascontiguousarray(v) for n, v in arrays.items()}
    nc = bacc.Bacc("TRN2", target_bir_lowering=False, num_devices=1)
    args = [nc.dram_tensor(n, v.shape, mybir.dt.from_np(v.dtype), kind="ExternalInput").ap() for n, v in arrays.items()]
    out = nc.dram_tensor("out", (T, D), F32, kind="ExternalOutput").ap()
    layer_kernel(nc, *args, out)
    r = run_bass_kernel_spmd(nc, [arrays], core_ids=[0])
    return r.results[0]["out"].reshape(4, 2048, D)
```

```python
from contextlib import ExitStack

import numpy as np

import concourse.bass as bass
from concourse import mybir

F32 = mybir.dt.float32
F32R = mybir.dt.float32r
BF16 = mybir.dt.bfloat16
I32 = mybir.dt.int32
U32 = mybir.dt.uint32
ALU = mybir.AluOpType
ACT = mybir.ActivationFunctionType
AX = mybir.AxisListType

P = 128
T = 4 * 2048
NT = T // P
D = 512
KD = D // P
H = 16
DH = 32
DR = 16
DQ = DH + DR
HS = 64
DC = 128
SCALE = 1.0 / float(np.sqrt(DQ))
E = 64
TOPK = 6
CAP = 128
I = 192
SI = 384
EPS = 1e-5
B4 = 4
NBLK = P // (2 * B4)
BIG = 1.0e30
KEY0 = 16384.0
PI = I // 2
NW = 4
G = 2
GU = SI + E // 2

C_ID, C_TRI, C_EB, C_NEG, C_TRASH, C_TOK, C_END = np.cumsum([0, P, P, E, B4, 8, 1]).tolist()


def constants():
    c = np.zeros((P, C_END), np.float32)
    p = np.arange(P)
    c[:, C_ID:C_ID + P] = np.eye(P)
    c[:, C_TRI:C_TRI + P] = p[:, None] < p[None, :]
    c[:, C_EB:C_EB + E] = KEY0 - CAP * np.arange(E)
    c[:, C_NEG:C_NEG + B4] = np.where((p[:, None] // H) % B4 == np.arange(B4), 0.0, -BIG)
    c[:, C_TRASH:C_TRASH + 8] = p[:, None] + P * np.arange(8) + E * CAP - KEY0
    c[:, C_TOK] = p
    slots = np.tile(T + np.arange(CAP, dtype=np.int32), E + TOPK).reshape((E + TOPK) * CAP, 1)
    return c, slots


class Count:

    def __init__(self, sem, per, total, n=1, place=0):
        self.sem, self.per, self.total, self.n, self.place = sem, per, total, n, place

    def at(self, t, k=None):
        k = self.per if k is None else k
        if not isinstance(t, int):
            return t * (self.per // self.n) + (k - self.place * self.per // self.n)
        m = (t - self.place) // self.n
        return min(max(m * self.per + k, 0) if m >= 0 else 0, self.total // self.n * self.per)


def settle(eng):
    eng.nop(nofuse=True)


def layer_kernel(nc, x, cst, slot_init, w_lat, b_lat, w_q, b_q, w_ck, b_ck, w_v, b_v, w_o, b_o,
                 w_gu, w_sd, w_eg, w_ed, out):
    x1_d = nc.dram_tensor("x1_scratch", (T, D), F32).ap()
    xf_d = nc.dram_tensor("xf_scratch", (T + CAP, D + E), F32).ap()
    acc_d = nc.dram_tensor("acc_scratch", (T + CAP, D), F32).ap()
    v_d = nc.dram_tensor("v_scratch", (2, P, D), F32).ap()
    o_d = nc.dram_tensor("o_scratch", (2, P, D), F32).ap()
    slot_d = nc.dram_tensor("slot_scratch", ((E + TOPK) * CAP, 1), I32).ap()

    with ExitStack() as ctx:
        def sb(name, shape, dt=F32):
            return ctx.enter_context(nc.sbuf_tensor(name, shape, dt))

        with ExitStack() as early:
            wlat, wq, wck, wv = (early.enter_context(nc.sbuf_tensor(name, shape, F32R)) for name, shape in (
                ("wlat", [P, 2, KD, 512]), ("wq", [P, 2, 1, H * DQ]), ("wck", [P, 2, 1, D]), ("wv", [P, 2, 1, D])))
        w1 = sb("w1", [P, NW, KD, 2 * I])
        w2 = sb("w2", [P, NW, 2, D])
        w_in = [Count(ctx.enter_context(nc.semaphore(f"w_in{n}")), 32, E, NW, n) for n in range(NW)]
        w1_d = w_eg.rearrange("e (p c) n -> (e p) (c n)", c=KD)
        w2_d = w_ed.rearrange("e (p c) n -> (e p) (c n)", c=2)

        def load_expert(sp, e, place):
            a, b = ((w1_d[e * P:(e + 1) * P, :], w2_d[e * PI:(e + 1) * PI, :]) if isinstance(e, int) else
                    (w1_d[bass.ts(e, P), :], w2_d[bass.ts(e, PI), :]))
            sp.dma_start(w1[:, place].rearrange("p c n -> p (c n)"), a).then_inc(w_in[place].sem, 16)
            sp.dma_start(w2[0:PI, place].rearrange("p c n -> p (c n)"), b).then_inc(w_in[place].sem, 16)

        token_pipeline(nc, x, cst, slot_init, w_lat, b_lat, w_q, b_q, w_ck, b_ck, w_v, b_v, w_o, b_o, w_gu, w_sd,
                       x1_d, xf_d, acc_d, v_d, o_d, slot_d, wlat, wq, wck, wv, load_expert)
        res = sb("res", [P, NT // G, G * D])
        res_in = ctx.enter_context(nc.semaphore("res_in"))
        experts(nc, cst, w1, w2, w_in, load_expert, xf_d, acc_d, slot_d, x1_d, res, res_in)
        last_norm(nc, acc_d, out, res, res_in)


def group(ap):
    return ap.rearrange("(g p r) d -> (g p) (r d)", p=P, r=G)


def token_pipeline(nc, x, cst, slot_init, w_lat, b_lat, w_q, b_q, w_ck, b_ck, w_v, b_v, w_o, b_o, w_gu, w_sd,
                   x1_d, xf_d, acc_d, v_d, o_d, slot_d, wlat, wq, wck, wv, load_expert):
    ctx = ExitStack()
    with ctx:
        def sb(name, shape, dt=F32):
            return ctx.enter_context(nc.sbuf_tensor(name, shape, dt))

        def sem(name):
            return ctx.enter_context(nc.semaphore(name))

        def count(name, per=1, n=1, place=0):
            return Count(sem(name), per, NT, n, place)

        bank = [ctx.enter_context(nc.psum_tensor(f"bank{n}", [P, 512], F32)) for n in range(2, 8)]
        score_ps = ctx.enter_context(nc.psum_tensor("score_ps", [P, 1024], F32))
        b2, b3, b4, b5, b6, b7 = (b[:] for b in bank)
        s0, s1 = score_ps[:, 0:512], score_ps[:, 512:1024]
        pos_ps = s1[:, 0:E]

        c = sb("c", [P, C_END])
        ident = c[:, C_ID:C_ID + P]
        tri = sb("tri", [P, P], BF16)
        ones = sb("ones", [P, P], BF16)
        mhalf = sb("mhalf", [P, 1])
        wo = sb("wo", [P, 2, KD, D], F32R)
        wgu = sb("wgu", [P, 2, KD, 2 * GU], F32R)
        wsd = sb("wsd", [P, 2, SI // P, D], F32R)
        blat = sb("blat", [P, 512])
        bq = sb("bq", [P, H * DQ])
        bck = sb("bck", [P, D])
        bv = sb("bv", [P, D])
        bo = sb("bo", [P, D])
        xin = sb("xin", [P, 2, D])
        xn = sb("xn", [P, D])
        xT = sb("xT", [P, 2, KD, P], F32R)
        lat = sb("lat", [P, 2 * DC])
        latT = sb("latT", [P, 2, 2, 2, P], F32R)
        q = sb("q", [P, H, HS])
        k = sb("k", [P, 2, H, HS])
        v = sb("v", [P, D])
        vbd = sb("vbd", [P, 2, NBLK, 2, DH])
        qT_all = sb("qT", [P, P, H])
        kT_all = sb("kT", [P, P, H])
        qT, kT = qT_all[0:DQ], kT_all[0:DQ]
        prob = sb("prob", [P, NBLK, B4, H])
        probT = sb("probT", [P, 8, P])
        o = sb("o", [P, D])
        oin = sb("oin", [P, D])
        oT = sb("oT", [P, 2, KD, P], F32R)
        y = sb("y", [P, D])
        yn = sb("yn", [P, D])
        xres = sb("xres", [P, D])
        x1 = sb("x1", [P, D])
        xf = sb("xf", [P, 2, D + E])
        xfT = sb("xfT", [P, 2, KD, P], F32R)
        th = sb("th", [P, 2, I])
        h = sb("h", [P, SI])
        hT = sb("hT", [P, 2, SI // P, P], F32R)
        sh = sb("sh", [P, D])
        zero = sb("zero", [P, D + E])
        st = [sb(f"st{n}", [P, 6]) for n in range(3)]
        mv = [sb(f"mv{n}", [P, 2]) for n in range(3)]
        ve = [sb(f"ve{n}", [P, 1]) for n in range(3)]
        rstd = [sb(f"rstd{n}", [P, 1]) for n in range(3)]
        smax4 = sb("smax4", [P, NBLK, B4])
        smask4 = sb("smask4", [P, NBLK, B4])
        smax = sb("smax", [P, NBLK])
        sref = sb("sref", [P, NBLK, B4])
        ssum = sb("ssum", [P, NBLK])
        srec = sb("srec", [P, NBLK])
        lg = sb("lg", [P, E + 2])
        top = sb("top", [P, 8])
        rep = sb("rep", [P, 8])
        lgr = sb("lgr", [P, E + 2])
        ntop = sb("ntop", [P, 1])
        ex = sb("ex", [P, E])
        esum = sb("esum", [P, 1])
        erec = sb("erec", [P, 1])
        chosen = sb("chosen", [P, E], BF16)
        before = sb("before", [P, E], BF16)
        fits = sb("fits", [P, E])
        key = sb("key", [P, E])
        key2 = sb("key2", [P, E])
        key8 = sb("key8", [P, 8])
        none8 = sb("none8", [P, 8])
        slot = sb("slot", [P, 8], I32)
        tok = sb("tok", [P, 1])
        toki = sb("toki", [P, 1], I32)

        qs, ks = qT_all[:].rearrange("p t h -> p (t h)"), kT_all[:].rearrange("p t h -> p (t h)")
        vs = vbd[:].rearrange("p a n b d -> p (a n b d)")
        ps, pts = prob[:].rearrange("p n t h -> p (n t h)"), probT[:].rearrange("p n t -> p (n t)")
        parts = [(qs[:, 512 * n:512 * n + 512], wlat, n, w_lat[n * P:(n + 1) * P, :]) for n in range(KD)]
        parts += [(ks[:, 0:H * DQ], wq, 0, w_q), (ks[:, 768:1280], wck, 0, w_ck), (ks[:, 1280:1792], wv, 0, w_v)]
        parts += [(vs[:, D * n:D * n + D], wo, n, w_o[n * P:(n + 1) * P, :]) for n in range(KD)]
        parts += [(stage, wgu, n, w_gu[n * P:(n + 1) * P, :])
                  for n, stage in enumerate((ps[:, 0:2 * GU], pts[:, 0:2 * GU], qs[:, 0:2 * GU], qs[:, 1024:1024 + 2 * GU]))]
        parts += [(ks[:, D * n:D * n + D], wsd, n, w_sd[n * P:(n + 1) * P, :]) for n in range(SI // P)]
        SPLIT_BEFORE = {13: 4, 14: 4, 15: 7, 16: 7, 17: 7}
        PART_AT = [-1] * 4 + [0] * 9 + [1] * 5

        consts_in = sem("consts_in")
        part_in = [sem(f"part_in{n}") for n in range(len(parts))]
        latent_bias_in = sem("latent_bias_in")
        biases_in = sem("biases_in")
        part_hi = sem("part_hi")
        part_lo = sem("part_lo")
        scratch_init = sem("scratch_init")
        zeroed = sem("zeroed")
        cast_done = sem("cast_done")
        x_in = [count(f"x_in{n}", 16, 2, n) for n in range(2)]
        xres_in = count("xres_in", 16)
        v_out = count("v_out", 16)
        v_in = [count(f"v_in{n}", 32, 2, n) for n in range(2)]
        o_out = count("o_out", 64)
        o_in = count("o_in", 16)
        x1_out = count("x1_out", 16)
        acc_out = count("acc_out", 16)
        xf_out = [count(f"xf_out{n}", 16, 2, n) for n in range(2)]
        slots_out = count("slots_out", 16 * TOPK)
        pe_xT = count("pe_xT")
        pe_lat = count("pe_lat")
        pe_latT = count("pe_latT")
        pe_q = count("pe_q", 2)
        pe_k = count("pe_k")
        pe_v = count("pe_v")
        pe_qT = count("pe_qT", 2)
        pe_kT = count("pe_kT", 2)
        pe_s = count("pe_s", 2)
        pe_pT = count("pe_pT", 2)
        pe_pv = count("pe_pv")
        pe_oT = count("pe_oT")
        pe_wo = count("pe_wo")
        pe_xfT = count("pe_xfT")
        pe_gu = count("pe_gu", 2)
        pe_hT = count("pe_hT")
        pe_sh = count("pe_sh")
        pe_pos = count("pe_pos")
        a_xT = count("a_xT")
        a_latT = count("a_latT")
        a_qT = count("a_qT", 4)
        a_kT = count("a_kT", 4)
        a_exp = count("a_exp", 2)
        a_pT = count("a_pT", 2)
        a_oT = count("a_oT")
        a_xfT = count("a_xfT")
        a_th = count("a_th", 2)
        a_hT = count("a_hT")
        a_sh = count("a_sh")
        a_gate = count("a_gate")
        d_ln = [count(f"d_ln{n}", 3) for n in range(3)]
        d_xT = count("d_xT")
        d_latT = count("d_latT")
        d_oT = count("d_oT")
        d_xfT = count("d_xfT")
        d_hT = count("d_hT")
        d_y = count("d_y")
        d_lat = count("d_lat", 2)
        d_q = count("d_q", 2)
        d_k = count("d_k")
        d_v = count("d_v")
        d_s = count("d_s", 9)
        d_pv = count("d_pv")
        d_h = count("d_h", 4)
        d_r = count("d_r", 9)
        d_pos = count("d_pos", 9)
        g_rstd = [count(f"g_rstd{n}", 2) for n in range(3)]
        g_x1 = count("g_x1")

        block = ctx.enter_context(nc.Block())

        FIRST, LOOP, LAST = -2, 6, NT + 5
        REST = NT - 2
        PAIRS = (REST - LOOP) // 2
        assert LOOP + 2 * PAIRS == REST

        def active(t):
            return not isinstance(t, int) or 0 <= t < NT

        def pipeline(eng, iteration):
            for i in range(FIRST, LOOP):
                iteration(i, i % 2)
            with eng.Fori(0, PAIRS) as r:
                for u in range(2):
                    iteration(r * 2 + (LOOP + u), (LOOP + u) % 2)
            for i in range(REST, LAST):
                iteration(i, i % 2)

        def rows(ap, t):
            return ap[t * P:(t + 1) * P, :] if isinstance(t, int) else ap[bass.ts(t, P), :]

        @block.sync
        def _(sp):
            for t in range(2):
                sp.dma_start(xin[:, t, :], rows(x, t)).then_inc(x_in[t].sem, 16)
            sp.dma_start(c[:], cst).then_inc(consts_in, 16)
            for n, (stage, _, _, src) in enumerate(parts):
                if n in SPLIT_BEFORE:
                    sp.wait_ge(part_lo, SPLIT_BEFORE[n])
                sp.dma_start(stage, src).then_inc(part_in[n], 16)
                if n == KD - 1:
                    sp.dma_start(blat[:], b_lat.partition_broadcast(P)).then_inc(latent_bias_in, 16)

            def iteration(i, par):
                if active(i - 3):
                    sp.wait_ge(d_pv.sem, d_pv.at(i - 3))
                    sp.wait_ge(o_in.sem, o_in.at(i - 5))
                    dst = o_d[1 - par].rearrange("(c g b t) (h d) -> g b (t h) c d", c=8, g=2, b=2, h=H)
                    src = o[:].rearrange("p (c b d) -> p b c d", c=8, b=2)
                    for g in range(2):
                        for b in range(2):
                            sp.dma_start(dst[g, b], src[64 * g:64 * g + 64, b]).then_inc(o_out.sem, 16)
                    sp.wait_ge(o_out.sem, o_out.at(i - 3))
                    sp.wait_ge(pe_oT.sem, pe_oT.at(i - 4))
                    sp.dma_start(oin[:], o_d[1 - par]).then_inc(o_in.sem, 16)
                if active(i + 2) and (not isinstance(i, int) or i >= 0):
                    sp.wait_ge(d_ln[0].sem, d_ln[0].at(i))
                    settle(sp)
                    sp.dma_start(xin[:, par, :], rows(x, i + 2)).then_inc(x_in[par].sem, 16)
                if isinstance(i, int) and i == FIRST:
                    sp.dma_start(slot_d, slot_init).then_inc(scratch_init, 16)
                    sp.wait_ge(zeroed, 2)
                    sp.dma_start(xf_d[T:T + CAP, :], zero[:]).then_inc(scratch_init, 16)
                    sp.dma_start(acc_d[T:T + CAP, :], zero[:, 0:D]).then_inc(scratch_init, 16)
                if active(i - 4):
                    sp.wait_ge(g_x1.sem, g_x1.at(i - 4))
                    settle(sp)
                    sp.dma_start(rows(x1_d, i - 4), x1[:]).then_inc(x1_out.sem, 16)
                if active(i - 3):
                    sp.wait_ge(g_x1.sem, g_x1.at(i - 4))
                    settle(sp)
                    sp.dma_start(xres[:], rows(x, i - 3)).then_inc(xres_in.sem, 16)
                if active(i - 5):
                    sp.wait_ge(a_sh.sem, a_sh.at(i - 5))
                    settle(sp)
                    sp.dma_start(rows(acc_d, i - 5), sh[:]).then_inc(acc_out.sem, 16)
                if isinstance(i, int) and i == 1:
                    sp.wait_ge(zeroed, 3)
                if active(i - 1):
                    sp.wait_ge(d_v.sem, d_v.at(i - 1))
                    sp.wait_ge(v_in[1 - par].sem, v_in[1 - par].at(i - 3))
                    sp.dma_start(v_d[1 - par], v[:]).then_inc(v_out.sem, 16)
                    sp.wait_ge(v_out.sem, v_out.at(i - 1))
                    settle(sp)
                    sp.wait_ge(pe_pv.sem, pe_pv.at(i - 3))
                    settle(sp)
                    src = v_d[1 - par].rearrange("(cg b t) (j d) -> b (t j) cg d", cg=NBLK, b=2, j=H)
                    for b in range(2):
                        sp.dma_start(vbd[64 * b:64 * b + 64, 1 - par, :, b, :], src[b]).then_inc(v_in[1 - par].sem, 16)
                if active(i - 4):
                    sp.wait_ge(d_r.sem, d_r.at(i - 4))
                    settle(sp)
                    sp.dma_start(rows(xf_d, i - 4), xf[:, par, :]).then_inc(xf_out[par].sem, 16)
                if isinstance(i, int) and i == NT + 2:
                    sp.wait_ge(pe_k.sem, pe_k.at(NT - 1))
                    for e in range(NW):
                        load_expert(sp, e, e)

            pipeline(sp, iteration)
            sp.wait_ge(acc_out.sem, acc_out.at(NT - 1))
            sp.wait_ge(x1_out.sem, x1_out.at(NT - 1))
            for n in range(2):
                sp.wait_ge(xf_out[n].sem, xf_out[n].at(NT - 2 + n))

        @block.tensor
        def _(pe):
            pe.wait_ge(consts_in, 16)
            pe.wait_ge(cast_done, 1)

            def transposes(dst, srcs, done):
                for n, s in enumerate(srcs):
                    last = nc.tensor.transpose(dst[0:s.shape[1], n * P:(n + 1) * P], s, ident)
                last.then_inc(done.sem, 1)

            def product(dst, lhs, rhs, low, t, done):
                for n, (a, b) in enumerate(zip(lhs, rhs)):
                    nc.tensor.matmul(dst, a[:, 0], b[:, 0], start=(n == 0), stop=False)
                    nc.tensor.matmul(dst, a[:, 0], b[:, 1], start=False, stop=False)
                pe.wait_ge(low.sem, low.at(t))
                for n, (a, b) in enumerate(zip(lhs, rhs)):
                    last = nc.tensor.matmul(dst, a[:, 1], b[:, 0], start=False, stop=(n == len(lhs) - 1))
                last.then_inc(done.sem, 1)

            def turn(src, done, n, dst):
                transposes(dst, [src[:, 2 * m:2 * m + 2, :].rearrange("p h d -> p (h d)")
                                 for m in range(4 * n, 4 * n + 4)], done)

            def scores(blocks):
                for blk in blocks:
                    for g in range(2):
                        t0 = (blk // 2) * 16 + g * 8 + (blk % 2) * B4
                        last = nc.tensor.matmul(score_ps[64 * g:64 * g + 64, blk * 64:blk * 64 + 64],
                                                qT[:, t0:t0 + B4, :].rearrange("p t h -> p (t h)"),
                                                kT[:, t0:t0 + B4, :].rearrange("p t h -> p (t h)"),
                                                start=True, stop=True)
                return last

            def iteration(i, par):
                if active(i - 2):
                    pe.wait_ge(d_q.sem, d_q.at(i - 2))
                    pe.wait_ge(d_latT.sem, d_latT.at(i - 1))
                    pe.wait_ge(d_k.sem, d_k.at(i - 2))
                    turn(q, pe_qT, 0, b3)
                if active(i - 2):
                    turn(q, pe_qT, 1, b6)
                if isinstance(i, int) and i == 0:
                    pe.wait_ge(part_lo, KD)
                if isinstance(i, int) and i == 1:
                    pe.wait_ge(part_lo, KD + 3)
                if isinstance(i, int) and i == 2:
                    pe.wait_ge(part_lo, len(parts))
                if active(i):
                    pe.wait_ge(a_xT.sem, a_xT.at(i))
                    pe.wait_ge(d_q.sem, d_q.at(i - 2))
                    product(b5, [xT[:, :, n, :] for n in range(KD)], [wlat[:, :, n, :] for n in range(KD)], d_xT, i, pe_lat)
                if active(i - 4):
                    pe.wait_ge(d_ln[2].sem, d_ln[2].at(i - 4))
                    pe.wait_ge(a_pT.sem, a_pT.at(i - 3, 1))
                    transposes(s0, [xf[:, par, n * P:(n + 1) * P] for n in range(KD)], pe_xfT)
                if active(i - 2):
                    pe.wait_ge(d_k.sem, d_k.at(i - 2))
                    pe.wait_ge(d_lat.sem, d_lat.at(i - 2))
                    pe.wait_ge(a_qT.sem, a_qT.at(i - 2, 2))
                    turn(k[:, par], pe_kT, 0, b3)
                    pe.wait_ge(d_xT.sem, d_xT.at(i))
                    turn(k[:, par], pe_kT, 1, b2)
                if active(i - 1):
                    pe.wait_ge(a_latT.sem, a_latT.at(i - 1))
                    pe.wait_ge(a_qT.sem, a_qT.at(i - 2))
                    product(b6, [latT[:, 1 - par, :, 1, :]], [wv[:, :, 0, :]], d_latT, i - 1, pe_v)
                if active(i - 4):
                    pe.wait_ge(a_xfT.sem, a_xfT.at(i - 4))
                    pe.wait_ge(a_sh.sem, a_sh.at(i - 5))
                    product(b7[:, 0:GU], [xfT[:, :, n, :] for n in range(KD)], [wgu[:, :, n, 0:GU] for n in range(KD)],
                            d_xfT, i - 4, pe_gu)
                if active(i - 2):
                    pe.wait_ge(a_kT.sem, a_kT.at(i - 2))
                    pe.wait_ge(d_xfT.sem, d_xfT.at(i - 4))
                    pe.wait_ge(a_pT.sem, a_pT.at(i - 3))
                    settle(pe)
                    scores(range(0, NBLK // 2)).then_inc(pe_s.sem, 1)
                if active(i - 4):
                    pe.wait_ge(d_pv.sem, d_pv.at(i - 3))
                    product(b4[:, 0:GU], [xfT[:, :, n, :] for n in range(KD)], [wgu[:, :, n, GU:] for n in range(KD)],
                            d_xfT, i - 4, pe_gu)
                if active(i - 2):
                    pe.wait_ge(d_pos.sem, d_pos.at(i - 5, 2))
                    settle(pe)
                    scores(range(NBLK // 2, NBLK * 3 // 4))
                if active(i - 3):
                    pe.wait_ge(o_in.sem, o_in.at(i - 3))
                    pe.wait_ge(a_kT.sem, a_kT.at(i - 2, 2))
                    transposes(b3, [oin[:, n * P:(n + 1) * P] for n in range(KD)], pe_oT)
                if active(i - 2):
                    scores(range(NBLK * 3 // 4, NBLK)).then_inc(pe_s.sem, 1)
                if active(i - 4):
                    pe.wait_ge(d_h.sem, d_h.at(i - 4))
                    pe.wait_ge(a_kT.sem, a_kT.at(i - 2, 4))
                    transposes(b2, [h[:, n * P:(n + 1) * P] for n in range(SI // P)], pe_hT)
                if active(i - 3):
                    pe.wait_ge(a_oT.sem, a_oT.at(i - 3))
                    pe.wait_ge(d_h.sem, d_h.at(i - 4, 2))
                    pe.wait_ge(d_r.sem, d_r.at(i - 4, 2))
                    product(b7, [oT[:, :, n, :] for n in range(KD)], [wo[:, :, n, :] for n in range(KD)], d_oT, i - 3, pe_wo)
                if active(i - 1):
                    pe.wait_ge(d_h.sem, d_h.at(i - 4))
                    pe.wait_ge(d_r.sem, d_r.at(i - 4, 2))
                    for n, b in enumerate((b4, b5)):
                        if n == 1:
                            pe.wait_ge(d_lat.sem, d_lat.at(i))
                        product(b[:, 0:8 * DQ], [latT[:, 1 - par, :, 0, :]], [wq[:, :, 0, n * 8 * DQ:(n + 1) * 8 * DQ]],
                                d_latT, i - 1, pe_q)
                    pe.wait_ge(d_v.sem, d_v.at(i - 1))
                    product(b6, [latT[:, 1 - par, :, 1, :]], [wck[:, :, 0, :]], d_latT, i - 1, pe_k)
                if active(i):
                    pe.wait_ge(d_lat.sem, d_lat.at(i))
                    pe.wait_ge(d_oT.sem, d_oT.at(i - 3))
                    transposes(b3, [lat[:, n * P:(n + 1) * P] for n in range(2)], pe_latT)
                if active(i - 2):
                    pe.wait_ge(a_exp.sem, a_exp.at(i - 2, 1))
                    pr = prob[:].rearrange("p n t h -> p (n t h)")
                    transposes(s0, [pr[:, n * P:(n + 1) * P] for n in range(4)], pe_pT)
                    pe.wait_ge(a_exp.sem, a_exp.at(i - 2, 2))
                    transposes(s1, [pr[:, n * P:(n + 1) * P] for n in range(4, 8)], pe_pT)
                if active(i + 1):
                    pe.wait_ge(d_ln[0].sem, d_ln[0].at(i + 1))
                    pe.wait_ge(d_hT.sem, d_hT.at(i - 4))
                    transposes(b2, [xn[:, n * P:(n + 1) * P] for n in range(KD)], pe_xT)
                if active(i - 4):
                    pe.wait_ge(a_hT.sem, a_hT.at(i - 4))
                    pe.wait_ge(d_y.sem, d_y.at(i - 3))
                    product(b7, [hT[:, :, n, :] for n in range(SI // P)], [wsd[:, :, n, :] for n in range(SI // P)],
                            d_hT, i - 4, pe_sh)
                if active(i - 4):
                    pe.wait_ge(d_r.sem, d_r.at(i - 4, 7))
                    pe.wait_ge(d_pos.sem, d_pos.at(i - 5))
                    pe.wait_ge(a_pT.sem, a_pT.at(i - 2))
                    nc.tensor.matmul(pos_ps, tri[:], chosen[:], start=True, stop=False)
                    nc.tensor.matmul(pos_ps, ones[:], before[:], start=False, stop=True).then_inc(pe_pos.sem, 1)
                if active(i - 2):
                    pe.wait_ge(a_pT.sem, a_pT.at(i - 2))
                    pe.wait_ge(d_q.sem, d_q.at(i - 1, 1))
                    pe.wait_ge(v_in[par].sem, v_in[par].at(i - 2))
                    settle(pe)
                    for n in range(8):
                        for g in range(2):
                            last = nc.tensor.matmul(b4[64 * g:64 * g + 64, n * 64:n * 64 + 64],
                                                    probT[:, n, 64 * g:64 * g + 64],
                                                    vbd[:, par, 2 * n + g].rearrange("p b d -> p (b d)"),
                                                    start=True, stop=True)
                    last.then_inc(pe_pv.sem, 1)

            pipeline(pe, iteration)

        @block.scalar
        def _(act):

            def split(i):
                for n, (stage, w, m, _) in enumerate(parts):
                    if PART_AT[n] == i:
                        act.wait_ge(part_in[n], 16)
                        nc.scalar.copy(w[:, 0, m, :], stage).then_inc(part_hi, 1)

            def copy(dst, src, done):
                nc.scalar.copy(dst, src).then_inc(done.sem, 1)

            def iteration(i, par):
                def spread(dst, src, done, n):
                    dv = dst.rearrange("p t (m a) -> p a m t", a=2)
                    for a in range(2):
                        copy(dv[:, a, 4 * n:4 * n + 4, :],
                             src[64 * a:64 * a + DQ, :].rearrange("p (m t) -> p m t", t=P), done)

                if isinstance(i, int) and i == 0:
                    for dst, src in ((bq, b_q), (bck, b_ck), (bv, b_v), (bo, b_o)):
                        act.dma_start(dst[:], src.partition_broadcast(P)).then_inc(biases_in, 16)
                if isinstance(i, int) and i in PART_AT:
                    split(i)
                if isinstance(i, int) and i == 2:
                    act.wait_ge(part_lo, len(parts))
                if active(i - 2):
                    act.wait_ge(pe_s.sem, pe_s.at(i - 3))
                    act.wait_ge(pe_qT.sem, pe_qT.at(i - 2, 1))
                    spread(qT, b3, a_qT, 0)
                    act.wait_ge(pe_qT.sem, pe_qT.at(i - 2, 2))
                    spread(qT, b6, a_qT, 1)
                if active(i - 4):
                    act.wait_ge(pe_xfT.sem, pe_xfT.at(i - 4))
                    act.wait_ge(pe_gu.sem, pe_gu.at(i - 5))
                    copy(xfT[:, 0].rearrange("p k t -> p (k t)"), s0, a_xfT)
                if active(i - 2):
                    act.wait_ge(pe_kT.sem, pe_kT.at(i - 2, 1))
                    spread(kT, b3, a_kT, 0)
                    act.wait_ge(pe_kT.sem, pe_kT.at(i - 2, 2))
                    spread(kT, b2, a_kT, 1)
                if active(i - 4):
                    for n, b in enumerate((b7, b4)):
                        act.wait_ge(pe_gu.sem, pe_gu.at(i - 4, n + 1))
                        act.wait_ge(d_h.sem, d_h.at(i - 5))
                        nc.scalar.activation(th[:, n, :], b[:, 0:I], ACT.Tanh, scale=0.5).then_inc(a_th.sem, 1)
                if active(i - 3):
                    act.wait_ge(pe_oT.sem, pe_oT.at(i - 3))
                    act.wait_ge(pe_wo.sem, pe_wo.at(i - 4))
                    copy(oT[:, 0].rearrange("p k t -> p (k t)"), b3, a_oT)
                if active(i - 4):
                    act.wait_ge(d_r.sem, d_r.at(i - 4, 4))
                    nc.scalar.activation(ex[:], lg[:, 0:E], ACT.Exp, bias=ntop[:, 0:1],
                                         accum_out=esum[:, 0:1]).then_inc(a_gate.sem, 1)
                    act.wait_ge(pe_hT.sem, pe_hT.at(i - 4))
                    act.wait_ge(pe_sh.sem, pe_sh.at(i - 5))
                    copy(hT[:, 0].rearrange("p k t -> p (k t)"), b2[:, 0:SI], a_hT)
                if active(i - 2):
                    for n in range(2):
                        act.wait_ge(d_s.sem, d_s.at(i - 2, 6 + n))
                        pf = prob[:, n * NBLK // 2:(n + 1) * NBLK // 2].rearrange("p n t h -> p (n t h)")
                        nc.scalar.activation(pf, pf, ACT.Exp, scale=SCALE).then_inc(a_exp.sem, 1)
                if active(i):
                    act.wait_ge(pe_latT.sem, pe_latT.at(i))
                    act.wait_ge(pe_k.sem, pe_k.at(i - 2))
                    copy(latT[:, par, 0].rearrange("p k t -> p (k t)"), b3[:, 0:2 * P], a_latT)
                if active(i - 2):
                    act.wait_ge(pe_pv.sem, pe_pv.at(i - 3))
                    for n, b in enumerate((s0, s1)):
                        act.wait_ge(pe_pT.sem, pe_pT.at(i - 2, n + 1))
                        copy(probT[:, 4 * n:4 * n + 4, :].rearrange("p k t -> p (k t)"), b, a_pT)
                if active(i + 1):
                    act.wait_ge(pe_xT.sem, pe_xT.at(i + 1))
                    act.wait_ge(pe_lat.sem, pe_lat.at(i))
                    copy(xT[:, 0].rearrange("p k t -> p (k t)"), b2, a_xT)
                if active(i - 4):
                    act.wait_ge(pe_sh.sem, pe_sh.at(i - 4))
                    act.wait_ge(acc_out.sem, acc_out.at(i - 5))
                    copy(sh[:], b7, a_sh)

            pipeline(act, iteration)

        @block.vector
        def _(dve):
            nc.vector.memset(zero[:], 0.0).then_inc(zeroed, 1)
            nc.vector.memset(q[:], 0.0)
            nc.vector.memset(k[:], 0.0)
            nc.vector.memset(before[:], 0.0)
            nc.vector.memset(ones[:], 1.0)
            nc.vector.memset(mhalf[:], -0.5)
            nc.vector.memset(lg[:, E:E + 1], -1.0e38)
            nc.vector.memset(lg[:, E + 1:E + 2], -2.0e38)
            nc.vector.memset(rep[:, 6:7], -1.0e38)
            nc.vector.memset(rep[:, 7:8], -2.0e38).then_inc(zeroed, 1)
            dve.wait_ge(consts_in, 16)
            nc.vector.tensor_copy(tok[:], c[:, C_TOK:C_TOK + 1])
            nc.vector.tensor_copy(tri[:], c[:, C_TRI:C_TRI + P]).then_inc(cast_done, 1)
            dve.wait_ge(zeroed, 2)
            dve.wait_ge(cast_done, 1)

            def split(i):
                for n, (stage, w, m, _) in enumerate(parts):
                    if PART_AT[n] == i:
                        dve.wait_ge(part_hi, n + 1)
                        nc.vector.tensor_tensor(w[:, 1, m, :], stage, w[:, 0, m, :].bitcast(F32),
                                                ALU.subtract).then_inc(part_lo, 1)

            def stats(n, src, t):
                nc.vector.bn_stats(st[n][:], src).then_inc(d_ln[n].sem, 1)
                dve.wait_ge(d_ln[n].sem, d_ln[n].at(t, 1))
                dve.wait_ge(g_rstd[n].sem, g_rstd[n].at(t - 1))
                settle(dve)
                nc.vector.bn_aggr(mv[n][:], st[n][:]).then_inc(d_ln[n].sem, 1)

            def normalise(n, dst, src, t):
                dve.wait_ge(g_rstd[n].sem, g_rstd[n].at(t))
                nc.vector.tensor_scalar(dst, src, mv[n][:, 0:1], rstd[n][:, 0:1], ALU.subtract,
                                        ALU.mult).then_inc(d_ln[n].sem, 1)

            def low_part(dst, src, done):
                nc.vector.tensor_tensor(dst[:, 1].rearrange("p k t -> p (k t)"), src,
                                        dst[:, 0].bitcast(F32).rearrange("p k t -> p (k t)"),
                                        ALU.subtract).then_inc(done.sem, 1)

            def gated(i, n, b):
                dve.wait_ge(a_th.sem, a_th.at(i - 4, n + 1))
                dve.wait_ge(pe_hT.sem, pe_hT.at(i - 5))
                nc.vector.scalar_tensor_tensor(th[:, n, :], th[:, n, :], 1.0, b[:, 0:I], ALU.add,
                                               ALU.mult).then_inc(d_h.sem, 1)
                if n == 0:
                    dve.wait_ge(a_gate.sem, a_gate.at(i - 5))
                    dve.wait_ge(d_r.sem, d_r.at(i - 5))
                nc.vector.tensor_copy(lg[:, n * 32:n * 32 + 32], b[:, 2 * I:GU]).then_inc(d_r.sem, 1)
                dve.wait_ge(d_h.sem, d_h.at(i - 4, 2 * n + 1))
                nc.vector.scalar_tensor_tensor(h[:, n * I:(n + 1) * I], th[:, n, :], 0.5, b[:, I:2 * I], ALU.mult,
                                               ALU.mult).then_inc(d_h.sem, 1)

            def iteration(i, par):
                if active(i + 1):
                    dve.wait_ge(x_in[1 - par].sem, x_in[1 - par].at(i + 1))
                    stats(0, xin[:, 1 - par, :], i + 1)
                if isinstance(i, int) and i in PART_AT:
                    split(i)
                if isinstance(i, int) and i == 0:
                    dve.wait_ge(latent_bias_in, 16)
                if isinstance(i, int) and i == 1:
                    dve.wait_ge(biases_in, 16 * 4)
                if active(i):
                    dve.wait_ge(pe_lat.sem, pe_lat.at(i))
                    dve.wait_ge(pe_latT.sem, pe_latT.at(i - 1))
                    nc.vector.tensor_tensor(lat[:], b5[:, 0:2 * DC], blat[:, 0:2 * DC], ALU.add).then_inc(d_lat.sem, 1)
                if active(i - 4):
                    dve.wait_ge(a_xfT.sem, a_xfT.at(i - 4))
                    low_part(xfT, s0, d_xfT)
                if active(i + 1):
                    dve.wait_ge(pe_xT.sem, pe_xT.at(i))
                    normalise(0, xn[:], xin[:, 1 - par, :], i + 1)
                if active(i):
                    dve.wait_ge(pe_kT.sem, pe_kT.at(i - 2))
                    nc.vector.tensor_tensor(k[:, par, :, DH:DQ], b5[:, 2 * DC:].rearrange("p (h d) -> p h d", h=H),
                                            blat[:, 2 * DC:].rearrange("p (h d) -> p h d", h=H),
                                            ALU.add).then_inc(d_lat.sem, 1)
                if active(i - 1):
                    dve.wait_ge(pe_v.sem, pe_v.at(i - 1))
                    dve.wait_ge(v_out.sem, v_out.at(i - 2))
                    nc.vector.tensor_tensor(v[:], b6[:], bv[:], ALU.add).then_inc(d_v.sem, 1)
                if active(i - 5):
                    dve.wait_ge(pe_pos.sem, pe_pos.at(i - 5))
                    nc.vector.scalar_tensor_tensor(fits[:], pos_ps, float(CAP), chosen[:], ALU.is_lt,
                                                   ALU.mult).then_inc(d_pos.sem, 1)
                    nc.vector.tensor_tensor(key[:], c[:, C_EB:C_EB + E], pos_ps, ALU.subtract).then_inc(d_pos.sem, 1)
                    dve.wait_ge(d_pos.sem, d_pos.at(i - 5, 2))
                    nc.vector.tensor_tensor(key2[:], key[:], fits[:], ALU.mult).then_inc(d_pos.sem, 1)
                    nc.vector.tensor_tensor(before[:], before[:], chosen[:], ALU.add).then_inc(d_pos.sem, 1)
                    dve.wait_ge(d_pos.sem, d_pos.at(i - 5, 3))
                    settle(dve)
                    nc.vector.max(key8[:], key2[:]).then_inc(d_pos.sem, 1)
                    dve.wait_ge(d_pos.sem, d_pos.at(i - 5, 5))
                    nc.vector.scalar_tensor_tensor(none8[:], key8[:], 0.0, c[:, C_TRASH:C_TRASH + 8], ALU.is_equal,
                                                   ALU.mult).then_inc(d_pos.sem, 1)
                    dve.wait_ge(slots_out.sem, slots_out.at(i - 6))
                    nc.vector.tensor_copy(toki[:], tok[:]).then_inc(d_pos.sem, 1)
                    dve.wait_ge(d_pos.sem, d_pos.at(i - 5, 7))
                    nc.vector.tensor_scalar(tok[:], tok[:], float(P), None, ALU.add).then_inc(d_pos.sem, 1)
                    nc.vector.scalar_tensor_tensor(slot[:], none8[:], KEY0, key8[:], ALU.add,
                                                   ALU.subtract).then_inc(d_pos.sem, 1)
                if active(i - 4):
                    gated(i, 0, b7)
                    gated(i, 1, b4)
                if active(i - 4):
                    dve.wait_ge(d_r.sem, d_r.at(i - 4, 2))
                    settle(dve)
                    nc.vector.max(top[:], lg[:, 0:E]).then_inc(d_r.sem, 1)
                    dve.wait_ge(d_r.sem, d_r.at(i - 4, 3))
                    nc.vector.tensor_scalar(ntop[:], top[:, 0:1], -1.0, None, ALU.mult).then_inc(d_r.sem, 1)
                    nc.vector.tensor_copy(rep[:, 0:TOPK], top[:, 0:TOPK]).then_inc(d_r.sem, 1)
                    dve.wait_ge(d_r.sem, d_r.at(i - 4, 5))
                    settle(dve)
                    nc.vector.match_replace(lgr[:], rep[:], lg[:], -3.0e38).then_inc(d_r.sem, 1)
                sp4 = score_ps[:].rearrange("p (n t h) -> p n t h", n=NBLK, t=B4)
                half = [slice(n * NBLK // 2, (n + 1) * NBLK // 2) for n in range(2)]
                if active(i - 2):
                    dve.wait_ge(pe_s.sem, pe_s.at(i - 2, 1))
                    nc.vector.tensor_reduce(smax4[:, half[0]], sp4[:, half[0]], AX.X, ALU.max).then_inc(d_s.sem, 1)
                if active(i - 3):
                    dve.wait_ge(a_oT.sem, a_oT.at(i - 3))
                    low_part(oT, b3, d_oT)
                if active(i - 2):
                    dve.wait_ge(pe_s.sem, pe_s.at(i - 2, 2))
                    nc.vector.tensor_reduce(smax4[:, half[1]], sp4[:, half[1]], AX.X, ALU.max).then_inc(d_s.sem, 1)
                    dve.wait_ge(d_s.sem, d_s.at(i - 2, 2))
                    neg = c[:, C_NEG:C_NEG + B4].unsqueeze(1).broadcast_to([P, NBLK, B4])
                    nc.vector.tensor_tensor(smask4[:], smax4[:], neg, ALU.add).then_inc(d_s.sem, 1)
                    dve.wait_ge(d_s.sem, d_s.at(i - 2, 3))
                    nc.vector.tensor_reduce(smax[:], smask4[:], AX.X, ALU.max).then_inc(d_s.sem, 1)
                    dve.wait_ge(d_s.sem, d_s.at(i - 2, 4))
                    nc.vector.tensor_tensor(sref[:], smax[:].unsqueeze(2).broadcast_to([P, NBLK, B4]), neg,
                                            ALU.subtract).then_inc(d_s.sem, 1)
                    dve.wait_ge(d_s.sem, d_s.at(i - 2, 5))
                    dve.wait_ge(pe_pT.sem, pe_pT.at(i - 3))
                    for n in range(2):
                        nc.vector.tensor_tensor(prob[:, half[n]], sp4[:, half[n]],
                                                sref[:, half[n]].unsqueeze(3).broadcast_to([P, NBLK // 2, B4, H]),
                                                ALU.subtract).then_inc(d_s.sem, 1)
                if active(i - 4):
                    dve.wait_ge(a_hT.sem, a_hT.at(i - 4))
                    low_part(hT, b2[:, 0:SI], d_hT)
                if active(i - 3):
                    dve.wait_ge(pe_wo.sem, pe_wo.at(i - 3))
                    dve.wait_ge(d_ln[1].sem, d_ln[1].at(i - 4))
                    nc.vector.tensor_tensor(y[:], b7, bo[:], ALU.add).then_inc(d_y.sem, 1)
                if active(i - 4):
                    dve.wait_ge(d_r.sem, d_r.at(i - 4, 6))
                    dve.wait_ge(pe_pos.sem, pe_pos.at(i - 5))
                    dve.wait_ge(d_pos.sem, d_pos.at(i - 5))
                    nc.vector.tensor_tensor(chosen[:], lgr[:, 0:E], lg[:, 0:E], ALU.not_equal).then_inc(d_r.sem, 1)
                if active(i - 3):
                    dve.wait_ge(d_y.sem, d_y.at(i - 3))
                    stats(1, y[:], i - 3)
                if active(i - 1):
                    dve.wait_ge(pe_qT.sem, pe_qT.at(i - 2))
                    for n, b in enumerate((b4, b5)):
                        dve.wait_ge(pe_q.sem, pe_q.at(i - 1, n + 1))
                        nc.vector.tensor_tensor(q[:, 8 * n:8 * n + 8, 0:DQ],
                                                b[:, 0:8 * DQ].rearrange("p (h d) -> p h d", d=DQ),
                                                bq[:, n * 8 * DQ:(n + 1) * 8 * DQ].rearrange("p (h d) -> p h d", d=DQ),
                                                ALU.add).then_inc(d_q.sem, 1)
                if active(i - 3):
                    dve.wait_ge(g_x1.sem, g_x1.at(i - 4))
                    normalise(1, yn[:], y[:], i - 3)
                if active(i):
                    dve.wait_ge(a_latT.sem, a_latT.at(i))
                    low_part(latT[:, par], b3[:, 0:2 * P], d_latT)
                if active(i - 1):
                    dve.wait_ge(pe_k.sem, pe_k.at(i - 1))
                    nc.vector.tensor_tensor(k[:, 1 - par, :, 0:DH], b6[:].rearrange("p (h d) -> p h d", d=DH),
                                            bck[:].rearrange("p (h d) -> p h d", d=DH), ALU.add).then_inc(d_k.sem, 1)
                if active(i + 1):
                    dve.wait_ge(a_xT.sem, a_xT.at(i + 1))
                    low_part(xT, b2, d_xT)
                if active(i - 3):
                    dve.wait_ge(g_x1.sem, g_x1.at(i - 3))
                    stats(2, x1[:], i - 3)
                if active(i - 4):
                    dve.wait_ge(a_gate.sem, a_gate.at(i - 4))
                    nc.vector.reciprocal(erec[:], esum[:]).then_inc(d_r.sem, 1)
                    dve.wait_ge(d_r.sem, d_r.at(i - 4, 8))
                    nc.vector.tensor_scalar(xf[:, par, D:D + E], ex[:], erec[:, 0:1], None, ALU.mult).then_inc(d_r.sem, 1)
                if active(i - 2):
                    dve.wait_ge(a_exp.sem, a_exp.at(i - 2))
                    nc.vector.tensor_reduce(ssum[:], prob[:].rearrange("p n t h -> p n (t h)"), AX.X,
                                            ALU.add).then_inc(d_s.sem, 1)
                    dve.wait_ge(d_s.sem, d_s.at(i - 2, 8))
                    dve.wait_ge(d_pv.sem, d_pv.at(i - 3))
                    nc.vector.reciprocal(srec[:], ssum[:]).then_inc(d_s.sem, 1)
                if active(i - 3):
                    dve.wait_ge(xf_out[1 - par].sem, xf_out[1 - par].at(i - 5))
                    normalise(2, xf[:, 1 - par, 0:D], x1[:], i - 3)
                if active(i - 2):
                    dve.wait_ge(pe_pv.sem, pe_pv.at(i - 2))
                    dve.wait_ge(o_out.sem, o_out.at(i - 3))
                    dve.wait_ge(d_s.sem, d_s.at(i - 2))
                    nc.vector.tensor_tensor(o[:].rearrange("p (n d) -> p n d", d=DH),
                                            b4[:].rearrange("p (n d) -> p n d", d=DH),
                                            srec[:].unsqueeze(2).broadcast_to([P, NBLK, DH]), ALU.mult).then_inc(d_pv.sem, 1)

            pipeline(dve, iteration)

        @block.gpsimd
        def _(pool):
            pool.wait_ge(zeroed, 2)

            def root(n, t):
                pool.wait_ge(d_ln[n].sem, d_ln[n].at(t, 2))
                settle(pool)
                nc.gpsimd.tensor_scalar(ve[n][:], mv[n][:, 1:2], EPS, None, ALU.add).then_inc(g_rstd[n].sem, 1)
                pool.wait_ge(g_rstd[n].sem, g_rstd[n].at(t, 1))
                nc.gpsimd.tensor_tensor(rstd[n][:], ve[n][:], mhalf[:], ALU.pow).then_inc(g_rstd[n].sem, 1)

            def iteration(i, par):
                if active(i + 1):
                    root(0, i + 1)
                if isinstance(i, int) and i == 5:
                    pool.wait_ge(scratch_init, 48)
                if isinstance(i, int) and i == 0:
                    pool.wait_ge(part_lo, 11)
                    nc.gpsimd.memset(vbd[:], 0.0).then_inc(zeroed, 1)
                if active(i - 5):
                    pool.wait_ge(d_pos.sem, d_pos.at(i - 5))
                    settle(pool)
                    for n in range(TOPK):
                        nc.gpsimd.indirect_dma_start(slot_d, bass.IndirectOffsetOnAxis(slot[:, n:n + 1].bitcast(U32), 0),
                                                     toki[:], None).then_inc(slots_out.sem, 16)
                if active(i - 3):
                    root(1, i - 3)
                    pool.wait_ge(d_ln[1].sem, d_ln[1].at(i - 3))
                    pool.wait_ge(xres_in.sem, xres_in.at(i - 3))
                    pool.wait_ge(x1_out.sem, x1_out.at(i - 4))
                    pool.wait_ge(d_ln[2].sem, d_ln[2].at(i - 4))
                    nc.gpsimd.tensor_tensor(x1[:], yn[:], xres[:], ALU.add).then_inc(g_x1.sem, 1)
                    root(2, i - 3)

            pipeline(pool, iteration)

            pool.wait_ge(slots_out.sem, slots_out.at(NT - 1))


def experts(nc, cst, w1, w2, w_in, load_expert, xf_d, acc_d, slot_d, x1_d, res, res_in):
    with ExitStack() as ctx:
        def sb(name, shape, dt=F32):
            return ctx.enter_context(nc.sbuf_tensor(name, shape, dt))

        def count(name, per=1, n=1, place=0):
            return Count(ctx.enter_context(nc.semaphore(name)), per, E, n, place)

        rowsT_ps, hidT_ps, out_ps, idx_ps = (ctx.enter_context(nc.psum_tensor(f"e_ps{n}", [P, 512], F32))[:]
                                             for n in range(4))
        gu_ps = [ctx.enter_context(nc.psum_tensor(f"e_gu{n}", [P, 2 * I], F32))[:] for n in range(2)]
        ident = sb("e_ident", [P, P])
        table = sb("table", [E, CAP], I32)
        tablef = sb("tablef", [E, CAP])
        idx = sb("idx", [CAP, E], I32)
        gidx = sb("gidx", [CAP, 2, 1], I32)
        sidx = sb("sidx", [CAP, 2, 1], I32)
        xg = sb("xg", [P, 2, D + E])
        xgT = sb("xgT", [P, 2, KD, P])
        gate = sb("gate", [P, 2])
        tanh = sb("tanh", [P, 2, I])
        hid = sb("hid", [P, 2, I])
        hidT = sb("hidT", [PI, 2, P])
        eo = sb("eo", [P, 2, D])

        start = ctx.enter_context(nc.semaphore("start"))
        setup = ctx.enter_context(nc.semaphore("setup"))
        x_got = [count(f"x_got{n}", 16, 2, n) for n in range(2)]
        added = count("added", 16)
        e_xT = count("e_xT")
        e_gu = count("e_gu")
        e_hT = count("e_hT")
        e_out = count("e_out")
        ea_xT = count("ea_xT")
        ea_tanh = count("ea_tanh")
        ea_hT = count("ea_hT")
        ea_out = count("ea_out")
        ed_gidx = count("ed_gidx")
        ed_sidx = count("ed_sidx")
        ed_gate = count("ed_gate")
        ed_h = count("ed_h", 2)

        block = ctx.enter_context(nc.Block())
        EARLY = NT // G // 8
        GROUPS = NT // G // (E // NW)
        WITH_X1 = (NT // G - EARLY) // GROUPS
        assert EARLY + WITH_X1 * GROUPS == NT // G and 1 + WITH_X1 <= E // NW
        FIRST, LOOP, LAST = -3, 2, E + 1
        ROUNDS = (E - 2 - LOOP) // NW
        REST = LOOP + ROUNDS * NW
        assert REST + 2 <= E

        def active(e):
            return not isinstance(e, int) or 0 <= e < E

        def pipeline(eng, iteration):
            for j in range(FIRST, LOOP):
                iteration(j, j % NW)
            with eng.Fori(0, ROUNDS) as r:
                for u in range(NW):
                    iteration(r * NW + (LOOP + u), (LOOP + u) % NW)
            for j in range(REST, LAST):
                iteration(j, j % NW)

        @block.sync
        def _(sp):
            sp.dma_start(table[:], slot_d[0:E * CAP, :].rearrange("(e s) o -> e (s o)", s=CAP)).then_inc(start, 16)
            sp.dma_start(ident[:], cst[:, C_ID:C_ID + P]).then_inc(start, 16)

            def load_group(g):
                g_rows = group(x1_d)[g * P:(g + 1) * P, :] if isinstance(g, int) else group(x1_d)[bass.ts(g, P), :]
                dst = res[:, g, :] if isinstance(g, int) else res[:, bass.ds(g, 1), :].rearrange("p g n -> p (g n)")
                sp.dma_start(dst, g_rows).then_inc(res_in, 16)

            def load_round(r, with_x1):
                for u in range(NW):
                    sp.wait_ge(e_out.sem, e_out.at((r - 1) * NW + u))
                    settle(sp)
                    load_expert(sp, r * NW + u, u)
                    if with_x1 and u % (NW // GROUPS) == 0:
                        load_group(r * GROUPS + (EARLY - GROUPS) + u // (NW // GROUPS))

            for g in range(EARLY):
                load_group(g)
            with sp.Fori(1, 1 + WITH_X1) as r:
                load_round(r, True)
            with sp.Fori(1 + WITH_X1, E // NW) as r:
                load_round(r, False)

        @block.tensor
        def _(pe):
            pe.wait_ge(start, 32)
            pe.wait_ge(setup, 1)
            nc.tensor.transpose(idx_ps[:, 0:E], tablef[:], ident[0:E, 0:E]).then_inc(setup, 1)

            def iteration(j, place):
                par = place % 2
                if active(j):
                    pe.wait_ge(ea_xT.sem, ea_xT.at(j))
                    pe.wait_ge(w_in[place].sem, w_in[place].at(j))
                    pe.wait_ge(ed_h.sem, ed_h.at(j - 2))
                    for n in range(KD):
                        last = nc.tensor.matmul(gu_ps[par], xgT[:, par, n, :], w1[:, place, n, :],
                                                start=(n == 0), stop=(n == KD - 1))
                    last.then_inc(e_gu.sem, 1)
                if active(j - 1):
                    pe.wait_ge(ed_h.sem, ed_h.at(j - 1))
                    pe.wait_ge(ea_hT.sem, ea_hT.at(j - 2))
                    for n in range(2):
                        last = nc.tensor.transpose(hidT_ps[0:PI, n * P:(n + 1) * P],
                                                   hid[:, 1 - par, :].rearrange("p (i c) -> p c i", c=2)[:, n, :],
                                                   ident[:])
                    last.then_inc(e_hT.sem, 1)
                if active(j + 1):
                    pe.wait_ge(x_got[1 - par].sem, x_got[1 - par].at(j + 1))
                    pe.wait_ge(ea_xT.sem, ea_xT.at(j))
                    for n in range(KD):
                        last = nc.tensor.transpose(rowsT_ps[:, n * P:(n + 1) * P],
                                                   xg[:, 1 - par, 0:D].rearrange("p (i c) -> p c i", c=KD)[:, n, :],
                                                   ident[:])
                    last.then_inc(e_xT.sem, 1)
                if active(j - 1):
                    pe.wait_ge(ea_hT.sem, ea_hT.at(j - 1))
                    pe.wait_ge(ea_out.sem, ea_out.at(j - 2))
                    for n in range(2):
                        last = nc.tensor.matmul(out_ps, hidT[:, n, :], w2[0:PI, (place - 1) % NW, n, :],
                                                start=(n == 0), stop=(n == 1))
                    last.then_inc(e_out.sem, 1)

            pipeline(pe, iteration)

        @block.scalar
        def _(act):
            def iteration(j, place):
                par = place % 2
                if active(j - 1):
                    act.wait_ge(e_hT.sem, e_hT.at(j - 1))
                    act.wait_ge(e_out.sem, e_out.at(j - 2))
                    nc.scalar.copy(hidT[:].rearrange("p c s -> p (c s)"), hidT_ps[0:PI, 0:2 * P]).then_inc(ea_hT.sem, 1)
                if active(j + 1):
                    act.wait_ge(e_xT.sem, e_xT.at(j + 1))
                    act.wait_ge(e_gu.sem, e_gu.at(j - 1))
                    nc.scalar.copy(xgT[:, 1 - par].rearrange("p k s -> p (k s)"), rowsT_ps).then_inc(ea_xT.sem, 1)
                if active(j - 1):
                    act.wait_ge(e_out.sem, e_out.at(j - 1))
                    act.wait_ge(added.sem, added.at(j - 3))
                    nc.scalar.copy(eo[:, 1 - par, :], out_ps).then_inc(ea_out.sem, 1)
                if active(j):
                    act.wait_ge(e_gu.sem, e_gu.at(j))
                    act.wait_ge(ed_h.sem, ed_h.at(j - 2))
                    nc.scalar.activation(tanh[:, par, :], gu_ps[par][:, 0:I], ACT.Tanh, scale=0.5).then_inc(ea_tanh.sem, 1)

            pipeline(act, iteration)

        @block.vector
        def _(dve):
            dve.wait_ge(start, 32)
            nc.vector.tensor_copy(tablef[:], table[:]).then_inc(setup, 1)
            dve.wait_ge(setup, 2)
            nc.vector.tensor_copy(idx[:], idx_ps[:, 0:E]).then_inc(setup, 1)
            dve.wait_ge(setup, 3)

            def column(ap, e):
                return ap[:, e:e + 1] if isinstance(e, int) else ap[:, bass.ds(e, 1)]

            def iteration(j, place):
                par = place % 2
                if active(j + 2):
                    dve.wait_ge(x_got[par].sem, x_got[par].at(j))
                    settle(dve)
                    nc.vector.tensor_copy(gidx[:, par, :], column(idx[:], j + 2)).then_inc(ed_gidx.sem, 1)
                if active(j - 1):
                    dve.wait_ge(added.sem, added.at(j - 3))
                    settle(dve)
                    nc.vector.tensor_copy(sidx[:, 1 - par, :], column(idx[:], j - 1)).then_inc(ed_sidx.sem, 1)
                if active(j):
                    dve.wait_ge(x_got[par].sem, x_got[par].at(j))
                    dve.wait_ge(ed_h.sem, ed_h.at(j - 1))
                    nc.vector.tensor_scalar(gate[:, par:par + 1], column(xg[:, par, D:D + E], j), 0.5, None,
                                            ALU.mult).then_inc(ed_gate.sem, 1)
                    dve.wait_ge(ea_tanh.sem, ea_tanh.at(j))
                    nc.vector.scalar_tensor_tensor(tanh[:, par, :], tanh[:, par, :], 1.0, gu_ps[par][:, 0:I],
                                                   ALU.add, ALU.mult).then_inc(ed_h.sem, 1)
                    dve.wait_ge(ed_h.sem, ed_h.at(j, 1))
                    dve.wait_ge(ed_gate.sem, ed_gate.at(j))
                    dve.wait_ge(e_hT.sem, e_hT.at(j - 2))
                    nc.vector.scalar_tensor_tensor(hid[:, par, :], tanh[:, par, :], gate[:, par:par + 1],
                                                   gu_ps[par][:, I:], ALU.mult, ALU.mult).then_inc(ed_h.sem, 1)

            pipeline(dve, iteration)

        @block.gpsimd
        def _(pool):
            def iteration(j, place):
                par = place % 2
                if active(j + 2):
                    pool.wait_ge(ed_gidx.sem, ed_gidx.at(j + 2))
                    pool.wait_ge(e_xT.sem, e_xT.at(j))
                    pool.wait_ge(ed_gate.sem, ed_gate.at(j))
                    settle(pool)
                    nc.gpsimd.indirect_dma_start(xg[:, par, :], None, xf_d, bass.IndirectOffsetOnAxis(
                        gidx[:, par, :].bitcast(U32), 0)).then_inc(x_got[par].sem, 16)
                if active(j - 1):
                    pool.wait_ge(ea_out.sem, ea_out.at(j - 1))
                    pool.wait_ge(ed_sidx.sem, ed_sidx.at(j - 1))
                    pool.wait_ge(added.sem, added.at(j - 2))
                    settle(pool)
                    nc.gpsimd.indirect_dma_start(acc_d, bass.IndirectOffsetOnAxis(
                        sidx[:, 1 - par, :].bitcast(U32), 0), eo[:, 1 - par, :], None,
                        compute_op=ALU.add).then_inc(added.sem, 16)

            pipeline(pool, iteration)
            pool.wait_ge(added.sem, added.at(E - 1))


def last_norm(nc, acc_d, out, res, res_in):
    NB = 8
    NG = NT // G
    with ExitStack() as ctx:
        def sb(name, shape, dt=F32):
            return ctx.enter_context(nc.sbuf_tensor(name, shape, dt))

        def count(name, per=1, n=1, place=0):
            return Count(ctx.enter_context(nc.semaphore(name)), per, NG, n, place)

        acc = sb("f_acc", [P, NB, G, D])
        st = sb("f_st", [P, NB, G, 6])
        mv = sb("f_mv", [P, NB, G, 2])
        ve = sb("f_ve", [P, NB, G])
        rstd = sb("f_rstd", [P, NB, G])
        shift = sb("f_shift", [P, NB])
        mhalf = sb("f_mhalf", [P, G])
        ready = ctx.enter_context(nc.semaphore("f_ready"))
        acc_in = [count(f"f_acc_in{n}", 16, NB, n) for n in range(NB)]
        out_done = count("f_out", 16)
        stats = count("f_stats", 2 * G)
        roots = count("f_roots", 4)
        v_norm = count("f_v_norm")
        a_norm = count("f_a_norm")
        g_sum = count("f_g_sum")
        v_sum = count("f_v_sum")

        def rows(ap, t):
            return ap[t * P:(t + 1) * P, :] if isinstance(t, int) else ap[bass.ts(t, P), :]

        def ring(eng, body):
            for u in range(NB):
                body(u, u)
            with eng.Fori(1, NG // NB) as r:
                for u in range(NB):
                    body(r * NB + u, u)

        def residual(t, g):
            return (res[:, t, g * D:(g + 1) * D] if isinstance(t, int) else
                    res[:, bass.ds(t, 1), g * D:(g + 1) * D].rearrange("p g n -> p (g n)"))

        block = ctx.enter_context(nc.Block())

        @block.sync
        def _(sp):
            def load(t, u):
                sp.wait_ge(g_sum.sem, g_sum.at(t - NB))
                sp.wait_ge(v_sum.sem, v_sum.at(t - NB))
                settle(sp)
                sp.dma_start(acc[:, u].rearrange("p r d -> p (r d)"), rows(group(acc_d[0:T, :]), t)).then_inc(acc_in[u].sem, 16)

            ring(sp, load)

        @block.scalar
        def _(act):
            def store(t):
                act.wait_ge(g_sum.sem, g_sum.at(t))
                act.wait_ge(v_sum.sem, v_sum.at(t))
                settle(act)
                src = res[:, t, :] if isinstance(t, int) else res[:, bass.ds(t, 1), :].rearrange("p g n -> p (g n)")
                act.dma_start(rows(group(out), t), src).then_inc(out_done.sem, 16)

            def body(t, u):
                act.wait_ge(roots.sem, roots.at(t))
                settle(act)
                nc.scalar.activation(acc[:, u, 1, :], acc[:, u, 1, :], ACT.Identity, bias=shift[:, u:u + 1],
                                     scale=rstd[:, u, 1:2]).then_inc(a_norm.sem, 1)
                if not isinstance(t, int) or t > 0:
                    store(t - 1)

            ring(act, body)
            store(NG - 1)
            act.wait_ge(out_done.sem, out_done.at(NG - 1))

        @block.vector
        def _(dve):
            nc.vector.memset(mhalf[:], -0.5).then_inc(ready, 1)
            dve.wait_ge(res_in, 16 * NG)

            def statistics(t, u):
                dve.wait_ge(acc_in[u].sem, acc_in[u].at(t))
                dve.wait_ge(roots.sem, roots.at(t - NB))
                for g in range(G):
                    nc.vector.bn_stats(st[:, u, g, :], acc[:, u, g, :]).then_inc(stats.sem, 1)
                dve.wait_ge(stats.sem, stats.at(t, G))
                settle(dve)
                for g in range(G):
                    nc.vector.bn_aggr(mv[:, u, g, :], st[:, u, g, :]).then_inc(stats.sem, 1)

            def normalise(t, u):
                dve.wait_ge(roots.sem, roots.at(t))
                nc.vector.tensor_scalar(acc[:, u, 0, :], acc[:, u, 0, :], mv[:, u, 0, 0:1], rstd[:, u, 0:1],
                                        ALU.subtract, ALU.mult).then_inc(v_norm.sem, 1)
                dve.wait_ge(a_norm.sem, a_norm.at(t))
                settle(dve)
                nc.vector.tensor_tensor(residual(t, 1), acc[:, u, 1, :], residual(t, 1), ALU.add).then_inc(v_sum.sem, 1)

            def body(t, u):
                statistics(t, u)
                if not isinstance(t, int) or t > 0:
                    normalise(t - 1, (u - 1) % NB)

            ring(dve, body)
            normalise(NG - 1, NB - 1)

        @block.gpsimd
        def _(pool):
            pool.wait_ge(ready, 1)
            pool.wait_ge(res_in, 16 * NG)

            def add(t, u):
                pool.wait_ge(v_norm.sem, v_norm.at(t))
                settle(pool)
                nc.gpsimd.tensor_tensor(residual(t, 0), acc[:, u, 0, :], residual(t, 0), ALU.add).then_inc(g_sum.sem, 1)

            def body(t, u):
                pool.wait_ge(stats.sem, stats.at(t))
                pool.wait_ge(v_norm.sem, v_norm.at(t - NB))
                pool.wait_ge(a_norm.sem, a_norm.at(t - NB))
                settle(pool)
                nc.gpsimd.tensor_scalar(ve[:, u], mv[:, u, :, 1], EPS, None, ALU.add).then_inc(roots.sem, 1)
                pool.wait_ge(roots.sem, roots.at(t, 1))
                nc.gpsimd.tensor_tensor(rstd[:, u], ve[:, u], mhalf[:], ALU.pow).then_inc(roots.sem, 1)
                pool.wait_ge(roots.sem, roots.at(t, 2))
                nc.gpsimd.tensor_tensor(shift[:, u:u + 1], mv[:, u, 1, 0:1], rstd[:, u, 1:2], ALU.mult).then_inc(roots.sem, 1)
                pool.wait_ge(roots.sem, roots.at(t, 3))
                settle(pool)
                nc.gpsimd.tensor_scalar(shift[:, u:u + 1], shift[:, u:u + 1], -1.0, None, ALU.mult).then_inc(roots.sem, 1)
                if not isinstance(t, int) or t > 0:
                    add(t - 1, (u - 1) % NB)

            ring(pool, body)
            add(NG - 1, NB - 1)


def kernel(**inputs):
    from concourse import bacc
    from concourse.bass_utils import run_bass_kernel_spmd

    a = {n: np.asarray(v) for n, v in inputs.items()}
    at, ff = (lambda n: a["L0_attn_" + n]), (lambda n: a["L0_ffn_" + n])
    cst, slot_init = constants()
    w_q = np.concatenate([at("Wcq").reshape(DC, H, DH), at("Wqr").reshape(DC, H, DR)], 2).reshape(DC, H * DQ)
    b_q = np.concatenate([at("bcq").reshape(H, DH), at("bqr").reshape(H, DR)], 1).reshape(H * DQ)
    g, u, r = ff("shared_gate_w").T, ff("shared_up_w").T, ff("gate_w").T
    w_gu = np.concatenate([g[:, 0:I], u[:, 0:I], r[:, 0:E // 2], g[:, I:], u[:, I:], r[:, E // 2:]], 1)
    arrays = {
        "x": at("h_t").reshape(T, D), "cst": cst, "slot_init": slot_init,
        "w_lat": np.concatenate([at("Wc"), at("Wckv"), at("Wkr")], 1),
        "b_lat": np.concatenate([at("bc"), at("bckv"), at("bkr")]),
        "w_q": w_q, "b_q": b_q, "w_ck": at("Wck"), "b_ck": at("bck"), "w_v": at("Wv"), "b_v": at("bv"),
        "w_o": at("Wo"), "b_o": at("bo"), "w_gu": w_gu, "w_sd": ff("shared_down_w").T,
        "w_eg": ff("gate_up_proj"), "w_ed": ff("down_proj"),
    }
    arrays = {n: np.ascontiguousarray(v) for n, v in arrays.items()}
    nc = bacc.Bacc("TRN2", target_bir_lowering=False, num_devices=1)
    args = [nc.dram_tensor(n, v.shape, mybir.dt.from_np(v.dtype), kind="ExternalInput").ap() for n, v in arrays.items()]
    out = nc.dram_tensor("out", (T, D), F32, kind="ExternalOutput").ap()
    layer_kernel(nc, *args, out)
    r = run_bass_kernel_spmd(nc, [arrays], core_ids=[0])
    return r.results[0]["out"].reshape(4, 2048, D)
```
